# Optimizing a Trainium2 kernel written in Bass

```python
import numpy as np
import jax
import jax.numpy as jnp

def _softmax(x, axis=-1):
    return jax.nn.softmax(x, axis=axis)

def _gelu(x):
    return jax.nn.gelu(x, approximate=True)

def _silu(x):
    return jax.nn.silu(x)

def _sigmoid(x):
    return jax.nn.sigmoid(x)

def _layernorm(x, axis=-1, eps=1e-05):
    m = jnp.mean(x, axis=axis, keepdims=True)
    v = jnp.var(x, axis=axis, keepdims=True)
    return (x - m) / jnp.sqrt(v + eps)

def _scatter_add(tgt, idx, src, axis=0):
    return tgt.at[idx].add(src)

def _segment_sum(src, seg, n):
    return jax.ops.segment_sum(src, seg, n)
kernel_name = 'mk_hybrid_d1_jaxref_r8_7649ba'

def setup_inputs(seed: int=0):
    np.random.seed(seed)
    _w = jnp.asarray

    def _L0_attn_a_setup():
        import math
        import jax, jax.numpy as jnp
        import numpy as np
        H = 32
        NOPE = 64
        ROPE = 64
        VD = 128
        QHD = NOPE + ROPE
        KVR = 32
        EPS = 1e-06

        def _yarn_cos_sin(seq_len, dim=ROPE, base=10000.0, factor=128.0, beta_fast=32.0, beta_slow=1.0, orig_max=1024, mscale=1.0, mscale_all_dim=1.0):

            def corr_dim(r):
                return dim * math.log(orig_max / (r * 2 * math.pi)) / (2 * math.log(base))
            low = max(math.floor(corr_dim(beta_fast)), 0)
            high = min(math.ceil(corr_dim(beta_slow)), dim - 1)
            hi = high + 0.001 if low == high else float(high)
            ramp = np.clip((np.arange(dim // 2, dtype=np.float32) - low) / (hi - low), 0.0, 1.0)
            inv_freq_mask = 1.0 - ramp
            freq_extra = 1.0 / base ** (np.arange(0, dim, 2, dtype=np.float32) / dim)
            freq_inter = freq_extra / factor
            inv_freq = freq_inter * (1.0 - inv_freq_mask) + freq_extra * inv_freq_mask
            t = np.arange(seq_len, dtype=np.float32)
            freqs = np.outer(t, inv_freq)
            emb = np.concatenate([freqs, freqs], axis=-1)

            def gm(s, m):
                return 1.0 if s <= 1 else 0.1 * m * math.log(s) + 1.0
            ms = gm(factor, mscale) / gm(factor, mscale_all_dim)
            return (jnp.asarray(np.cos(emb) * ms), jnp.asarray(np.sin(emb) * ms))

        def _rmsnorm(x, w, eps=EPS):
            var = jnp.mean(jnp.square(x), axis=-1, keepdims=True)
            return x * jax.lax.rsqrt(var + eps) * w

        def _deinterleave(x):
            d = x.shape[-1]
            x = x.reshape(*x.shape[:-1], d // 2, 2)
            return jnp.concatenate([x[..., 0], x[..., 1]], axis=-1)

        def _rotate_half(x):
            d = x.shape[-1] // 2
            return jnp.concatenate([-x[..., d:], x[..., :d]], axis=-1)

        def _apply_rope(x, cos, sin):
            return x * cos + _rotate_half(x) * sin
        key = jax.random.key(seed)
        ks = jax.random.split(key, 6)
        B, S, D = (1, 256, 512)
        std = 0.02
        return {'x': jax.random.normal(ks[0], (B, S, D), dtype=jnp.float32), 'wq_a': jax.random.normal(ks[1], (128, D), dtype=jnp.float32) * std, 'q_a_ln_w': jnp.ones((128,), dtype=jnp.float32), 'wq_b': jax.random.normal(ks[2], (H * QHD, 128), dtype=jnp.float32) * std, 'wkv_a': jax.random.normal(ks[3], (KVR + ROPE, D), dtype=jnp.float32) * std, 'kv_a_ln_w': jnp.ones((KVR,), dtype=jnp.float32), 'wkv_b': jax.random.normal(ks[4], (H * (NOPE + VD), KVR), dtype=jnp.float32) * std, 'wo': jax.random.normal(ks[5], (D, H * VD), dtype=jnp.float32) * std}
    _L0_attn_a_in = _L0_attn_a_setup()

    def _L0_attn_b_setup():
        import jax, jax.numpy as jnp
        import numpy as np
        H = 512
        D_IN = 1024
        N = 16
        K = 4
        R = 32
        EPS = 1e-06

        def rms_forward(x, eps=EPS):
            xf = x.astype(jnp.float32)
            var = jnp.mean(xf * xf, axis=-1, keepdims=True)
            return (xf * jax.lax.rsqrt(var + eps)).astype(x.dtype)
        key = jax.random.key(seed)
        ks = jax.random.split(key, 10)
        s = 0.02
        hidden_states = jax.random.normal(ks[0], (2, 128, H), dtype=jnp.float32)
        W_in = jax.random.normal(ks[1], (2 * D_IN, H), dtype=jnp.float32) * s
        conv_w = jax.random.normal(ks[2], (D_IN, K), dtype=jnp.float32) * 0.2
        conv_b = jax.random.normal(ks[3], (D_IN,), dtype=jnp.float32) * 0.02
        W_x = jax.random.normal(ks[4], (R + 2 * N, D_IN), dtype=jnp.float32) * s
        W_dt = jax.random.normal(ks[5], (D_IN, R), dtype=jnp.float32) * s
        b_dt = jax.random.normal(ks[6], (D_IN,), dtype=jnp.float32) * 0.02
        A_log = jnp.log(jnp.broadcast_to(jnp.arange(1, N + 1, dtype=jnp.float32)[None, :], (D_IN, N)))
        D = jnp.ones((D_IN,), dtype=jnp.float32)
        W_out = jax.random.normal(ks[7], (H, D_IN), dtype=jnp.float32) * s
        return {'hidden_states': hidden_states, 'W_in': W_in, 'conv_w': conv_w, 'conv_b': conv_b, 'W_x': W_x, 'W_dt': W_dt, 'b_dt': b_dt, 'A_log': A_log, 'D': D, 'W_out': W_out}
    _L0_attn_b_in = _L0_attn_b_setup()

    def _L0_ffn_setup():
        import jax, jax.numpy as jnp
        import numpy as np
        D_MODEL = 512
        D_FF = 1376
        key = jax.random.key(seed)
        k1, k2, k3, k4 = jax.random.split(key, 4)
        x = jax.random.normal(k1, (2, 256, D_MODEL), dtype=jnp.float32)
        W_gate = jax.random.normal(k2, (D_FF, D_MODEL), dtype=jnp.float32) * D_MODEL ** (-0.5)
        W_up = jax.random.normal(k3, (D_FF, D_MODEL), dtype=jnp.float32) * D_MODEL ** (-0.5)
        W_down = jax.random.normal(k4, (D_MODEL, D_FF), dtype=jnp.float32) * D_FF ** (-0.5)
        return {'x': x, 'W_gate': W_gate, 'W_up': W_up, 'W_down': W_down}
    _L0_ffn_in = _L0_ffn_setup()
    _d = {'L0_attn_a_x': _L0_attn_a_in['x'], 'L0_attn_a_wq_a': _L0_attn_a_in['wq_a'], 'L0_attn_a_q_a_ln_w': _L0_attn_a_in['q_a_ln_w'], 'L0_attn_a_wq_b': _L0_attn_a_in['wq_b'], 'L0_attn_a_wkv_a': _L0_attn_a_in['wkv_a'], 'L0_attn_a_kv_a_ln_w': _L0_attn_a_in['kv_a_ln_w'], 'L0_attn_a_wkv_b': _L0_attn_a_in['wkv_b'], 'L0_attn_a_wo': _L0_attn_a_in['wo'], 'L0_attn_b_W_in': _L0_attn_b_in['W_in'], 'L0_attn_b_conv_w': _L0_attn_b_in['conv_w'], 'L0_attn_b_conv_b': _L0_attn_b_in['conv_b'], 'L0_attn_b_W_x': _L0_attn_b_in['W_x'], 'L0_attn_b_W_dt': _L0_attn_b_in['W_dt'], 'L0_attn_b_b_dt': _L0_attn_b_in['b_dt'], 'L0_attn_b_A_log': _L0_attn_b_in['A_log'], 'L0_attn_b_D': _L0_attn_b_in['D'], 'L0_attn_b_W_out': _L0_attn_b_in['W_out'], 'L0_ffn_W_gate': _L0_ffn_in['W_gate'], 'L0_ffn_W_up': _L0_ffn_in['W_up'], 'L0_ffn_W_down': _L0_ffn_in['W_down']}
    _x0 = _d['L0_attn_a_x']
    _d['L0_attn_a_x'] = jax.random.normal(jax.random.fold_in(jax.random.key(seed), 1), (1, 1024, 512), dtype=_x0.dtype)
    del _x0
    return _d

def reference(L0_attn_a_x, L0_attn_a_wq_a, L0_attn_a_q_a_ln_w, L0_attn_a_wq_b, L0_attn_a_wkv_a, L0_attn_a_kv_a_ln_w, L0_attn_a_wkv_b, L0_attn_a_wo, L0_attn_b_W_in, L0_attn_b_conv_w, L0_attn_b_conv_b, L0_attn_b_W_x, L0_attn_b_W_dt, L0_attn_b_b_dt, L0_attn_b_A_log, L0_attn_b_D, L0_attn_b_W_out, L0_ffn_W_gate, L0_ffn_W_up, L0_ffn_W_down):

    def _L0_attn_a_ref(x, wq_a, q_a_ln_w, wq_b, wkv_a, kv_a_ln_w, wkv_b, wo):
        import math
        import jax, jax.numpy as jnp
        import numpy as np
        H = 32
        NOPE = 64
        ROPE = 64
        VD = 128
        QHD = NOPE + ROPE
        KVR = 32
        EPS = 1e-06

        def _yarn_cos_sin(seq_len, dim=ROPE, base=10000.0, factor=128.0, beta_fast=32.0, beta_slow=1.0, orig_max=1024, mscale=1.0, mscale_all_dim=1.0):

            def corr_dim(r):
                return dim * math.log(orig_max / (r * 2 * math.pi)) / (2 * math.log(base))
            low = max(math.floor(corr_dim(beta_fast)), 0)
            high = min(math.ceil(corr_dim(beta_slow)), dim - 1)
            hi = high + 0.001 if low == high else float(high)
            ramp = np.clip((np.arange(dim // 2, dtype=np.float32) - low) / (hi - low), 0.0, 1.0)
            inv_freq_mask = 1.0 - ramp
            freq_extra = 1.0 / base ** (np.arange(0, dim, 2, dtype=np.float32) / dim)
            freq_inter = freq_extra / factor
            inv_freq = freq_inter * (1.0 - inv_freq_mask) + freq_extra * inv_freq_mask
            t = np.arange(seq_len, dtype=np.float32)
            freqs = np.outer(t, inv_freq)
            emb = np.concatenate([freqs, freqs], axis=-1)

            def gm(s, m):
                return 1.0 if s <= 1 else 0.1 * m * math.log(s) + 1.0
            ms = gm(factor, mscale) / gm(factor, mscale_all_dim)
            return (jnp.asarray(np.cos(emb) * ms), jnp.asarray(np.sin(emb) * ms))

        def _rmsnorm(x, w, eps=EPS):
            var = jnp.mean(jnp.square(x), axis=-1, keepdims=True)
            return x * jax.lax.rsqrt(var + eps) * w

        def _deinterleave(x):
            d = x.shape[-1]
            x = x.reshape(*x.shape[:-1], d // 2, 2)
            return jnp.concatenate([x[..., 0], x[..., 1]], axis=-1)

        def _rotate_half(x):
            d = x.shape[-1] // 2
            return jnp.concatenate([-x[..., d:], x[..., :d]], axis=-1)

        def _apply_rope(x, cos, sin):
            return x * cos + _rotate_half(x) * sin
        B, S, D = x.shape
        m = 0.1 * 1.0 * math.log(128.0) + 1.0
        softmax_scale = QHD ** (-0.5) * m * m
        q = _rmsnorm(x @ wq_a.T, q_a_ln_w) @ wq_b.T
        q = q.reshape(B, S, H, QHD)
        q_nope, q_pe = (q[..., :NOPE], q[..., NOPE:])
        ckv_kpe = x @ wkv_a.T
        ckv, k_pe = (ckv_kpe[..., :KVR], ckv_kpe[..., KVR:])
        kv = _rmsnorm(ckv, kv_a_ln_w) @ wkv_b.T
        kv = kv.reshape(B, S, H, NOPE + VD)
        k_nope, v = (kv[..., :NOPE], kv[..., NOPE:])
        cos, sin = _yarn_cos_sin(S)
        q_pe = _apply_rope(_deinterleave(q_pe), cos[None, :, None, :], sin[None, :, None, :])
        k_pe = _apply_rope(_deinterleave(k_pe), cos[None, :, :], sin[None, :, :])
        q_full = jnp.concatenate([q_nope, q_pe], axis=-1)
        k_full = jnp.concatenate([k_nope, jnp.broadcast_to(k_pe[:, :, None, :], (B, S, H, ROPE))], axis=-1)
        scores = jnp.einsum('bqhd,bkhd->bhqk', q_full, k_full) * softmax_scale
        causal = jnp.tril(jnp.ones((S, S), dtype=bool))
        scores = jnp.where(causal[None, None], scores, jnp.finfo(scores.dtype).min)
        attn = jax.nn.softmax(scores, axis=-1)
        out = jnp.einsum('bhqk,bkhd->bqhd', attn, v).reshape(B, S, H * VD)
        return out @ wo.T

    def _L0_attn_b_ref(hidden_states, W_in, conv_w, conv_b, W_x, W_dt, b_dt, A_log, D, W_out):
        import jax, jax.numpy as jnp
        import numpy as np
        H = 512
        D_IN = 1024
        N = 16
        K = 4
        R = 32
        EPS = 1e-06

        def rms_forward(x, eps=EPS):
            xf = x.astype(jnp.float32)
            var = jnp.mean(xf * xf, axis=-1, keepdims=True)
            return (xf * jax.lax.rsqrt(var + eps)).astype(x.dtype)
        b, L, _ = hidden_states.shape
        proj = hidden_states @ W_in.T
        x, gate = (proj[..., :D_IN], proj[..., D_IN:])
        xpad = jnp.pad(x, ((0, 0), (K - 1, 0), (0, 0)))
        xc = conv_b
        for j in range(K):
            xc = xc + conv_w[:, j] * xpad[:, j:j + L, :]
        x = jax.nn.silu(xc)
        ssm = x @ W_x.T
        ts, Bm, Cm = (ssm[..., :R], ssm[..., R:R + N], ssm[..., R + N:])
        ts = rms_forward(ts)
        Bm = rms_forward(Bm)
        Cm = rms_forward(Cm)
        dt = jax.nn.softplus(ts @ W_dt.T + b_dt)
        A = -jnp.exp(A_log.astype(jnp.float32))

        def step(state, inp):
            dt_t, B_t, C_t, u_t = inp
            dA = jnp.exp(dt_t[..., None] * A)
            state = state * dA + (dt_t * u_t)[..., None] * B_t[:, None, :]
            y = jnp.einsum('bdn,bn->bd', state, C_t)
            return (state, y)
        init = jnp.zeros((b, D_IN, N), dtype=jnp.float32)
        xs = (dt.transpose(1, 0, 2), Bm.transpose(1, 0, 2), Cm.transpose(1, 0, 2), x.transpose(1, 0, 2))
        _, ys = jax.lax.scan(step, init, xs)
        y = ys.transpose(1, 0, 2) + x * D
        y = y * jax.nn.silu(gate)
        return y @ W_out.T

    def _L0_ffn_ref(x, W_gate, W_up, W_down):
        import jax, jax.numpy as jnp
        import numpy as np
        D_MODEL = 512
        D_FF = 1376
        out_shape = x.shape[:-1] + (W_down.shape[0],)
        xf = x.reshape(-1, x.shape[-1])
        up = jnp.einsum('td,fd->tf', xf, W_up)
        gate = jax.nn.silu(jnp.einsum('td,fd->tf', xf, W_gate))
        h = gate * up
        y = jnp.einsum('tf,df->td', h, W_down)
        return y.reshape(out_shape)
    x = L0_attn_a_x
    x = x + _L0_attn_a_ref(_layernorm(x, axis=-1), L0_attn_a_wq_a, L0_attn_a_q_a_ln_w, L0_attn_a_wq_b, L0_attn_a_wkv_a, L0_attn_a_kv_a_ln_w, L0_attn_a_wkv_b, L0_attn_a_wo)
    x = x + _L0_ffn_ref(_layernorm(x, axis=-1), L0_ffn_W_gate, L0_ffn_W_up, L0_ffn_W_down)
    x = x + _L0_attn_b_ref(_layernorm(x, axis=-1), L0_attn_b_W_in, L0_attn_b_conv_w, L0_attn_b_conv_b, L0_attn_b_W_x, L0_attn_b_W_dt, L0_attn_b_b_dt, L0_attn_b_A_log, L0_attn_b_D, L0_attn_b_W_out)
    x = x + _L0_ffn_ref(_layernorm(x, axis=-1), L0_ffn_W_gate, L0_ffn_W_up, L0_ffn_W_down)
    return x

_drawn_inputs = setup_inputs


def setup_inputs(seed=0):
    import zlib

    import numpy as np

    out = dict(_drawn_inputs(seed))
    spreads = {'L0_attn_a_q_a_ln_w': (1.0, 0.6),
     'L0_attn_a_kv_a_ln_w': (1.0, 0.6),
     'L0_attn_b_D': (1.0, 0.6)}
    factors = {'L0_attn_a_wq_a': 8.0,
     'L0_attn_a_wq_b': 8.0,
     'L0_attn_a_wkv_a': 3.824,
     'L0_attn_a_wkv_b': 3.879,
     'L0_attn_a_wo': 3.664,
     'L0_attn_b_conv_b': 8.0,
     'L0_attn_b_W_dt': 31.073,
     'L0_attn_b_b_dt': 64.0,
     'L0_attn_b_A_log': 64.0}
    for name, (base, spread) in spreads.items():
        noise = np.random.default_rng([zlib.crc32(name.encode()), seed]).standard_normal(out[name].shape)
        drawn = base * np.exp(spread * noise) if base else spread * noise
        out[name] = jnp.asarray(drawn.astype(out[name].dtype))
    for name, factor in factors.items():
        out[name] = (out[name] * factor).astype(out[name].dtype)
    return out
```

```python
import math
from contextlib import ExitStack

import numpy as np

import concourse.bass as bass
from concourse import mybir

F32 = mybir.dt.float32
F32R = mybir.dt.float32r
BF16 = mybir.dt.bfloat16
ALU = mybir.AluOpType
ACT = mybir.ActivationFunctionType
AX_X = mybir.AxisListType.X

P = 128
S, DM = 1024, 512
NT = S // P
DC = DM // P
H, NOPE, ROPE, VD = 32, 64, 64, 128
QR, KVR = 128, 32
HG = 4
NG = H // HG
QW = ROPE + KVR
QK = QW + 1
SOFTMAX_SCALE = (NOPE + ROPE) ** -0.5 * (0.1 * math.log(128.0) + 1.0) ** 2
MASKED = -1e30
A_LOG_MAX = 80.0
FF = 1376
FT = -(-FF // P)
DI, NS, KC, RK = 1024, 16, 4, 32
DJ = DI // P
CH = 512
NCH = S // CH
TPC = CH // P


def rope_tables():
    base, factor, orig = 10000.0, 128.0, 1024

    def corr_dim(r):
        return ROPE * math.log(orig / (r * 2 * math.pi)) / (2 * math.log(base))

    low = max(math.floor(corr_dim(32.0)), 0)
    high = min(math.ceil(corr_dim(1.0)), ROPE - 1)
    hi = high + 0.001 if low == high else float(high)
    ramp = np.clip((np.arange(ROPE // 2, dtype=np.float32) - low) / (hi - low), 0.0, 1.0)
    mask = 1.0 - ramp
    extra = 1.0 / base ** (np.arange(0, ROPE, 2, dtype=np.float32) / ROPE)
    inter = extra / factor
    freqs = np.outer(np.arange(S, dtype=np.float32), inter * (1.0 - mask) + extra * mask)
    cos, sin = np.cos(freqs).astype(np.float32), np.sin(freqs).astype(np.float32)
    return np.concatenate([cos, cos], axis=1), np.concatenate([-sin, sin], axis=1)


class Run:
    def __init__(self, handle, base):
        self.sem, self.base = handle, base

    def __call__(self, value):
        return self.sem, self.base + value


def layer(nc, x, wq_a, q_ln, wq_b, wkv_a, kv_ln, wkv_b, wo, w_in, conv_w, conv_b, w_x, w_dt, b_dt,
          a_log, d_skip, w_out, w_gate, w_up, w_down, rope_cos, rope_sin, out):
    top = ExitStack()

    def sb_in(stack, name, shape, dt=F32):
        return stack.enter_context(nc.sbuf_tensor(name, shape, dt))

    def sem(name):
        return top.enter_context(nc.semaphore(name))

    with top:
        bank = [top.enter_context(nc.psum_tensor(f"bank{i}", [P, 512], F32)) for i in range(8)]
        X = sb_in(top, "X", [P, NT, DM])
        XnT = sb_in(top, "XnT", [P, DC, S])
        ident = sb_in(top, "ident", [P, P])
        identb = sb_in(top, "identb", [P, P], BF16)
        ones = sb_in(top, "ones", [P, KVR])
        neghalf = sb_in(top, "neghalf", [P, 16])
        stats = sb_in(top, "stats", [P, NT, 6])
        meanvar = sb_in(top, "meanvar", [P, NT, 2])
        veps = sb_in(top, "veps", [P, 16])
        rstd = sb_in(top, "rstd", [P, 16])

        runs = {}

        def again(name, total):
            if name not in runs:
                runs[name] = [sem(name), 0]
            handle, base = runs[name]
            runs[name][1] += total
            return Run(handle, base)

        x_in = sem("x_in")
        consts = sem("consts")
        const_step = sem("const_step")

        def layer_norm(tag, load=None):
            mem = ExitStack()
            Xn = sb_in(mem, f"Xn_{tag}", [P, NT, DM])
            mem.close()
            stats_done, aggr_done = again("stats_done", NT), again("aggr_done", NT)
            eps_done, rstd_done = again("eps_done", 1), again("rstd_done", 1)
            xn_done, xnt_psum, xnt_done = again("xn_done", NT), again("xnt_psum", NT), again("xnt_done", NT)
            with nc.Block() as block:
                @block.vector
                def _(dve):
                    if load is not None:
                        dve.wait_ge(load, 16)
                    for t in range(NT):
                        dve.bn_stats(stats[:, t, :], X[:, t, :]).then_inc(stats_done.sem, 1)
                    for t in range(NT):
                        dve.wait_ge(*stats_done(t + 1))
                        dve.bn_aggr(meanvar[:, t, :], stats[:, t, :]).then_inc(aggr_done.sem, 1)
                    dve.wait_ge(*rstd_done(1))
                    for t in range(NT):
                        dve.tensor_scalar(Xn[:, t, :], X[:, t, :], meanvar[:, t, 0:1], rstd[:, t:t + 1],
                                          ALU.subtract, ALU.mult).then_inc(xn_done.sem, 1)

                @block.gpsimd
                def _(pool):
                    if load is not None:
                        pool.memset(neghalf[:], -0.5).then_inc(const_step, 1)
                        pool.memset(ident[:], 0.0).then_inc(const_step, 1)
                        pool.memset(ones[:], 1.0).then_inc(consts, 1)
                        pool.wait_ge(const_step, 2)
                        pool.affine_select(out=ident[:], in_=ident[:], compare_op=ALU.not_equal, fill=1.0, base=0,
                                           pattern=[[-1, P]], channel_multiplier=1).then_inc(consts, 1)
                        pool.wait_ge(consts, 2)
                        pool.tensor_copy(identb[:], ident[:]).then_inc(consts, 1)
                    pool.wait_ge(*aggr_done(NT))
                    pool.tensor_scalar(veps[:, 0:NT], meanvar[:, :, 1], 1e-5, None, ALU.add).then_inc(eps_done.sem, 1)
                    pool.wait_ge(*eps_done(1))
                    pool.tensor_tensor(rstd[:, 0:NT], veps[:, 0:NT], neghalf[:, 0:NT], ALU.pow).then_inc(rstd_done.sem, 1)

                @block.tensor
                def _(pe):
                    pe.wait_ge(consts, 3)
                    for t in range(NT):
                        pe.wait_ge(*xn_done(t + 1))
                        if t >= 2:
                            pe.wait_ge(*xnt_done(t - 1))
                        for c in range(DC):
                            last = pe.transpose(bank[t % 2][:, c * P:(c + 1) * P], Xn[:, t, c * P:(c + 1) * P], ident[:])
                        last.then_inc(xnt_psum.sem, 1)

                @block.scalar
                def _(act):
                    for t in range(NT):
                        act.wait_ge(*xnt_psum(t + 1))
                        act.copy(XnT[:, :, t * P:(t + 1) * P],
                                 bank[t % 2][:].rearrange("p (c n) -> p c n", c=DC)).then_inc(xnt_done.sem, 1)

                @block.sync
                def _(sp):
                    if load is not None:
                        sp.dma_start(X[:], x[0].rearrange("(t p) d -> p t d", p=P)).then_inc(load, 16)

        layer_norm("a", x_in)

        att = ExitStack()
        WQ = sb_in(att, "WQ", [P, H * QW])
        WVO = sb_in(att, "WVO", [P, NG, DM])
        QnT = sb_in(att, "QnT", [P, S])
        KTM = sb_in(att, "KTM", [P, NT, QK])
        KTh = sb_in(att, "KTh", [QK, S], F32R)
        KTl = sb_in(att, "KTl", [QK, S], F32R)
        cosT = sb_in(att, "cosT", [P, NT, 2, 32])
        sinT = sb_in(att, "sinT", [P, NT, 2, 32])
        maskqk = sb_in(att, "maskqk", [P, P], BF16)
        maskkq = sb_in(att, "maskkq", [P, P], BF16)

        prep = ExitStack()
        wa_nat = sb_in(prep, "wa_nat", [P, DM])
        wkva_nat = sb_in(prep, "wkva_nat", [KVR + ROPE, DM])
        WaT = sb_in(prep, "WaT", [P, DC, QR + KVR + ROPE])
        wqb_nat = sb_in(prep, "wqb_nat", [P, H, QR])
        wk_nat = sb_in(prep, "wk_nat", [NOPE, H, KVR])
        wv_nat = sb_in(prep, "wv_nat", [P, H, KVR])
        wo_nat = sb_in(prep, "wo_nat", [P, DC, H * VD // 2])
        woT = sb_in(prep, "woT", [P, 2, HG, DM])
        qlnw = sb_in(prep, "qlnw", [P, QR])
        kvlnw = sb_in(prep, "kvlnw", [P, KVR])
        QA = sb_in(prep, "QA", [P, NT, QR + KVR + ROPE])
        SQ = sb_in(prep, "SQ", [P, NT, QR + KVR])
        QAn = sb_in(prep, "QAn", [P, NT, QR])
        RAk = sb_in(prep, "RAk", [P, NT, 2, 32])
        RBk = sb_in(prep, "RBk", [P, NT, 2, 32])
        rs = sb_in(prep, "rs", [P, 2 * NT])
        ms = sb_in(prep, "ms", [P, 2 * NT])
        prep.close()

        ld_a, ld_q, ld_kv, ld_small = sem("ld_a"), sem("ld_q"), sem("ld_kv"), sem("ld_small")
        ld_wo = [sem(f"ld_wo{i}") for i in range(2)]
        wo_used = sem("wo_used")
        masks0, masks = sem("masks0"), sem("masks")
        evac_in, evac_out = sem("evac_in"), sem("evac_out")
        proj_psum, proj_out = sem("proj_psum"), sem("proj_out")
        wot_psum, wot_done, wvo_psum, wvo_done = sem("wot_psum"), sem("wot_done"), sem("wvo_psum"), sem("wvo_done")
        sq_done, ms_done, rs_step, rs_done = sem("sq_done"), sem("ms_done"), sem("rs_step"), sem("rs_done")
        kstep, qn_done, ktm_done = sem("kstep"), sem("qn_done"), sem("ktm_done")
        kt_psum, kth_done, ktl_done = sem("kt_psum"), sem("kth_done"), sem("ktl_done")
        NQW = QR + KVR + ROPE

        with nc.Block() as block:
            @block.sync
            def _(sp):
                sp.dma_start(wa_nat[:], wq_a).then_inc(ld_a, 16)
                sp.dma_start(wkva_nat[:], wkv_a).then_inc(ld_a, 16)
                kvb = wkv_b.rearrange("(h m) r -> m h r", m=NOPE + VD)
                sp.dma_start(wqb_nat[:], wq_b.rearrange("(h m) r -> m h r", m=P)).then_inc(ld_q, 16)
                sp.dma_start(wk_nat[:], kvb[0:NOPE]).then_inc(ld_kv, 16)
                sp.dma_start(wv_nat[:], kvb[NOPE:NOPE + VD]).then_inc(ld_kv, 16)
                sp.dma_start(cosT[:], rope_cos.rearrange("(t p) (a i) -> p t a i", p=P, a=2)).then_inc(ld_small, 16)
                sp.dma_start(sinT[:], rope_sin.rearrange("(t p) (a i) -> p t a i", p=P, a=2)).then_inc(ld_small, 16)
                sp.dma_start(qlnw[:], q_ln.rearrange("(a r) -> a r", a=1).to_broadcast([P, QR])).then_inc(ld_small, 16)
                sp.dma_start(kvlnw[:], kv_ln.rearrange("(a r) -> a r", a=1).to_broadcast([P, KVR])).then_inc(ld_small, 16)
                wo_rows = wo.rearrange("(c p) k -> p c k", p=P)
                HW = H * VD // 2
                for half in range(2):
                    if half:
                        sp.wait_ge(wo_used, 1)
                    sp.dma_start(wo_nat[:], wo_rows[:, :, half * HW:(half + 1) * HW]).then_inc(ld_wo[half], 16)

            @block.gpsimd
            def _(pool):
                pool.memset(maskqk[:], 0.0).then_inc(masks0, 1)
                pool.memset(maskkq[:], 0.0).then_inc(masks0, 1)
                pool.wait_ge(masks0, 2)
                pool.affine_select(out=maskqk[:], in_=maskqk[:], compare_op=ALU.is_ge, fill=MASKED, base=0,
                                   pattern=[[-1, P]], channel_multiplier=1).then_inc(masks, 1)
                pool.affine_select(out=maskkq[:], in_=maskkq[:], compare_op=ALU.is_ge, fill=MASKED, base=0,
                                   pattern=[[1, P]], channel_multiplier=-1).then_inc(masks, 1)
                pool.memset(KTM[:, :, QW:QK], 1.0).then_inc(ktm_done, 1)
                pool.wait_ge(ms_done, 2)
                pool.tensor_scalar(veps[:, 0:NT], ms[:, 0:NT], 1.0 / QR, 1e-6, ALU.mult, ALU.add).then_inc(rs_step, 1)
                pool.tensor_scalar(veps[:, NT:], ms[:, NT:], 1.0 / KVR, 1e-6, ALU.mult, ALU.add).then_inc(rs_step, 1)
                pool.wait_ge(rs_step, 2)
                pool.tensor_tensor(rs[:], veps[:], neghalf[:], ALU.pow).then_inc(rs_done, 1)

            @block.tensor
            def _(pe):
                pe.wait_ge(ld_a, 32)
                for c in range(DC):
                    if c >= 2:
                        pe.wait_ge(evac_out, c - 1)
                    pe.transpose(bank[c % 2][:, 0:QR], wa_nat[:, c * P:(c + 1) * P], ident[:])
                    pe.transpose(bank[c % 2][:, QR:NQW], wkva_nat[:, c * P:(c + 1) * P],
                                 ident[0:KVR + ROPE, 0:KVR + ROPE]).then_inc(evac_in, 1)
                pe.wait_ge(evac_out, DC)
                for t in range(NT):
                    if t >= 2:
                        pe.wait_ge(proj_out, t - 1)
                    for c in range(DC):
                        last = pe.matmul(bank[2 + t % 2][:, 0:NQW], XnT[:, c, t * P:(t + 1) * P], WaT[:, c, :],
                                         start=(c == 0), stop=(c == DC - 1))
                    last.then_inc(proj_psum, 1)
                pe.wait_ge(ld_q, 16)
                pe.wait_ge(ld_kv, 32)
                pe.wait_ge(proj_out, NT)
                for g in range(NG):
                    pe.wait_ge(evac_out, DC + max(g - 1, 0))
                    for j in range(HG):
                        h = HG * g + j
                        pe.transpose(bank[g % 2][:, j * ROPE:(j + 1) * ROPE], wqb_nat[NOPE:P, h, :], ident[NOPE:P, NOPE:P])
                        last = pe.matmul(bank[2 + g % 2][:, j * KVR:(j + 1) * KVR], wqb_nat[0:NOPE, h, :],
                                         wk_nat[:, h, :], start=True, stop=True)
                    last.then_inc(evac_in, 1)
                for g in range(NG):
                    pe.wait_ge(ld_wo[g // 4], 16)
                    for j in range(HG):
                        h = HG * g + j
                        if h >= 2:
                            pe.wait_ge(wot_done, h - 1)
                        for c in range(DC):
                            last = pe.transpose(bank[4 + h % 2][:, c * P:(c + 1) * P],
                                                wo_nat[:, c, (h % 16) * VD:(h % 16 + 1) * VD], ident[:])
                        last.then_inc(wot_psum, 1)
                    if g == 3:
                        pe.wait_ge(wot_done, 16)
                    pe.wait_ge(wot_done, HG * (g + 1))
                    if g >= 2:
                        pe.wait_ge(wvo_done, g - 1)
                    for j in range(HG):
                        last = pe.matmul(bank[6 + g % 2][32 * j:32 * j + 32, :], wv_nat[:, HG * g + j, :],
                                         woT[:, g % 2, j, :], start=True, stop=True)
                    last.then_inc(wvo_psum, 1)
                pe.wait_ge(evac_out, DC + NG)
                pe.wait_ge(qn_done, 1)
                for i in range(2):
                    for k in range(4):
                        last = pe.transpose(bank[i][:, k * P:(k + 1) * P], QAn[:, 4 * i + k, :], ident[:])
                    last.then_inc(evac_in, 1)
                pe.wait_ge(ktm_done, 3)
                pe.wait_ge(evac_out, DC + NG)
                for i in range(2):
                    for k in range(4):
                        last = pe.transpose(bank[2 + i][0:QK, k * P:(k + 1) * P], KTM[:, 4 * i + k, :], ident[:])
                    last.then_inc(kt_psum, 1)

            @block.scalar
            def _(act):
                for c in range(DC):
                    act.wait_ge(evac_in, c + 1)
                    act.copy(WaT[:, c, :], bank[c % 2][:, 0:NQW]).then_inc(evac_out, 1)
                for g in range(NG):
                    act.wait_ge(evac_in, DC + g + 1)
                    dst = WQ[:, g * HG * QW:(g + 1) * HG * QW].rearrange("p (j w) -> p j w", j=HG)
                    src = bank[g % 2][:, 0:HG * ROPE].rearrange("p (j w) -> p j w", j=HG)
                    for a in range(2):
                        act.copy(dst[:, :, 32 * a:32 * a + 32], src[:, :, a:ROPE:2])
                    act.copy(dst[:, :, ROPE:QW], bank[2 + g % 2][:, 0:HG * KVR].rearrange("p (j w) -> p j w", j=HG)).then_inc(evac_out, 1)
                for g in range(NG):
                    act.wait_ge(wvo_psum, g + 1)
                    act.copy(WVO[:, g, :], bank[6 + g % 2][:]).then_inc(wvo_done, 1)
                for i in range(2):
                    act.wait_ge(evac_in, DC + NG + i + 1)
                    act.copy(QnT[:, i * 512:(i + 1) * 512], bank[i][:]).then_inc(evac_out, 1)
                for i in range(2):
                    act.wait_ge(kt_psum, i + 1)
                    act.copy(KTh[:, i * 512:(i + 1) * 512], bank[2 + i][0:QK, :]).then_inc(kth_done, 1)

            @block.vector
            def _(dve):
                for t in range(NT):
                    dve.wait_ge(proj_psum, t + 1)
                    dve.tensor_copy(QA[:, t, :], bank[2 + t % 2][:, 0:NQW]).then_inc(proj_out, 1)
                dve.wait_ge(proj_out, NT)
                dve.tensor_tensor(SQ[:], QA[:, :, 0:QR + KVR], QA[:, :, 0:QR + KVR], ALU.mult).then_inc(sq_done, 1)
                dve.wait_ge(sq_done, 1)
                dve.tensor_reduce(ms[:, 0:NT], SQ[:, :, 0:QR], AX_X, ALU.add).then_inc(ms_done, 1)
                dve.tensor_reduce(ms[:, NT:], SQ[:, :, QR:], AX_X, ALU.add).then_inc(ms_done, 1)
                dve.wait_ge(ld_small, 64)
                pairs = QA[:, :, QR + KVR:].rearrange("p t (i a) -> p t a i", a=2)
                for a in range(2):
                    dve.tensor_tensor(RAk[:, :, a, :], pairs[:, :, a, :], cosT[:, :, a, :], ALU.mult)
                    last = dve.tensor_tensor(RBk[:, :, a, :], pairs[:, :, 1 - a, :], sinT[:, :, a, :], ALU.mult)
                last.then_inc(kstep, 1)
                dve.wait_ge(kstep, 1)
                dve.tensor_tensor(KTM[:, :, 0:ROPE], RAk[:].rearrange("p t a i -> p t (a i)"),
                                  RBk[:].rearrange("p t a i -> p t (a i)"), ALU.add).then_inc(ktm_done, 1)
                dve.wait_ge(rs_done, 1)
                dve.tensor_tensor(SQ[:, :, 0:QR], QA[:, :, 0:QR], rs[:, 0:NT].unsqueeze(2).to_broadcast([P, NT, QR]),
                                  ALU.mult).then_inc(kstep, 1)
                dve.tensor_tensor(SQ[:, :, QR:], QA[:, :, QR:QR + KVR],
                                  rs[:, NT:].unsqueeze(2).to_broadcast([P, NT, KVR]), ALU.mult).then_inc(kstep, 1)
                dve.wait_ge(kstep, 3)
                dve.tensor_tensor(QAn[:], SQ[:, :, 0:QR], qlnw[:].unsqueeze(1).to_broadcast([P, NT, QR]),
                                  ALU.mult).then_inc(qn_done, 1)
                dve.tensor_tensor(KTM[:, :, ROPE:QW], SQ[:, :, QR:], kvlnw[:].unsqueeze(1).to_broadcast([P, NT, KVR]),
                                  ALU.mult).then_inc(ktm_done, 1)
                for h in range(H):
                    dve.wait_ge(wot_psum, h + 1)
                    if h >= 2 * HG:
                        dve.wait_ge(wvo_psum, h // HG - 1)
                    if h == 15:
                        dve.tensor_copy(woT[:, (h // HG) % 2, h % HG, :], bank[4 + h % 2][:]).then_inc(wot_done, 1)
                        dve.wait_ge(wot_done, 16)
                        dve.sem_inc(wo_used, 1)
                    else:
                        dve.tensor_copy(woT[:, (h // HG) % 2, h % HG, :], bank[4 + h % 2][:]).then_inc(wot_done, 1)
                for i in range(2):
                    dve.wait_ge(kth_done, i + 1)
                    dve.tensor_tensor(KTl[:, i * 512:(i + 1) * 512], bank[2 + i][0:QK, :],
                                      KTh[:, i * 512:(i + 1) * 512].bitcast(F32), ALU.subtract).then_inc(ktl_done, 1)

        core = ExitStack()
        OT = sb_in(core, "OT", [P, NG * S])
        QT = [(sb_in(core, f"QTh{i}", [QK, HG * P], F32R), sb_in(core, f"QTl{i}", [QK, HG * P], F32R)) for i in range(4)]
        Qtm = [sb_in(core, f"Qtm{i}", [P, HG, QW]) for i in range(2)]
        RA = [sb_in(core, f"RA{i}", [P, HG, 2, 32]) for i in range(2)]
        RB = [sb_in(core, f"RB{i}", [P, HG, 2, 32]) for i in range(2)]
        mx = [sb_in(core, f"mx{i}", [P, HG, 2]) for i in range(2)]
        negm = [sb_in(core, f"negm{i}", [P, HG], BF16) for i in range(2)]
        NPT = 6
        PT = [sb_in(core, f"PT{i}", [P, HG * P]) for i in range(NPT)]
        PS = [sb_in(core, f"PS{i}", [P, HG * P]) for i in range(2)]
        rD = [sb_in(core, f"rD{i}", [P, P]) for i in range(2)]
        core.close()
        att.close()

        q_psum, ra_done, rope_done = sem("q_psum"), sem("ra_done"), sem("rope_done")
        t_psum, qh_done, ql_done = sem("t_psum"), sem("qh_done"), sem("ql_done")
        p1_psum, p1_read, m_done, mrow_psum, mrow_done = (sem("p1_psum"), sem("p1_read"), sem("m_done"),
                                                          sem("mrow_psum"), sem("mrow_done"))
        s_psum, p_done, pv_done, sum_done = sem("s_psum"), sem("p_done"), sem("pv_done"), sem("sum_done")
        den_psum, rd_done, o_done, qlzero = sem("den_psum"), sem("rd_done"), sem("o_done"), sem("qlzero")
        RING, TB, ST, OD = (0, 1), 2, (3, 4, 5), (6, 7)

        ORDER = [7, 0, 6, 1, 5, 2, 4, 3]
        UNITS, PAIR = NG * NT, NT + 1
        STEPS = NT * (NT + 1) // 2
        first_step = [sum(ORDER[i] + 1 for i in range(n)) for n in range(NT)]

        def tile_of(n):
            return ORDER[n % NT]

        def unit_of(x):
            i = max(i for i in range(NT) if first_step[i] <= x % STEPS)
            return x // STEPS * NT + i, x % STEPS - first_step[i]

        def step_of(n, k):
            return n // NT * STEPS + first_step[n % NT] + k

        def sums_through(x):
            n, _ = unit_of(x)
            return x + 1 - (n + 1)

        def max_chunks(n):
            keys = (tile_of(n) + 1) * P
            if keys <= 256:
                return [((0, 1), 0, keys), ((2, 3), 0, keys)]
            return [((j,), a, min(keys, a + 512) - a) for j in range(HG) for a in range(0, keys, 512)]

        CHUNKS = sum(len(max_chunks(i)) for i in range(NT))

        def chunk_of(n, c):
            return n // NT * CHUNKS + sum(len(max_chunks(i)) for i in range(n % NT)) + c

        def side_work(x):
            w, cur = x % PAIR, x // PAIR * 2
            a1, b1, a2 = cur + 2, cur + 3, cur + 4
            nb = len(max_chunks(b1))
            todo = {0: [("project", b1, 0)], 1: [("transpose", a1, 0), ("maxrow", cur + 1, 0)],
                    5: [("chunk", a1, 6), ("chunk", a1, 7), ("transpose", b1, 0)],
                    6: [("maxrow", a1, 0)] + [("chunk", b1, c) for c in range(nb // 2)],
                    7: [("chunk", b1, c) for c in range(nb // 2, nb)], 8: [("project", a2, 0)]}.get(w, [])
            if 2 <= w <= 4:
                todo = [("chunk", a1, 2 * w - 4), ("chunk", a1, 2 * w - 3)]
            for late in (1, 2):
                if x >= late:
                    n, k = unit_of(x - late)
                    if k == tile_of(n) and late == (1 if ORDER[(n + 1) % NT] == 0 else 2):
                        todo = [("denominator", n, 0)] + todo
            return [e for e in todo if e[1] < UNITS]

        PROLOGUE = ([("project", 0, 0), ("project", 1, 0), ("transpose", 0, 0)] + [("chunk", 0, c) for c in range(8)]
                    + [("transpose", 1, 0)] + [("chunk", 1, c) for c in range(2)] + [("maxrow", 0, 0), ("project", 2, 0)])

        ring = [e for e in PROLOGUE if e[0] in ("project", "chunk")]
        for x in range(UNITS // NT * STEPS):
            ring += [e for e in side_work(x) if e[0] in ("project", "chunk")]
        place = {e: i for i, e in enumerate(ring)}

        def groups(eng, prologue, step, epilogue=None):
            prologue()
            for x in range(STEPS):
                step(x, lambda v, per: v)
            with eng.Fori(1, NG - 1) as g:
                for x in range(STEPS, 2 * STEPS):
                    step(x, lambda v, per: g * per + (v - per))
            for x in range((NG - 1) * STEPS, NG * STEPS):
                step(x, lambda v, per: v)
            if epilogue is not None:
                epilogue()

        with nc.Block() as block:
            @block.tensor
            def _(pe):
                def ring_bank(e, at):
                    i = place[e]
                    if i >= 2:
                        kind, n, c = ring[i - 2]
                        if kind == "project":
                            pe.wait_ge(ra_done, at(n + 1, NT))
                        else:
                            pe.wait_ge(p1_read, at(chunk_of(n, c) + 1, CHUNKS))
                    return bank[RING[i % 2]]

                def project(n, at):
                    t = tile_of(n)
                    b = ring_bank(("project", n, 0), at)
                    pe.matmul(b[:, 0:HG * QW], QnT[:, t * P:(t + 1) * P],
                              WQ[:, bass.ds(at(n // NT, 1) * (HG * QW), HG * QW)], start=True, stop=True).then_inc(q_psum, 1)

                def transpose(n, at):
                    pe.wait_ge(rope_done, at(n + 1, NT))
                    if n >= 1:
                        pe.wait_ge(ql_done, at(n, NT))
                    for j in range(HG):
                        last = pe.transpose(bank[TB][0:QW, j * P:(j + 1) * P], Qtm[n % 2][:, j, :], ident[:])
                    last.then_inc(t_psum, 1)

                def chunk(n, c, at):
                    qh = QT[n % 4][0]
                    heads, a, m = max_chunks(n)[c]
                    b = ring_bank(("chunk", n, c), at)
                    pe.wait_ge(qh_done, at(n + 1, NT))
                    diag = a + m == (tile_of(n) + 1) * P
                    for i, j in enumerate(heads):
                        last = pe.matmul(b[:, i * m:(i + 1) * m], qh[0:QW, j * P:(j + 1) * P], KTh[0:QW, a:a + m],
                                         start=(i == 0), stop=not diag, skip_group_check=True)
                    if diag:
                        for i in range(len(heads)):
                            last = pe.matmul(b[:, (i + 1) * m - P:(i + 1) * m], identb[:], maskqk[:],
                                             start=False, stop=True, skip_group_check=True)
                    last.then_inc(p1_psum, 1)

                def max_row(n, at):
                    pe.wait_ge(m_done, at(n + 1, NT))
                    if n >= 1:
                        pe.wait_ge(mrow_done, at(n, NT))
                    for j in range(HG):
                        last = pe.matmul(bank[TB][QW:QK, j * P:(j + 1) * P], negm[n % 2][:, j:j + 1], identb[:],
                                         start=True, stop=True)
                    last.then_inc(mrow_psum, 1)

                def scores(x, at):
                    n, k = unit_of(x)
                    b = bank[ST[x % 3]]
                    if x >= 3:
                        pe.wait_ge(p_done, at(x - 2, STEPS))
                    if k == 0:
                        pe.wait_ge(mrow_done, at(n + 1, NT))
                        pe.wait_ge(ql_done, at(n + 1, NT))
                    qh, ql = QT[n % 4]
                    kt = slice(k * P, (k + 1) * P)
                    diag = k == tile_of(n)
                    pe.matmul(b[:], KTh[:, kt], qh[:], start=True, stop=False)
                    pe.matmul(b[:], KTh[:, kt], ql[:], start=False, stop=False)
                    last = pe.matmul(b[:], KTl[:, kt], qh[:], start=False, stop=not diag)
                    if diag:
                        last = pe.matmul(b[:].rearrange("p (j n) -> p j n", j=HG), identb[:],
                                         maskkq[:].unsqueeze(1).to_broadcast([P, HG, P]), start=False, stop=True)
                    last.then_inc(s_psum, 1)

                def values(x, at):
                    n, k = unit_of(x)
                    pe.wait_ge(p_done, at(x + 1, STEPS))
                    if k == 0 and n >= 2:
                        pe.wait_ge(o_done, at(n - 1, NT))
                    for j in range(HG):
                        last = pe.matmul(bank[OD[n % 2]][32 * j:32 * j + 32, 0:P], KTM[:, k, ROPE:QW],
                                         PT[x % NPT][:, j * P:(j + 1) * P], start=(k == 0), stop=(k == tile_of(n)),
                                         skip_group_check=True)
                    last.then_inc(pv_done, 1)

                def denominator(n, at):
                    t = tile_of(n)
                    last_step = step_of(n, t)
                    if t:
                        pe.wait_ge(sum_done, at(sums_through(last_step), STEPS - NT))
                    src = PS[n % 2] if t else PT[last_step % NPT]
                    for j in range(HG):
                        last = pe.matmul(bank[OD[n % 2]][32 * j:32 * j + 32, P:2 * P], ones[:], src[:, j * P:(j + 1) * P],
                                         start=False, stop=True, skip_group_check=True)
                    last.then_inc(den_psum, 1)

                def side(kind, n, c, at):
                    if kind == "project":
                        project(n, at)
                    elif kind == "transpose":
                        transpose(n, at)
                    elif kind == "chunk":
                        chunk(n, c, at)
                    elif kind == "maxrow":
                        max_row(n, at)
                    else:
                        denominator(n, at)

                def prologue():
                    pe.wait_ge(qlzero, 4)
                    for e in PROLOGUE:
                        side(*e, lambda v, per: v)
                    for x in range(2):
                        scores(x, lambda v, per: v)

                def step(x, at):
                    if x + 2 < NG * STEPS:
                        scores(x + 2, at)
                    for e in side_work(x):
                        side(*e, at)
                    values(x, at)

                groups(pe, prologue, step, lambda: denominator(UNITS - 1, lambda v, per: v))

            @block.vector
            def _(dve):
                def rope(n, at):
                    t = tile_of(n)
                    q = bank[RING[place[("project", n, 0)] % 2]][:, 0:HG * QW].rearrange("p (j w) -> p j w", j=HG)
                    rot = q[:, :, 0:ROPE].rearrange("p j (a i) -> p j a i", a=2)
                    dve.wait_ge(q_psum, at(n + 1, NT))
                    if n >= 2:
                        dve.wait_ge(rope_done, at(n - 1, NT))
                        dve.wait_ge(t_psum, at(n - 1, NT))
                    dve.tensor_copy(Qtm[n % 2][:, :, ROPE:QW], q[:, :, ROPE:QW])
                    dve.tensor_tensor(RA[n % 2][:], rot, cosT[:, t].unsqueeze(1).to_broadcast([P, HG, 2, 32]), ALU.mult)
                    dve.tensor_tensor(RB[n % 2][:], rot[:, :, ::-1, :],
                                      sinT[:, t].unsqueeze(1).to_broadcast([P, HG, 2, 32]), ALU.mult).then_inc(ra_done, 1)

                def low_part(n, at):
                    qh, ql = QT[n % 4]
                    dve.wait_ge(qh_done, at(n + 1, NT))
                    dve.tensor_tensor(ql[0:QW, :], bank[TB][0:QW, :], qh[0:QW, :].bitcast(F32),
                                      ALU.subtract).then_inc(ql_done, 1)

                def maxima(n, c, at):
                    m, chunks = mx[n % 2], max_chunks(n)
                    heads, a, w = chunks[c]
                    dve.wait_ge(p1_psum, at(chunk_of(n, c) + 1, CHUNKS))
                    dve.tensor_reduce(m[:, heads[0]:heads[-1] + 1, a // 512:a // 512 + 1],
                                      bank[RING[place[("chunk", n, c)] % 2]][:, 0:len(heads) * w].rearrange(
                                          "p (s n) -> p s n", n=w), AX_X, ALU.max).then_inc(p1_read, 1)
                    if c == len(chunks) - 1:
                        dve.wait_ge(p1_read, at(chunk_of(n, c) + 1, CHUNKS))
                        if n >= 2:
                            dve.wait_ge(mrow_psum, at(n - 1, NT))
                        dve.tensor_reduce(negm[n % 2][:], m[:, :, 0:a // 512 + 1], AX_X, ALU.max,
                                          negate=True).then_inc(m_done, 1)

                def normalize(n, at):
                    od, t = bank[OD[n % 2]], tile_of(n)
                    dve.wait_ge(den_psum, at(n + 1, NT))
                    dve.reciprocal(rD[n % 2][:], od[:, P:2 * P]).then_inc(rd_done, 1)
                    dve.wait_ge(rd_done, at(n + 1, NT))
                    dve.tensor_tensor(OT[:, bass.ds(at(n // NT, 1) * S + t * P, P)], od[:, 0:P], rD[n % 2][:],
                                      ALU.mult).then_inc(o_done, 1)

                def side(kind, n, c, at):
                    if kind == "project":
                        rope(n, at)
                    elif kind == "transpose":
                        low_part(n, at)
                    elif kind == "chunk":
                        maxima(n, c, at)
                    elif kind == "denominator":
                        normalize(n, at)

                def prologue():
                    for i in range(4):
                        dve.memset(QT[i][1][:].bitcast(F32), 0.0).then_inc(qlzero, 1)
                    dve.wait_ge(qlzero, 4)
                    for e in PROLOGUE:
                        side(*e, lambda v, per: v)

                def step(x, at):
                    for e in side_work(x):
                        side(*e, at)

                groups(dve, prologue, step, lambda: normalize(UNITS - 1, lambda v, per: v))

            @block.gpsimd
            def _(pool):
                def rope_sum(n, at):
                    pool.wait_ge(ra_done, at(n + 1, NT))
                    pool.tensor_tensor(Qtm[n % 2][:, :, 0:ROPE], RA[n % 2][:].rearrange("p j a i -> p j (a i)"),
                                       RB[n % 2][:].rearrange("p j a i -> p j (a i)"), ALU.add).then_inc(rope_done, 1)

                def prologue():
                    for kind, n, _ in PROLOGUE:
                        if kind == "project":
                            rope_sum(n, lambda v, per: v)

                def add(x, at):
                    n, k = unit_of(x)
                    pool.wait_ge(p_done, at(x + 1, STEPS))
                    if k == 1 and n >= 2:
                        pool.wait_ge(den_psum, at(n - 1, NT))
                    if k >= 2:
                        pool.wait_ge(sum_done, at(sums_through(x - 1), STEPS - NT))
                    pool.tensor_tensor(PS[n % 2][:], PT[(x - 1) % NPT][:] if k == 1 else PS[n % 2][:], PT[x % NPT][:],
                                       ALU.add).then_inc(sum_done, 1)

                def step(x, at):
                    if unit_of(x)[1]:
                        add(x, at)
                    for kind, n, _ in side_work(x):
                        if kind == "project":
                            rope_sum(n, at)

                groups(pool, prologue, step)

            @block.scalar
            def _(act):
                def high_part(n, at):
                    act.wait_ge(t_psum, at(n + 1, NT))
                    act.copy(QT[n % 4][0][0:QW, :], bank[TB][0:QW, :]).then_inc(qh_done, 1)

                def copy_max_row(n, at):
                    act.wait_ge(mrow_psum, at(n + 1, NT))
                    act.copy(QT[n % 4][0][QW:QK, :], bank[TB][QW:QK, :]).then_inc(mrow_done, 1)

                def probabilities(x, at):
                    act.wait_ge(s_psum, at(x + 1, STEPS))
                    if x >= NPT:
                        n, k = unit_of(x - NPT)
                        act.wait_ge(pv_done, at(x - NPT + 1, STEPS))
                        y = x - NPT + 1 if unit_of(x - NPT + 1)[1] == 1 else x - NPT
                        act.wait_ge(sum_done, at(sums_through(y), STEPS - NT))
                        if tile_of(n) == 0:
                            act.wait_ge(den_psum, at(n + 1, NT))
                    act.activation(PT[x % NPT][:], bank[ST[x % 3]][:], ACT.Exp, scale=SOFTMAX_SCALE).then_inc(p_done, 1)

                def side(kind, n, at):
                    if kind == "transpose":
                        high_part(n, at)
                    elif kind == "maxrow":
                        copy_max_row(n, at)

                def prologue():
                    for kind, n, _ in PROLOGUE:
                        side(kind, n, lambda v, per: v)
                    for x in range(2):
                        probabilities(x, lambda v, per: v)

                def step(x, at):
                    if x + 2 < NG * STEPS:
                        probabilities(x + 2, at)
                    for kind, n, _ in side_work(x):
                        side(kind, n, at)

                groups(act, prologue, step)

        def project_onto_x(tag, lhs, rhs, n, tiles=range(NT)):
            psum_full, added = again("psum_full", len(tiles)), again("added", len(tiles))
            with nc.Block() as block:
                @block.tensor
                def _(pe):
                    for i, t in enumerate(tiles):
                        if i >= 2:
                            pe.wait_ge(*added(i - 1))
                        for k in range(n):
                            last = pe.matmul(bank[i % 2][:], lhs(k, t), rhs(k), start=(k == 0), stop=(k == n - 1))
                        last.then_inc(psum_full.sem, 1)

                @block.vector
                def _(dve):
                    for i, t in enumerate(tiles):
                        dve.wait_ge(*psum_full(i + 1))
                        dve.tensor_tensor(X[:, t, :], bank[i % 2][:], X[:, t, :], ALU.add).then_inc(added.sem, 1)

        project_onto_x("attn", lambda g, t: OT[:, g * S + t * P:g * S + (t + 1) * P], lambda g: WVO[:, g, :], NG)

        def ffn(tag):
            layer_norm(tag)
            mem = ExitStack()
            WgT = sb_in(mem, f"WgT_{tag}", [P, DC, FF])
            WuT = sb_in(mem, f"WuT_{tag}", [P, DC, FF])
            WdT = sb_in(mem, f"WdT_{tag}", [P, FT, DM])
            nat = [sb_in(mem, f"nat{i}_{tag}", [P, FT * DM]) for i in range(2)]
            HT = sb_in(mem, f"HT_{tag}", [P, FT, CH])
            SG = [sb_in(mem, f"SG{i}_{tag}", [P, CH]) for i in range(2)]
            mem.close()
            ld = [again(f"ffn_ld{i}", 16 if i == 2 else 32) for i in range(3)]
            nat_free = again("nat_free", 1)
            tp, td = again("wt_psum", 3 * FT), again("wt_done", 3 * FT)
            gate_psum, up_psum, silu_done, h_done = (again(n, NCH * FT) for n in
                                                     ("gate_psum", "up_psum", "silu_done", "h_done"))
            down_psum, down_added = again("down_psum", NT), again("down_added", NT)
            rows = [min(P, FF - f * P) for f in range(FT)]
            FULL = FF // P
            with nc.Block() as block:
                @block.sync
                def _(sp):
                    for i, w in enumerate((w_gate, w_up)):
                        v = nat[i][:].rearrange("p (f d) -> p f d", f=FT)
                        sp.dma_start(v[:, 0:FULL, :], w[0:FULL * P].rearrange("(f p) d -> p f d", p=P)).then_inc(ld[i].sem, 16)
                        sp.dma_start(v[0:FF - FULL * P, FULL, :], w[FULL * P:FF]).then_inc(ld[i].sem, 16)
                    sp.wait_ge(*nat_free(1))
                    sp.dma_start(nat[0][:, 0:DC * FF].rearrange("p (c f) -> p c f", c=DC),
                                 w_down.rearrange("(c p) f -> p c f", p=P)).then_inc(ld[2].sem, 16)

                @block.tensor
                def _(pe):
                    i = 0
                    for m in range(2):
                        pe.wait_ge(*ld[m](32))
                        for f in range(FT):
                            if i >= 2:
                                pe.wait_ge(*td(i - 1))
                            v = nat[m][:].rearrange("p (f d) -> p f d", f=FT)
                            for c in range(DC):
                                last = pe.transpose(bank[i % 2][:, c * P:c * P + rows[f]],
                                                    v[0:rows[f], f, c * P:(c + 1) * P], ident[0:rows[f], 0:rows[f]])
                            last.then_inc(tp.sem, 1)
                            i += 1
                    pe.wait_ge(*ld[2](16))
                    v = nat[0][:, 0:DC * FF].rearrange("p (c f) -> p c f", c=DC)
                    for f in range(FT):
                        pe.wait_ge(*td(i - 1))
                        for c in range(DC):
                            last = pe.transpose(bank[i % 2][0:rows[f], c * P:(c + 1) * P],
                                                v[:, c, f * P:f * P + rows[f]], ident[:])
                        last.then_inc(tp.sem, 1)
                        i += 1
                    pe.wait_ge(*td(3 * FT))
                    for ch in range(NCH):
                        for f in range(FT):
                            n = ch * FT + f
                            if n >= 2:
                                pe.wait_ge(*h_done(n - 1))
                            for w, b, s in ((WgT, bank[2 + n % 2], gate_psum.sem), (WuT, bank[4 + n % 2], up_psum.sem)):
                                for c in range(DC):
                                    last = pe.matmul(b[0:rows[f], :], w[:, c, f * P:f * P + rows[f]],
                                                     XnT[:, c, ch * CH:(ch + 1) * CH], start=(c == 0), stop=(c == DC - 1))
                                last.then_inc(s, 1)
                        for k in range(TPC):
                            t = ch * TPC + k
                            if t >= 2:
                                pe.wait_ge(*down_added(t - 1))
                            for f in range(FT):
                                if k == 0:
                                    pe.wait_ge(*h_done(ch * FT + f + 1))
                                last = pe.matmul(bank[6 + t % 2][:], HT[0:rows[f], f, k * P:(k + 1) * P],
                                                 WdT[0:rows[f], f, :], start=(f == 0), stop=(f == FT - 1))
                            last.then_inc(down_psum.sem, 1)

                @block.scalar
                def _(act):
                    for i in range(3 * FT):
                        m, f = divmod(i, FT)
                        act.wait_ge(*tp(i + 1))
                        if m < 2:
                            act.copy((WgT, WuT)[m][:, :, f * P:f * P + rows[f]],
                                     bank[i % 2][:].rearrange("p (c n) -> p c n", c=DC)[:, :, 0:rows[f]]).then_inc(td.sem, 1)
                        else:
                            act.copy(WdT[0:rows[f], f, :], bank[i % 2][0:rows[f], :]).then_inc(td.sem, 1)
                        if i == FT - 1:
                            act.wait_ge(*td(FT))
                            act.sem_inc(nat_free.sem, 1)
                    for n in range(NCH * FT):
                        r = rows[n % FT]
                        act.wait_ge(*gate_psum(n + 1))
                        if n >= 2:
                            act.wait_ge(*h_done(n - 1))
                        act.activation(SG[n % 2][0:r, :], bank[2 + n % 2][0:r, :], ACT.Silu).then_inc(silu_done.sem, 1)

                @block.vector
                def _(dve):
                    for ch in range(NCH):
                        for f in range(FT):
                            n = ch * FT + f
                            dve.wait_ge(*up_psum(n + 1))
                            dve.wait_ge(*silu_done(n + 1))
                            if ch:
                                dve.wait_ge(*down_psum(ch * TPC))
                            dve.tensor_tensor(HT[0:rows[f], f, :], bank[4 + n % 2][0:rows[f], :],
                                              SG[n % 2][0:rows[f], :], ALU.mult).then_inc(h_done.sem, 1)
                        for k in range(TPC):
                            t = ch * TPC + k
                            dve.wait_ge(*down_psum(t + 1))
                            dve.tensor_tensor(X[:, t, :], bank[6 + t % 2][:], X[:, t, :], ALU.add).then_inc(down_added.sem, 1)

        ffn("f1")

        layer_norm("s")
        ssm = ExitStack()
        XS = sb_in(ssm, "XS", [P, DJ, S])
        G = sb_in(ssm, "G", [P, DJ, S])
        WoutT = sb_in(ssm, "WoutT", [P, DJ, DM])
        WxT = sb_in(ssm, "WxT", [P, DJ, RK + 2 * NS])
        WdtT = sb_in(ssm, "WdtT", [RK, DI])
        convw = sb_in(ssm, "convw", [P, DJ, KC])
        convb = sb_in(ssm, "convb", [P, DJ])
        bdt = sb_in(ssm, "bdt", [P, DJ])
        dsk = sb_in(ssm, "dsk", [P, DJ])
        Aneg = sb_in(ssm, "Aneg", [P, DJ, NS])
        state = sb_in(ssm, "state", [P, DJ, NS])
        inp = ExitStack()
        WinT = sb_in(inp, "WinT", [P, DC, 2 * DI])
        natw = [sb_in(inp, f"natw{i}", [P, 4, DM]) for i in range(2)]
        XP = [sb_in(inp, f"XP{i}", [P, KC - 1 + CH]) for i in range(2)]
        halo = sb_in(inp, "halo", [P, DJ, KC - 1])
        acc = [sb_in(inp, f"acc{i}", [P, CH]) for i in range(2)]
        wx_nat = sb_in(inp, "wx_nat", [RK + 2 * NS, DI])
        wdt_nat = sb_in(inp, "wdt_nat", [P, DJ, RK])
        wout_nat = sb_in(inp, "wout_nat", [P, DC, DI])
        inp.close()

        ld_in = [sem(f"ld_in{i}") for i in range(4)]
        ld_s, ld_v = sem("ld_s"), sem("ld_v")
        in_t, in_e = sem("in_t"), sem("in_e")
        xp_psum, xp_done, conv_step, conv_done, xs_done = (sem("xp_psum"), sem("xp_done"), sem("conv_step"),
                                                           sem("conv_done"), sem("xs_done"))
        halo_done, g_psum, g_done = sem("halo_done"), sem("g_psum"), sem("g_done")
        a_clamped, a_step, zero_done = sem("a_clamped"), sem("a_step"), sem("zero_done")
        NW = 4
        with nc.Block() as block:
            @block.sync
            def _(sp):
                rows_in = w_in.rearrange("(q f p) d -> q p f d", p=P, q=4)
                for q in range(4):
                    if q >= 2:
                        sp.wait_ge(in_e, 4 * (q - 1))
                    sp.dma_start(natw[q % 2][:], rows_in[q]).then_inc(ld_in[q], 16)
                    if q == 1:
                        sp.dma_start(wx_nat[:], w_x).then_inc(ld_s, 16)
                        sp.dma_start(wdt_nat[:], w_dt.rearrange("(j p) r -> p j r", p=P)).then_inc(ld_s, 16)
                        sp.dma_start(wout_nat[:], w_out.rearrange("(c p) f -> p c f", p=P)).then_inc(ld_s, 16)
                        sp.dma_start(convw[:], conv_w.rearrange("(j p) k -> p j k", p=P)).then_inc(ld_v, 16)
                        sp.dma_start(Aneg[:], a_log.rearrange("(j p) n -> p j n", p=P)).then_inc(ld_v, 16)
                        with nc.allow_non_contiguous_dma(reason="one value to a partition"):
                            for dst, src in ((convb, conv_b), (bdt, b_dt), (dsk, d_skip)):
                                sp.dma_start(dst[:], src.rearrange("(j p) -> p j", p=P)).then_inc(ld_v, 16)

            @block.tensor
            def _(pe):
                i = 0
                for q in range(4):
                    pe.wait_ge(ld_in[q], 16)
                    for f in range(4):
                        if i >= 2:
                            pe.wait_ge(in_e, i - 1)
                        for c in range(DC):
                            last = pe.transpose(bank[i % 2][:, c * P:(c + 1) * P], natw[q % 2][:, f, c * P:(c + 1) * P], ident[:])
                        last.then_inc(in_t, 1)
                        i += 1
                pe.wait_ge(ld_s, 48)
                for j in range(DJ):
                    pe.wait_ge(in_e, i - 1)
                    for c in range(DC):
                        last = pe.transpose(bank[i % 2][:, c * P:(c + 1) * P], wout_nat[:, c, j * P:(j + 1) * P], ident[:])
                    last.then_inc(in_t, 1)
                    i += 1
                pe.wait_ge(in_e, i - 1)
                W3 = RK + 2 * NS
                for j in range(DJ):
                    last = pe.transpose(bank[i % 2][:, j * W3:(j + 1) * W3], wx_nat[:, j * P:(j + 1) * P], ident[0:W3, 0:W3])
                last.then_inc(in_t, 1)
                i += 1
                for m in range(2):
                    pe.wait_ge(in_e, i - 1)
                    for k in range(4):
                        last = pe.transpose(bank[i % 2][0:RK, k * P:(k + 1) * P], wdt_nat[:, 4 * m + k, :], ident[:])
                    last.then_inc(in_t, 1)
                    i += 1
                pe.wait_ge(in_e, i)
                for ch in range(NCH):
                    for j in range(DJ):
                        n = ch * DJ + j
                        for part, b, full, free in ((0, bank[2 + n % 2], xp_psum, xp_done), (1, bank[4 + n % 2], g_psum, g_done)):
                            if n >= 2:
                                pe.wait_ge(free, n - 1)
                            for c in range(DC):
                                o = part * DI + j * P
                                last = pe.matmul(b[:], WinT[:, c, o:o + P], XnT[:, c, ch * CH:(ch + 1) * CH],
                                                 start=(c == 0), stop=(c == DC - 1))
                            last.then_inc(full, 1)

            @block.scalar
            def _(act):
                for i in range(16):
                    act.wait_ge(in_t, i + 1)
                    act.copy(WinT[:, :, i * P:(i + 1) * P], bank[i % 2][:].rearrange("p (c n) -> p c n", c=DC)).then_inc(in_e, 1)
                for j in range(DJ):
                    act.wait_ge(in_t, 17 + j)
                    act.copy(WoutT[:, j, :], bank[j % 2][:]).then_inc(in_e, 1)
                act.wait_ge(in_t, 25)
                act.copy(WxT[:].rearrange("p j w -> p (j w)"), bank[0][:]).then_inc(in_e, 1)
                for m in range(2):
                    act.wait_ge(in_t, 26 + m)
                    act.copy(WdtT[:, m * 512:(m + 1) * 512], bank[(1 + m) % 2][0:RK, :]).then_inc(in_e, 1)
                act.wait_ge(a_clamped, 1)
                act.activation(Aneg[:], Aneg[:], ACT.Exp).then_inc(a_step, 1)
                act.wait_ge(a_step, 1)
                act.mul(Aneg[:], Aneg[:], -1.0).then_inc(a_step, 1)

                def conv_silu(n):
                    ch, j = divmod(n, DJ)
                    act.wait_ge(conv_done, n + 1)
                    act.activation(XS[:, j, ch * CH:(ch + 1) * CH], acc[n % 2][:], ACT.Silu,
                                   bias=convb[:, j:j + 1]).then_inc(xs_done, 1)

                for n in range(NCH * DJ):
                    ch, j = divmod(n, DJ)
                    act.wait_ge(xp_psum, n + 1)
                    if n >= 2:
                        act.wait_ge(conv_done, n - 1)
                        act.wait_ge(halo_done, 2 * n - 2)
                    act.copy(XP[n % 2][:, KC - 1:], bank[2 + n % 2][:]).then_inc(xp_done, 1)
                    act.wait_ge(g_psum, n + 1)
                    act.activation(G[:, j, ch * CH:(ch + 1) * CH], bank[4 + n % 2][:], ACT.Silu).then_inc(g_done, 1)
                    if n:
                        conv_silu(n - 1)
                conv_silu(NCH * DJ - 1)

            @block.gpsimd
            def _(pool):
                pool.memset(halo[:], 0.0).then_inc(zero_done, 1)
                pool.memset(state[:], 0.0).then_inc(zero_done, 1)
                pool.wait_ge(zero_done, 1)
                for n in range(NCH * DJ):
                    ch, j = divmod(n, DJ)
                    if n >= 2:
                        pool.wait_ge(conv_done, n - 1)
                    if ch:
                        pool.wait_ge(halo_done, 2 * (n - DJ) + 2)
                    pool.tensor_copy(XP[n % 2][:, 0:KC - 1], halo[:, j, :]).then_inc(halo_done, 1)
                    pool.wait_ge(xp_done, n + 1)
                    pool.wait_ge(halo_done, 2 * n + 1)
                    pool.tensor_copy(halo[:, j, :], XP[n % 2][:, CH:CH + KC - 1]).then_inc(halo_done, 1)

            @block.vector
            def _(dve):
                dve.wait_ge(ld_v, 80)
                dve.tensor_scalar(Aneg[:], Aneg[:], A_LOG_MAX, None, ALU.min).then_inc(a_clamped, 1)
                for n in range(NCH * DJ):
                    ch, j = divmod(n, DJ)
                    dve.wait_ge(xp_done, n + 1)
                    dve.wait_ge(halo_done, 2 * n + 1)
                    if n >= 2:
                        dve.wait_ge(xs_done, n - 1)
                    a = acc[n % 2][:]
                    dve.tensor_scalar(a, XP[n % 2][:, KC - 1:], convw[:, j, KC - 1:KC], None, ALU.mult).then_inc(conv_step, 1)
                    for k in range(KC - 1):
                        dve.wait_ge(conv_step, 3 * n + k + 1)
                        dve.scalar_tensor_tensor(a, XP[n % 2][:, k:k + CH], convw[:, j, k:k + 1], a, ALU.mult,
                                                 ALU.add).then_inc(conv_done if k == KC - 2 else conv_step, 1)

        W3 = RK + 2 * NS
        for ch in range(NCH):
            lo = ch * CH
            mem = ExitStack()
            BC = sb_in(mem, f"BC{ch}", [P, 2 * NS, CH])
            SS = sb_in(mem, f"SS{ch}", [P, TPC, W3])
            SSq = sb_in(mem, f"SSq{ch}", [P, TPC, W3])
            SSn = sb_in(mem, f"SSn{ch}", [P, TPC, W3])
            m3 = sb_in(mem, f"m3{ch}", [P, 3, TPC])
            r3 = sb_in(mem, f"r3{ch}", [P, 3, TPC])
            ssT = sb_in(mem, f"ssT{ch}", [W3, CH])
            work = ExitStack()
            Z = [sb_in(work, f"Z{ch}{i}", [P, CH]) for i in range(2)]
            E = sb_in(work, f"E{ch}", [P, CH])
            L = [sb_in(work, f"L{ch}{i}", [P, CH]) for i in range(2)]
            DT = [sb_in(work, f"DT{ch}{i}", [P, CH]) for i in range(2)]
            DTU = [sb_in(work, f"DTU{ch}{i}", [P, CH]) for i in range(2)]
            dA = [XnT[:, (0 + i) // 2, (i % 2) * CH:(i % 2 + 1) * CH] for i in range(2)]
            dBu = [XnT[:, (2 + i) // 2, (i % 2) * CH:(i % 2 + 1) * CH] for i in range(2)]
            Hs = [XnT[:, (4 + i) // 2, (i % 2) * CH:(i % 2 + 1) * CH] for i in range(2)]
            HC = [XnT[:, (6 + i) // 2, (i % 2) * CH:(i % 2 + 1) * CH] for i in range(2)]
            work.close()
            mem.close()
            sx_psum, sx_step, sx_ms = again("sx_psum", 1), again("sx_step", 2), again("sx_ms", 3)
            sx_eps, sx_r, sx_n = again("sx_eps", 3), again("sx_r", 1), again("sx_n", 3)
            st_psum, st_done = again("st_psum", 1), again("st_done", 1)
            bc_psum, bc_done = again("bc_psum", 2 * NS), again("bc_done", 2 * NS)
            GROUPS = ((0, RK), (RK, RK + NS), (RK + NS, W3))
            with nc.Block() as block:
                @block.tensor
                def _(pe):
                    for k in range(TPC):
                        for j in range(DJ):
                            last = pe.matmul(bank[0][:, k * W3:(k + 1) * W3], XS[:, j, lo + k * P:lo + (k + 1) * P],
                                             WxT[:, j, :], start=(j == 0), stop=(j == DJ - 1))
                    last.then_inc(sx_psum.sem, 1)
                    pe.wait_ge(*sx_n(3))
                    for k in range(TPC):
                        last = pe.transpose(bank[1][0:W3, k * P:(k + 1) * P], SSn[:, k, :], ident[:])
                    last.then_inc(st_psum.sem, 1)
                    pe.wait_ge(*st_done(1))
                    for n in range(2 * NS):
                        if n >= 2:
                            pe.wait_ge(*bc_done(n - 1))
                        pe.matmul(bank[2 + n % 2][:], ident[0:W3, RK + n:RK + n + 1].to_broadcast([W3, P]), ssT[:],
                                  start=True, stop=True).then_inc(bc_psum.sem, 1)

                @block.vector
                def _(dve):
                    dve.wait_ge(*sx_psum(1))
                    dve.tensor_copy(SS[:].rearrange("p k w -> p (k w)"), bank[0][:, 0:TPC * W3]).then_inc(sx_step.sem, 1)
                    dve.wait_ge(*sx_step(1))
                    dve.tensor_tensor(SSq[:], SS[:], SS[:], ALU.mult).then_inc(sx_step.sem, 1)
                    dve.wait_ge(*sx_step(2))
                    for i, (a, b) in enumerate(GROUPS):
                        dve.tensor_reduce(m3[:, i, :], SSq[:, :, a:b], AX_X, ALU.add).then_inc(sx_ms.sem, 1)
                    dve.wait_ge(*sx_r(1))
                    for i, (a, b) in enumerate(GROUPS):
                        dve.tensor_tensor(SSn[:, :, a:b], SS[:, :, a:b], r3[:, i, :].unsqueeze(2).to_broadcast([P, TPC, b - a]),
                                          ALU.mult).then_inc(sx_n.sem, 1)

                @block.gpsimd
                def _(pool):
                    pool.wait_ge(*sx_ms(3))
                    for i, (a, b) in enumerate(GROUPS):
                        pool.tensor_scalar(veps[:, TPC * i:TPC * i + TPC], m3[:, i, :], 1.0 / (b - a), 1e-6, ALU.mult,
                                           ALU.add).then_inc(sx_eps.sem, 1)
                    pool.wait_ge(*sx_eps(3))
                    pool.tensor_tensor(r3[:].rearrange("p i k -> p (i k)"), veps[:, 0:3 * TPC], neghalf[:, 0:3 * TPC],
                                       ALU.pow).then_inc(sx_r.sem, 1)

                @block.scalar
                def _(act):
                    act.wait_ge(*st_psum(1))
                    act.copy(ssT[:], bank[1][0:W3, :]).then_inc(st_done.sem, 1)
                    for n in range(2 * NS):
                        act.wait_ge(*bc_psum(n + 1))
                        act.copy(BC[:, n, :], bank[2 + n % 2][:]).then_inc(bc_done.sem, 1)

            z_psum, z_done, l_done, dt_done, dtu_done, yg_done, y_done = (
                again(n, DJ) for n in ("z_psum", "z_done", "l_done", "dt_done", "dtu_done", "yg_done", "y_done"))
            e_step = again("e_step", 2 * DJ)
            da_done, db_done, h_done, hc_done, y_acc, st_copied = (
                again(n, DJ * NS) for n in ("da_done", "db_done", "hs_done", "hc_done", "y_acc", "st_copied"))
            with nc.Block() as block:
                @block.tensor
                def _(pe):
                    def delta(j):
                        if j >= 2:
                            pe.wait_ge(*z_done(j - 1))
                        pe.matmul(bank[4 + j % 2][:], WdtT[:, j * P:(j + 1) * P], ssT[0:RK, :], start=True,
                                  stop=True).then_inc(z_psum.sem, 1)

                    delta(0)
                    for j in range(DJ):
                        if j + 1 < DJ:
                            delta(j + 1)
                        for n in range(NS):
                            i = j * NS + n
                            pe.wait_ge(*hc_done(i + 1))
                            if n == 0 and j >= 2:
                                pe.wait_ge(*yg_done(j - 1))
                            pe.matmul(bank[j % 2][:], ident[:], HC[i % 2], start=(n == 0),
                                      stop=(n == NS - 1)).then_inc(y_acc.sem, 1)

                @block.scalar
                def _(act):
                    def softplus(j):
                        act.wait_ge(*z_done(j + 1))
                        if j >= 2:
                            act.wait_ge(*dt_done(j - 1))
                        act.activation(E[:], Z[j % 2][:], ACT.Abs).then_inc(e_step.sem, 1)
                        act.wait_ge(*e_step(2 * j + 1))
                        act.activation(E[:], E[:], ACT.Exp, scale=-1.0).then_inc(e_step.sem, 1)
                        act.wait_ge(*e_step(2 * j + 2))
                        act.activation(L[j % 2][:], E[:], ACT.Ln, bias=1.0).then_inc(l_done.sem, 1)

                    softplus(0)
                    for j in range(DJ):
                        for n in range(NS):
                            i = j * NS + n
                            if n == 0:
                                act.wait_ge(*dt_done(j + 1))
                            if i >= 2:
                                act.wait_ge(*h_done(i - 1))
                            act.activation(dA[i % 2], DT[j % 2][:], ACT.Exp, scale=Aneg[:, j, n:n + 1]).then_inc(da_done.sem, 1)
                            if n == 8 and j + 1 < DJ:
                                softplus(j + 1)

                @block.gpsimd
                def _(pool):
                    for j in range(DJ):
                        pool.wait_ge(*dtu_done(j + 1))
                        for n in range(NS):
                            i = j * NS + n
                            if i >= 2:
                                pool.wait_ge(*h_done(i - 1))
                            pool.tensor_tensor(dBu[i % 2], DTU[j % 2][:], BC[:, n, :], ALU.mult).then_inc(db_done.sem, 1)

                @block.vector
                def _(dve):
                    def bias(j):
                        dve.wait_ge(*z_psum(j + 1))
                        if j >= 2:
                            dve.wait_ge(*dt_done(j - 1))
                        dve.tensor_scalar(Z[j % 2][:], bank[4 + j % 2][:], bdt[:, j:j + 1], None, ALU.add).then_inc(z_done.sem, 1)

                    def delta(j):
                        dve.wait_ge(*l_done(j + 1))
                        if j >= 2:
                            dve.wait_ge(*da_done(NS * (j - 1)))
                            dve.wait_ge(*db_done(NS * (j - 1)))
                        dve.scalar_tensor_tensor(DT[j % 2][:], Z[j % 2][:], 0.0, L[j % 2][:], ALU.max, ALU.add).then_inc(dt_done.sem, 1)
                        dve.wait_ge(*dt_done(j + 1))
                        dve.tensor_tensor(DTU[j % 2][:], DT[j % 2][:], XS[:, j, lo:lo + CH], ALU.mult).then_inc(dtu_done.sem, 1)

                    def weigh(i):
                        dve.wait_ge(*h_done(i + 1))
                        if i >= 2:
                            dve.wait_ge(*y_acc(i - 1))
                        dve.tensor_tensor(HC[i % 2], Hs[i % 2], BC[:, NS + i % NS, :], ALU.mult).then_inc(hc_done.sem, 1)

                    def gate(j):
                        dve.wait_ge(*y_acc(NS * (j + 1)))
                        dve.scalar_tensor_tensor(XS[:, j, lo:lo + CH], XS[:, j, lo:lo + CH], dsk[:, j:j + 1], bank[j % 2][:], ALU.mult,
                                                 ALU.add).then_inc(yg_done.sem, 1)
                        dve.wait_ge(*yg_done(j + 1))
                        dve.tensor_tensor(XS[:, j, lo:lo + CH], XS[:, j, lo:lo + CH], G[:, j, lo:lo + CH], ALU.mult).then_inc(y_done.sem, 1)

                    bias(0)
                    delta(0)
                    for j in range(DJ):
                        for n in range(NS):
                            i = j * NS + n
                            dve.wait_ge(*da_done(i + 1))
                            dve.wait_ge(*db_done(i + 1))
                            if i >= 2:
                                dve.wait_ge(*hc_done(i - 1))
                                dve.wait_ge(*st_copied(i - 1))
                            dve.tensor_tensor_scan(Hs[i % 2], dA[i % 2], dBu[i % 2], state[:, j, n:n + 1], ALU.mult,
                                                   ALU.add).then_inc(h_done.sem, 1)
                            if i:
                                weigh(i - 1)
                            dve.wait_ge(*h_done(i + 1))
                            dve.tensor_copy(state[:, j, n:n + 1], Hs[i % 2][:, CH - 1:CH]).then_inc(st_copied.sem, 1)
                            if n == 4 and j + 1 < DJ:
                                bias(j + 1)
                            if n == 12 and j + 1 < DJ:
                                delta(j + 1)
                            if n == 2 and j:
                                gate(j - 1)
                    weigh(DJ * NS - 1)
                    gate(DJ - 1)

            project_onto_x(f"ssm{ch}", lambda j, t: XS[:, j, t * P:(t + 1) * P], lambda j: WoutT[:, j, :], DJ,
                           tiles=range(ch * TPC, (ch + 1) * TPC))
        ssm.close()

        ffn("f2")
        stored = sem("stored")
        with nc.Block() as block:
            @block.sync
            def _(sp):
                sp.dma_start(out[0].rearrange("(t p) d -> p t d", p=P), X[:]).then_inc(stored, 16)
                sp.wait_ge(stored, 16)


NAMES = ["x", "wq_a", "q_a_ln_w", "wq_b", "wkv_a", "kv_a_ln_w", "wkv_b", "wo"]
INPUTS = ([f"L0_attn_a_{n}" for n in NAMES]
          + [f"L0_attn_b_{n}" for n in ("W_in", "conv_w", "conv_b", "W_x", "W_dt", "b_dt", "A_log", "D", "W_out")]
          + [f"L0_ffn_{n}" for n in ("W_gate", "W_up", "W_down")])


def kernel(**inputs):
    import concourse.bacc as bacc
    from concourse.bass_utils import run_bass_kernel_spmd

    nc = bacc.Bacc("TRN2", target_bir_lowering=False, num_devices=1)
    arrays = {f"in_{n}": np.ascontiguousarray(inputs[n]) for n in INPUTS}
    arrays["rope_cos"], arrays["rope_sin"] = rope_tables()
    args = [nc.dram_tensor(n, a.shape, mybir.dt.from_np(a.dtype), kind="ExternalInput").ap() for n, a in arrays.items()]
    args.append(nc.dram_tensor("out", (1, S, DM), F32, kind="ExternalOutput").ap())
    layer(nc, *args)
    r = run_bass_kernel_spmd(nc, [arrays], core_ids=[0])
    return r.results[0]["out"]
```

```python
import math
from contextlib import ExitStack

import numpy as np

import concourse.bass as bass
from concourse import mybir

F32 = mybir.dt.float32
F32R = mybir.dt.float32r
BF16 = mybir.dt.bfloat16
ALU = mybir.AluOpType
ACT = mybir.ActivationFunctionType
AX_X = mybir.AxisListType.X

P = 128
S, DM = 1024, 512
NT = S // P
DC = DM // P
H, NOPE, ROPE, VD = 32, 64, 64, 128
QR, KVR = 128, 32
HG = 4
NG = H // HG
QW = ROPE + KVR
QK = QW + 1
SOFTMAX_SCALE = (NOPE + ROPE) ** -0.5 * (0.1 * math.log(128.0) + 1.0) ** 2
MASKED = -1e30
A_LOG_MAX = 80.0
FF = 1376
FT = -(-FF // P)
DI, NS, KC, RK = 1024, 16, 4, 32
DJ = DI // P
CH = 512
NCH = S // CH
TPC = CH // P


def rope_tables():
    base, factor, orig = 10000.0, 128.0, 1024

    def corr_dim(r):
        return ROPE * math.log(orig / (r * 2 * math.pi)) / (2 * math.log(base))

    low = max(math.floor(corr_dim(32.0)), 0)
    high = min(math.ceil(corr_dim(1.0)), ROPE - 1)
    hi = high + 0.001 if low == high else float(high)
    ramp = np.clip((np.arange(ROPE // 2, dtype=np.float32) - low) / (hi - low), 0.0, 1.0)
    mask = 1.0 - ramp
    extra = 1.0 / base ** (np.arange(0, ROPE, 2, dtype=np.float32) / ROPE)
    inter = extra / factor
    freqs = np.outer(np.arange(S, dtype=np.float32), inter * (1.0 - mask) + extra * mask)
    cos, sin = np.cos(freqs).astype(np.float32), np.sin(freqs).astype(np.float32)
    return np.concatenate([cos, cos], axis=1), np.concatenate([-sin, sin], axis=1)


class Run:
    def __init__(self, handle, base):
        self.sem, self.base = handle, base

    def __call__(self, value):
        return self.sem, self.base + value


def layer(nc, x, wq_a, q_ln, wq_b, wkv_a, kv_ln, wkv_b, wo, w_in, conv_w, conv_b, w_x, w_dt, b_dt,
          a_log, d_skip, w_out, w_gate, w_up, w_down, rope_cos, rope_sin, out):
    top = ExitStack()

    def sb_in(stack, name, shape, dt=F32):
        return stack.enter_context(nc.sbuf_tensor(name, shape, dt))

    def sem(name):
        return top.enter_context(nc.semaphore(name))

    with top:
        bank = [top.enter_context(nc.psum_tensor(f"bank{i}", [P, 512], F32)) for i in range(8)]
        X = sb_in(top, "X", [P, NT, DM])
        scan_space = ExitStack()
        dA, Hs, DT, DTU = ([sb_in(scan_space, f"{n}{i}", [P, CH]) for i in range(ring)]
                           for n, ring in (("dA", 3), ("Hs", 7), ("DT", 2), ("DTU", 2)))
        ssT = sb_in(scan_space, "ssT", [2 * (RK + 2 * NS), S])
        scan_space.close()
        XnT = [sb_in(top, f"XnT{i}", [P, DC, S], F32R) for i in "hl"]
        Xn = [sb_in(top, f"Xn{i}", [P, DM]) for i in range(2)]
        ident = sb_in(top, "ident", [P, P])
        identb = sb_in(top, "identb", [P, P], BF16)
        identr = sb_in(top, "identr", [P, P], F32R)
        ones = sb_in(top, "ones", [P, KVR])
        neghalf = sb_in(top, "neghalf", [P, 16])
        stats = sb_in(top, "stats", [P, NT, 6])
        meanvar = sb_in(top, "meanvar", [P, NT, 2])
        veps = sb_in(top, "veps", [P, 16])
        rstd = sb_in(top, "rstd", [P, 16])

        runs = {}

        def again(name, total):
            if name not in runs:
                runs[name] = [sem(name), 0]
            handle, base = runs[name]
            runs[name][1] += total
            return Run(handle, base)

        consts = sem("consts")
        stored = sem("stored")
        const_step = sem("const_step")

        class Norm:

            def __init__(self):
                self.high, self.low = XnT
                (self.stats_done, self.aggr_done, self.eps_done, self.rstd_done, self.xn_done, self.psum_full,
                 self.high_done, self.low_done) = (again(f"norm_{n}", NT) for n in
                                                   ("stats", "aggr", "eps", "rstd", "xn", "psum", "high", "low"))

            def tile(self, t):
                return t, bank[t % 2][:].rearrange("p (c n) -> p c n", c=DC), slice(t * P, (t + 1) * P)

            def vector_stats(self, dve, t):
                i, _, _ = self.tile(t)
                dve.bn_stats(stats[:, t, :], X[:, t, :]).then_inc(self.stats_done.sem, 1)
                dve.wait_ge(*self.stats_done(i + 1))
                dve.bn_aggr(meanvar[:, t, :], stats[:, t, :]).then_inc(self.aggr_done.sem, 1)

            def pool_rstd(self, pool, t):
                i, _, _ = self.tile(t)
                pool.wait_ge(*self.aggr_done(i + 1))
                pool.tensor_scalar(veps[:, t:t + 1], meanvar[:, t, 1:2], 1e-5, None, ALU.add).then_inc(self.eps_done.sem, 1)
                pool.wait_ge(*self.eps_done(i + 1))
                pool.tensor_tensor(rstd[:, t:t + 1], veps[:, t:t + 1], neghalf[:, 0:1], ALU.pow).then_inc(self.rstd_done.sem, 1)

            def vector_normalize(self, dve, t):
                i, _, _ = self.tile(t)
                dve.wait_ge(*self.rstd_done(i + 1))
                if i >= 2:
                    dve.wait_ge(*self.psum_full(i - 1))
                dve.tensor_scalar(Xn[i % 2][:], X[:, t, :], meanvar[:, t, 0:1], rstd[:, t:t + 1],
                                  ALU.subtract, ALU.mult).then_inc(self.xn_done.sem, 1)

            def tensor_transpose(self, pe, t):
                i, _, _ = self.tile(t)
                pe.wait_ge(*self.xn_done(i + 1))
                if i >= 2:
                    pe.wait_ge(*self.low_done(i - 1))
                for c in range(DC):
                    last = pe.transpose(bank[i % 2][:, c * P:(c + 1) * P], Xn[i % 2][:, c * P:(c + 1) * P], ident[:])
                last.then_inc(self.psum_full.sem, 1)

            def scalar_high(self, act, t):
                i, b, cols = self.tile(t)
                act.wait_ge(*self.psum_full(i + 1))
                act.copy(self.high[:, :, cols], b).then_inc(self.high_done.sem, 1)

            def vector_low(self, dve, t):
                i, b, cols = self.tile(t)
                dve.wait_ge(*self.high_done(i + 1))
                dve.tensor_tensor(self.low[:, :, cols], b, self.high[:, :, cols].bitcast(F32),
                                  ALU.subtract).then_inc(self.low_done.sem, 1)

            def vector_step(self, dve, i):
                if i < NT:
                    self.vector_stats(dve, i)
                if 0 <= i - 1 < NT:
                    self.vector_normalize(dve, i - 1)
                if 0 <= i - 3 < NT:
                    self.vector_low(dve, i - 3)

        def three_products(pe, out, lhs, rhs, first, last):
            (lh, ll), (rh, rl) = lhs, rhs
            pe.matmul(out, lh, rh, start=first, stop=False)
            pe.matmul(out, lh, rl, start=False, stop=False)
            return pe.matmul(out, ll, rh, start=False, stop=last)

        att = ExitStack()
        WVO = [sb_in(att, f"WVO{i}", [P, NG, DM], F32R) for i in "hl"]
        NQW = QR + KVR + ROPE
        HQ = H // 4
        early = ExitStack()
        wqb_nat = sb_in(early, "wqb_nat", [P, H, QR])
        QA = sb_in(early, "QA", [P, NT, NQW])
        SQ = sb_in(early, "SQ", [P, NT, QR + KVR])
        early.close()
        early = ExitStack()
        woT = sb_in(early, "woT", [P, 2, HG, DM])
        wo_nat = [sb_in(early, "wo_q0", [P, DC, HQ * VD])]
        early.close()
        OT = sb_in(att, "OT", [P, NG * S])
        WQ = [sb_in(att, f"WQ{i}", [P, H * QW], F32R) for i in "hl"]
        QnT = [sb_in(att, f"QnT{i}", [P, S], F32R) for i in "hl"]
        KTM = sb_in(att, "KTM", [P, NT, QK])
        KTh = sb_in(att, "KTh", [QK, S], F32R)
        KTl = sb_in(att, "KTl", [QK, S], F32R)
        cosT = sb_in(att, "cosT", [P, NT, 2, 32])
        sinT = sb_in(att, "sinT", [P, NT, 2, 32])
        maskqk = sb_in(att, "maskqk", [P, P], BF16)
        maskkq = sb_in(att, "maskkq", [P, P], BF16)

        prep = ExitStack()
        na = Norm()
        wa_nat = sb_in(prep, "wa_nat", [P, DM])
        wkva_nat = sb_in(prep, "wkva_nat", [KVR + ROPE, DM])
        WaT = [sb_in(prep, f"WaT{i}", [P, DC, NQW], F32R) for i in "hl"]
        wk_nat = sb_in(prep, "wk_nat", [NOPE, H, KVR])
        qlnw = sb_in(prep, "qlnw", [P, QR])
        kvlnw = sb_in(prep, "kvlnw", [P, KVR])
        QAn = sb_in(prep, "QAn", [P, NT, QR])
        RAk = sb_in(prep, "RAk", [P, NT, 2, 32])
        RBk = sb_in(prep, "RBk", [P, NT, 2, 32])
        rs = sb_in(prep, "rs", [P, 2 * NT])
        ms = sb_in(prep, "ms", [P, 2 * NT])
        prep.close()
        ld_x, ld_a, ld_q, ld_kv, ld_small = sem("ld_x"), sem("ld_a"), sem("ld_q"), sem("ld_kv"), sem("ld_small")
        masks0, masks = sem("masks0"), sem("masks")
        wa_psum, wa_high, wa_low = sem("wa_psum"), sem("wa_high"), sem("wa_low")
        proj_psum, proj_out = sem("proj_psum"), sem("proj_out")
        wq_psum, wq_high, wq_low = sem("wq_psum"), sem("wq_high"), sem("wq_low")
        qn_psum, qn_high, qn_low = sem("qn_psum"), sem("qn_high"), sem("qn_low")
        kt_psum, kt_high, kt_low = sem("kt_psum"), sem("kt_high"), sem("kt_low")
        sq_done, ms_done, rs_step, rs_done = sem("sq_done"), sem("ms_done"), sem("rs_step"), sem("rs_done")
        kstep, qn_done, ktm_done = sem("kstep"), sem("qn_done"), sem("ktm_done")

        with nc.Block() as block:
            @block.sync
            def _(sp):
                rows = x[0].rearrange("(t p) d -> p t d", p=P)
                for i in range(4):
                    sp.dma_start(X[:, 2 * i:2 * i + 2, :], rows[:, 2 * i:2 * i + 2, :]).then_inc(ld_x, 16)
                    if i == 0:
                        sp.dma_start(wa_nat[:], wq_a).then_inc(ld_a, 16)
                        sp.dma_start(wkva_nat[:], wkv_a).then_inc(ld_a, 16)
                kvb = wkv_b.rearrange("(h m) r -> m h r", m=NOPE + VD)
                sp.dma_start(wqb_nat[:], wq_b.rearrange("(h m) r -> m h r", m=P)).then_inc(ld_q, 16)
                sp.dma_start(wk_nat[:], kvb[0:NOPE]).then_inc(ld_kv, 16)
                sp.dma_start(cosT[:], rope_cos.rearrange("(t p) (a i) -> p t a i", p=P, a=2)).then_inc(ld_small, 16)
                sp.dma_start(sinT[:], rope_sin.rearrange("(t p) (a i) -> p t a i", p=P, a=2)).then_inc(ld_small, 16)
                sp.dma_start(qlnw[:], q_ln.rearrange("(a r) -> a r", a=1).to_broadcast([P, QR])).then_inc(ld_small, 16)
                sp.dma_start(kvlnw[:], kv_ln.rearrange("(a r) -> a r", a=1).to_broadcast([P, KVR])).then_inc(ld_small, 16)

            @block.gpsimd
            def _(pool):
                pool.memset(neghalf[:], -0.5).then_inc(const_step, 1)
                pool.memset(ident[:], 0.0).then_inc(const_step, 1)
                pool.memset(ones[:], 1.0).then_inc(consts, 1)
                pool.wait_ge(const_step, 2)
                pool.affine_select(out=ident[:], in_=ident[:], compare_op=ALU.not_equal, fill=1.0, base=0,
                                   pattern=[[-1, P]], channel_multiplier=1).then_inc(consts, 1)
                pool.wait_ge(consts, 2)
                pool.tensor_copy(identb[:], ident[:]).then_inc(consts, 1)
                pool.tensor_copy(identr[:], ident[:]).then_inc(consts, 1)
                for t in range(NT):
                    na.pool_rstd(pool, t)
                pool.memset(maskqk[:], 0.0).then_inc(masks0, 1)
                pool.memset(maskkq[:], 0.0).then_inc(masks0, 1)
                pool.wait_ge(masks0, 2)
                pool.affine_select(out=maskqk[:], in_=maskqk[:], compare_op=ALU.is_ge, fill=MASKED, base=0,
                                   pattern=[[-1, P]], channel_multiplier=1).then_inc(masks, 1)
                pool.affine_select(out=maskkq[:], in_=maskkq[:], compare_op=ALU.is_ge, fill=MASKED, base=0,
                                   pattern=[[1, P]], channel_multiplier=-1).then_inc(masks, 1)
                pool.memset(KTM[:, :, QW:QK], 1.0).then_inc(ktm_done, 1)
                pool.wait_ge(ms_done, 2)
                pool.tensor_scalar(veps[:, 0:NT], ms[:, 0:NT], 1.0 / QR, 1e-6, ALU.mult, ALU.add).then_inc(rs_step, 1)
                pool.tensor_scalar(veps[:, NT:], ms[:, NT:], 1.0 / KVR, 1e-6, ALU.mult, ALU.add).then_inc(rs_step, 1)
                pool.wait_ge(rs_step, 2)
                pool.tensor_tensor(rs[:], veps[:], neghalf[:], ALU.pow).then_inc(rs_done, 1)

            @block.tensor
            def _(pe):
                pe.wait_ge(consts, 4)
                pe.wait_ge(ld_a, 32)
                for c in range(DC):
                    if c >= 2:
                        pe.wait_ge(wa_low, c - 1)
                    pe.transpose(bank[2 + c % 2][:, 0:QR], wa_nat[:, c * P:(c + 1) * P], ident[:])
                    pe.transpose(bank[2 + c % 2][:, QR:NQW], wkva_nat[:, c * P:(c + 1) * P],
                                 ident[0:KVR + ROPE, 0:KVR + ROPE]).then_inc(wa_psum, 1)

                def project(t):
                    pe.wait_ge(*na.low_done(t + 1))
                    if t == 0:
                        pe.wait_ge(wa_low, DC)
                    if t >= 2:
                        pe.wait_ge(proj_out, t - 1)
                    tk = slice(t * P, (t + 1) * P)
                    for c in range(DC):
                        last = three_products(pe, bank[4 + t % 2][:, 0:NQW], (na.high[:, c, tk], na.low[:, c, tk]),
                                              (WaT[0][:, c, :], WaT[1][:, c, :]), c == 0, c == DC - 1)
                    last.then_inc(proj_psum, 1)

                for t in range(NT):
                    na.tensor_transpose(pe, t)
                    if t >= 2:
                        project(t - 2)
                project(NT - 2)
                project(NT - 1)
                pe.wait_ge(ld_q, 16)
                pe.wait_ge(ld_kv, 16)
                for g in range(NG):
                    if g >= 2:
                        pe.wait_ge(wq_low, g - 1)
                    for j in range(HG):
                        h = HG * g + j
                        pe.transpose(bank[2 + g % 2][:, j * ROPE:(j + 1) * ROPE], wqb_nat[NOPE:P, h, :], ident[NOPE:P, NOPE:P])
                        last = pe.matmul(bank[6 + g % 2][:, j * KVR:(j + 1) * KVR], wqb_nat[0:NOPE, h, :],
                                         wk_nat[:, h, :], start=True, stop=True)
                    last.then_inc(wq_psum, 1)
                pe.wait_ge(qn_done, 1)
                pe.wait_ge(*na.low_done(NT))
                for i in range(2):
                    for k in range(4):
                        last = pe.transpose(bank[i][:, k * P:(k + 1) * P], QAn[:, 4 * i + k, :], ident[:])
                    last.then_inc(qn_psum, 1)
                pe.wait_ge(ktm_done, 3)
                pe.wait_ge(proj_out, NT)
                for i in range(2):
                    for k in range(4):
                        last = pe.transpose(bank[4 + i][0:QK, k * P:(k + 1) * P], KTM[:, 4 * i + k, :], ident[:])
                    last.then_inc(kt_psum, 1)

            @block.scalar
            def _(act):
                for c in range(DC):
                    act.wait_ge(wa_psum, c + 1)
                    act.copy(WaT[0][:, c, :], bank[2 + c % 2][:, 0:NQW]).then_inc(wa_high, 1)
                for t in range(NT):
                    na.scalar_high(act, t)
                for g in range(NG):
                    act.wait_ge(wq_psum, g + 1)
                    dst = WQ[0][:, g * HG * QW:(g + 1) * HG * QW].rearrange("p (j w) -> p j w", j=HG)
                    src = bank[2 + g % 2][:, 0:HG * ROPE].rearrange("p (j w) -> p j w", j=HG)
                    for a in range(2):
                        act.copy(dst[:, :, 32 * a:32 * a + 32], src[:, :, a:ROPE:2])
                    act.copy(dst[:, :, ROPE:QW],
                             bank[6 + g % 2][:, 0:HG * KVR].rearrange("p (j w) -> p j w", j=HG)).then_inc(wq_high, 1)
                for i in range(2):
                    act.wait_ge(qn_psum, i + 1)
                    act.copy(QnT[0][:, i * 512:(i + 1) * 512], bank[i][:]).then_inc(qn_high, 1)
                for i in range(2):
                    act.wait_ge(kt_psum, i + 1)
                    act.copy(KTh[:, i * 512:(i + 1) * 512], bank[4 + i][0:QK, :]).then_inc(kt_high, 1)

            @block.vector
            def _(dve):
                for c in range(DC):
                    dve.wait_ge(wa_high, c + 1)
                    dve.tensor_tensor(WaT[1][:, c, :], bank[2 + c % 2][:, 0:NQW], WaT[0][:, c, :].bitcast(F32),
                                      ALU.subtract).then_inc(wa_low, 1)
                for t in range(NT + 4):
                    if t < NT:
                        dve.wait_ge(ld_x, 16 * NT // 2)
                        na.vector_stats(dve, t)
                    if 1 <= t <= NT:
                        na.vector_normalize(dve, t - 1)
                    if 2 <= t <= NT + 1:
                        na.vector_low(dve, t - 2)
                    if t >= 4:
                        dve.wait_ge(proj_psum, t - 3)
                        dve.tensor_copy(QA[:, t - 4, :], bank[4 + t % 2][:, 0:NQW]).then_inc(proj_out, 1)
                dve.wait_ge(proj_out, NT)
                dve.tensor_tensor(SQ[:], QA[:, :, 0:QR + KVR], QA[:, :, 0:QR + KVR], ALU.mult).then_inc(sq_done, 1)
                dve.wait_ge(sq_done, 1)
                dve.tensor_reduce(ms[:, 0:NT], SQ[:, :, 0:QR], AX_X, ALU.add).then_inc(ms_done, 1)
                dve.tensor_reduce(ms[:, NT:], SQ[:, :, QR:], AX_X, ALU.add).then_inc(ms_done, 1)
                dve.wait_ge(ld_small, 64)
                pairs = QA[:, :, QR + KVR:].rearrange("p t (i a) -> p t a i", a=2)
                for a in range(2):
                    dve.tensor_tensor(RAk[:, :, a, :], pairs[:, :, a, :], cosT[:, :, a, :], ALU.mult)
                    last = dve.tensor_tensor(RBk[:, :, a, :], pairs[:, :, 1 - a, :], sinT[:, :, a, :], ALU.mult)
                last.then_inc(kstep, 1)
                dve.wait_ge(kstep, 1)
                dve.tensor_tensor(KTM[:, :, 0:ROPE], RAk[:].rearrange("p t a i -> p t (a i)"),
                                  RBk[:].rearrange("p t a i -> p t (a i)"), ALU.add).then_inc(ktm_done, 1)
                dve.wait_ge(rs_done, 1)
                dve.tensor_tensor(SQ[:, :, 0:QR], QA[:, :, 0:QR], rs[:, 0:NT].unsqueeze(2).to_broadcast([P, NT, QR]),
                                  ALU.mult).then_inc(kstep, 1)
                dve.tensor_tensor(SQ[:, :, QR:], QA[:, :, QR:QR + KVR],
                                  rs[:, NT:].unsqueeze(2).to_broadcast([P, NT, KVR]), ALU.mult).then_inc(kstep, 1)
                dve.wait_ge(kstep, 3)
                dve.tensor_tensor(QAn[:], SQ[:, :, 0:QR], qlnw[:].unsqueeze(1).to_broadcast([P, NT, QR]),
                                  ALU.mult).then_inc(qn_done, 1)
                dve.tensor_tensor(KTM[:, :, ROPE:QW], SQ[:, :, QR:], kvlnw[:].unsqueeze(1).to_broadcast([P, NT, KVR]),
                                  ALU.mult).then_inc(ktm_done, 1)
                for g in range(NG):
                    dve.wait_ge(wq_high, g + 1)
                    dst, high = (w[:, g * HG * QW:(g + 1) * HG * QW].rearrange("p (j w) -> p j w", j=HG) for w in WQ[::-1])
                    src = bank[2 + g % 2][:, 0:HG * ROPE].rearrange("p (j w) -> p j w", j=HG)
                    for a in range(2):
                        cols = slice(32 * a, 32 * a + 32)
                        dve.tensor_tensor(dst[:, :, cols], src[:, :, a:ROPE:2], high[:, :, cols].bitcast(F32), ALU.subtract)
                    dve.tensor_tensor(dst[:, :, ROPE:QW], bank[6 + g % 2][:, 0:HG * KVR].rearrange("p (j w) -> p j w", j=HG),
                                      high[:, :, ROPE:QW].bitcast(F32), ALU.subtract).then_inc(wq_low, 1)
                for i in range(2):
                    cols = slice(i * 512, (i + 1) * 512)
                    dve.wait_ge(qn_high, i + 1)
                    dve.tensor_tensor(QnT[1][:, cols], bank[i][:], QnT[0][:, cols].bitcast(F32), ALU.subtract).then_inc(qn_low, 1)
                for i in range(2):
                    cols = slice(i * 512, (i + 1) * 512)
                    dve.wait_ge(kt_high, i + 1)
                    dve.tensor_tensor(KTl[:, cols], bank[4 + i][0:QK, :], KTh[:, cols].bitcast(F32),
                                      ALU.subtract).then_inc(kt_low, 1)

        ld_wo = [sem(f"ld_wo{i}") for i in range(4)]
        wot_psum, wot_done = sem("wot_psum"), sem("wot_done")
        wvo_psum, wvo_high, wvo_low = sem("wvo_psum"), sem("wvo_high"), sem("wvo_low")
        wv = ExitStack()
        wv_nat = sb_in(wv, "wv_nat", [P, H, KVR])
        wo_nat.append(sb_in(wv, "wo_q1", [P, DC, HQ * VD]))
        wv.close()
        with nc.Block() as block:
            @block.sync
            def _(sp):
                sp.dma_start(wv_nat[:], wkv_b.rearrange("(h m) r -> m h r", m=NOPE + VD)[NOPE:NOPE + VD]).then_inc(ld_kv, 16)
                rows = wo.rearrange("(c p) k -> p c k", p=P)
                for q in range(4):
                    if q >= 2:
                        sp.wait_ge(wot_psum, HQ * (q - 1))
                    sp.dma_start(wo_nat[q % 2][:], rows[:, :, q * HQ * VD:(q + 1) * HQ * VD]).then_inc(ld_wo[q], 16)

            @block.tensor
            def _(pe):
                pe.wait_ge(ld_kv, 32)
                for g in range(NG):
                    pe.wait_ge(ld_wo[g // 2], 16)
                    for j in range(HG):
                        h = HG * g + j
                        if h >= 4:
                            pe.wait_ge(wot_done, h - 3)
                        for c in range(DC):
                            last = pe.transpose(bank[h % 4][:, c * P:(c + 1) * P],
                                                wo_nat[g // 2 % 2][:, c, (h % HQ) * VD:(h % HQ + 1) * VD], ident[:])
                        last.then_inc(wot_psum, 1)
                    pe.wait_ge(wot_done, HG * (g + 1))
                    if g >= 2:
                        pe.wait_ge(wvo_low, g - 1)
                    for j in range(HG):
                        last = pe.matmul(bank[6 + g % 2][32 * j:32 * j + 32, :], wv_nat[:, HG * g + j, :],
                                         woT[:, g % 2, j, :], start=True, stop=True)
                    last.then_inc(wvo_psum, 1)

            @block.scalar
            def _(act):
                for g in range(NG):
                    for h in (HG * g + 1, HG * g + 3):
                        act.wait_ge(wot_psum, h + 1)
                        act.wait_ge(wot_done, h)
                        if g >= 2:
                            act.wait_ge(wvo_psum, g - 1)
                        act.copy(woT[:, g % 2, h % HG, :], bank[h % 4][:]).then_inc(wot_done, 1)
                    act.wait_ge(wvo_psum, g + 1)
                    act.copy(WVO[0][:, g, :], bank[6 + g % 2][:]).then_inc(wvo_high, 1)

            @block.vector
            def _(dve):
                for g in range(NG):
                    for h in (HG * g, HG * g + 2):
                        dve.wait_ge(wot_psum, h + 1)
                        if h:
                            dve.wait_ge(wot_done, h)
                        if g >= 2:
                            dve.wait_ge(wvo_psum, g - 1)
                        dve.tensor_copy(woT[:, g % 2, h % HG, :], bank[h % 4][:]).then_inc(wot_done, 1)
                    dve.wait_ge(wvo_high, g + 1)
                    dve.tensor_tensor(WVO[1][:, g, :], bank[6 + g % 2][:], WVO[0][:, g, :].bitcast(F32),
                                      ALU.subtract).then_inc(wvo_low, 1)

        core = ExitStack()
        QT = [(sb_in(core, f"QTh{i}", [QK, HG * P], F32R), sb_in(core, f"QTl{i}", [QK, HG * P], F32R)) for i in range(4)]
        Qtm = [sb_in(core, f"Qtm{i}", [P, HG, QW]) for i in range(2)]
        RA = [sb_in(core, f"RA{i}", [P, HG, 2, 32]) for i in range(2)]
        RB = [sb_in(core, f"RB{i}", [P, HG, 2, 32]) for i in range(2)]
        mx = [sb_in(core, f"mx{i}", [P, HG, 2]) for i in range(2)]
        negm = [sb_in(core, f"negm{i}", [P, HG], BF16) for i in range(2)]
        NPT = 6
        PT = [sb_in(core, f"PT{i}", [P, HG * P]) for i in range(NPT)]
        PS = [sb_in(core, f"PS{i}", [P, HG * P]) for i in range(2)]
        rD = [sb_in(core, f"rD{i}", [P, P]) for i in range(2)]
        core.close()
        att.close()

        q_psum, ra_done, rope_done = sem("q_psum"), sem("ra_done"), sem("rope_done")
        t_psum, qh_done, ql_done = sem("t_psum"), sem("qh_done"), sem("ql_done")
        p1_psum, p1_read, m_done, mrow_psum, mrow_done = (sem("p1_psum"), sem("p1_read"), sem("m_done"),
                                                          sem("mrow_psum"), sem("mrow_done"))
        s_psum, p_done, pv_done, sum_done = sem("s_psum"), sem("p_done"), sem("pv_done"), sem("sum_done")
        den_psum, rd_done, o_done, qlzero = sem("den_psum"), sem("rd_done"), sem("o_done"), sem("qlzero")
        RING, TB, ST, OD = (0, 1), 2, (3, 4, 5), (6, 7)

        ORDER = [7, 0, 6, 1, 5, 2, 4, 3]
        UNITS, PAIR = NG * NT, NT + 1
        STEPS = NT * (NT + 1) // 2
        first_step = [sum(ORDER[i] + 1 for i in range(n)) for n in range(NT)]

        def tile_of(n):
            return ORDER[n % NT]

        def unit_of(x):
            i = max(i for i in range(NT) if first_step[i] <= x % STEPS)
            return x // STEPS * NT + i, x % STEPS - first_step[i]

        def step_of(n, k):
            return n // NT * STEPS + first_step[n % NT] + k

        def sums_through(x):
            n, _ = unit_of(x)
            return x + 1 - (n + 1)

        def max_chunks(n):
            keys = (tile_of(n) + 1) * P
            if keys <= 256:
                return [((0, 1), 0, keys), ((2, 3), 0, keys)]
            return [((j,), a, min(keys, a + 512) - a) for j in range(HG) for a in range(0, keys, 512)]

        CHUNKS = sum(len(max_chunks(i)) for i in range(NT))

        def chunk_of(n, c):
            return n // NT * CHUNKS + sum(len(max_chunks(i)) for i in range(n % NT)) + c

        def side_work(x):
            w, cur = x % PAIR, x // PAIR * 2
            a1, b1, a2 = cur + 2, cur + 3, cur + 4
            nb = len(max_chunks(b1))
            todo = {0: [("project", b1, 0)], 1: [("transpose", a1, 0), ("maxrow", cur + 1, 0)],
                    5: [("chunk", a1, 6), ("chunk", a1, 7), ("transpose", b1, 0)],
                    6: [("maxrow", a1, 0)] + [("chunk", b1, c) for c in range(nb // 2)],
                    7: [("chunk", b1, c) for c in range(nb // 2, nb)], 8: [("project", a2, 0)]}.get(w, [])
            if 2 <= w <= 4:
                todo = [("chunk", a1, 2 * w - 4), ("chunk", a1, 2 * w - 3)]
            for late in (1, 2):
                if x >= late:
                    n, k = unit_of(x - late)
                    if k == tile_of(n) and late == (1 if ORDER[(n + 1) % NT] == 0 else 2):
                        todo = [("denominator", n, 0)] + todo
            return [e for e in todo if e[1] < UNITS]

        PROLOGUE = ([("project", 0, 0), ("project", 1, 0), ("transpose", 0, 0)] + [("chunk", 0, c) for c in range(8)]
                    + [("transpose", 1, 0)] + [("chunk", 1, c) for c in range(2)] + [("maxrow", 0, 0), ("project", 2, 0)])

        ring = [e for e in PROLOGUE if e[0] in ("project", "chunk")]
        for x in range(UNITS // NT * STEPS):
            ring += [e for e in side_work(x) if e[0] in ("project", "chunk")]
        place = {e: i for i, e in enumerate(ring)}

        def groups(eng, prologue, step, epilogue=None):
            prologue()
            for x in range(STEPS):
                step(x, lambda v, per: v)
            with eng.Fori(1, NG - 1) as g:
                for x in range(STEPS, 2 * STEPS):
                    step(x, lambda v, per: g * per + (v - per))
            for x in range((NG - 1) * STEPS, NG * STEPS):
                step(x, lambda v, per: v)
            if epilogue is not None:
                epilogue()

        with nc.Block() as block:
            @block.tensor
            def _(pe):
                def ring_bank(e, at):
                    i = place[e]
                    if i >= 2:
                        kind, n, c = ring[i - 2]
                        if kind == "project":
                            pe.wait_ge(ra_done, at(n + 1, NT))
                        else:
                            pe.wait_ge(p1_read, at(chunk_of(n, c) + 1, CHUNKS))
                    return bank[RING[i % 2]]

                def project(n, at):
                    t = tile_of(n)
                    b = ring_bank(("project", n, 0), at)
                    cols = bass.ds(at(n // NT, 1) * (HG * QW), HG * QW)
                    tk = slice(t * P, (t + 1) * P)
                    three_products(pe, b[:, 0:HG * QW], (QnT[0][:, tk], QnT[1][:, tk]), (WQ[0][:, cols], WQ[1][:, cols]),
                                   True, True).then_inc(q_psum, 1)

                def transpose(n, at):
                    pe.wait_ge(rope_done, at(n + 1, NT))
                    if n >= 1:
                        pe.wait_ge(ql_done, at(n, NT))
                    for j in range(HG):
                        last = pe.transpose(bank[TB][0:QW, j * P:(j + 1) * P], Qtm[n % 2][:, j, :], ident[:])
                    last.then_inc(t_psum, 1)

                def chunk(n, c, at):
                    qh = QT[n % 4][0]
                    heads, a, m = max_chunks(n)[c]
                    b = ring_bank(("chunk", n, c), at)
                    pe.wait_ge(qh_done, at(n + 1, NT))
                    diag = a + m == (tile_of(n) + 1) * P
                    for i, j in enumerate(heads):
                        last = pe.matmul(b[:, i * m:(i + 1) * m], qh[0:QW, j * P:(j + 1) * P], KTh[0:QW, a:a + m],
                                         start=(i == 0), stop=not diag, skip_group_check=True)
                    if diag:
                        for i in range(len(heads)):
                            last = pe.matmul(b[:, (i + 1) * m - P:(i + 1) * m], identb[:], maskqk[:],
                                             start=False, stop=True, skip_group_check=True)
                    last.then_inc(p1_psum, 1)

                def max_row(n, at):
                    pe.wait_ge(m_done, at(n + 1, NT))
                    if n >= 1:
                        pe.wait_ge(mrow_done, at(n, NT))
                    for j in range(HG):
                        last = pe.matmul(bank[TB][QW:QK, j * P:(j + 1) * P], negm[n % 2][:, j:j + 1], identb[:],
                                         start=True, stop=True)
                    last.then_inc(mrow_psum, 1)

                def scores(x, at):
                    n, k = unit_of(x)
                    b = bank[ST[x % 3]]
                    if x >= 3:
                        pe.wait_ge(p_done, at(x - 2, STEPS))
                    if k == 0:
                        pe.wait_ge(mrow_done, at(n + 1, NT))
                        pe.wait_ge(ql_done, at(n + 1, NT))
                    qh, ql = QT[n % 4]
                    kt = slice(k * P, (k + 1) * P)
                    diag = k == tile_of(n)
                    pe.matmul(b[:], KTh[:, kt], qh[:], start=True, stop=False)
                    pe.matmul(b[:], KTh[:, kt], ql[:], start=False, stop=False)
                    last = pe.matmul(b[:], KTl[:, kt], qh[:], start=False, stop=not diag)
                    if diag:
                        last = pe.matmul(b[:].rearrange("p (j n) -> p j n", j=HG), identb[:],
                                         maskkq[:].unsqueeze(1).to_broadcast([P, HG, P]), start=False, stop=True)
                    last.then_inc(s_psum, 1)

                def values(x, at):
                    n, k = unit_of(x)
                    pe.wait_ge(p_done, at(x + 1, STEPS))
                    if k == 0 and n >= 2:
                        pe.wait_ge(o_done, at(n - 1, NT))
                    for j in range(HG):
                        last = pe.matmul(bank[OD[n % 2]][32 * j:32 * j + 32, 0:P], KTM[:, k, ROPE:QW],
                                         PT[x % NPT][:, j * P:(j + 1) * P], start=(k == 0), stop=(k == tile_of(n)),
                                         skip_group_check=True)
                    last.then_inc(pv_done, 1)

                def denominator(n, at):
                    t = tile_of(n)
                    last_step = step_of(n, t)
                    if t:
                        pe.wait_ge(sum_done, at(sums_through(last_step), STEPS - NT))
                    src = PS[n % 2] if t else PT[last_step % NPT]
                    for j in range(HG):
                        last = pe.matmul(bank[OD[n % 2]][32 * j:32 * j + 32, P:2 * P], ones[:], src[:, j * P:(j + 1) * P],
                                         start=False, stop=True, skip_group_check=True)
                    last.then_inc(den_psum, 1)

                def side(kind, n, c, at):
                    if kind == "project":
                        project(n, at)
                    elif kind == "transpose":
                        transpose(n, at)
                    elif kind == "chunk":
                        chunk(n, c, at)
                    elif kind == "maxrow":
                        max_row(n, at)
                    else:
                        denominator(n, at)

                def prologue():
                    pe.wait_ge(qlzero, 4)
                    for e in PROLOGUE:
                        side(*e, lambda v, per: v)
                    for x in range(2):
                        scores(x, lambda v, per: v)

                def step(x, at):
                    if x + 2 < NG * STEPS:
                        scores(x + 2, at)
                    for e in side_work(x):
                        side(*e, at)
                    values(x, at)

                groups(pe, prologue, step, lambda: denominator(UNITS - 1, lambda v, per: v))

            @block.vector
            def _(dve):
                def rope(n, at):
                    t = tile_of(n)
                    q = bank[RING[place[("project", n, 0)] % 2]][:, 0:HG * QW].rearrange("p (j w) -> p j w", j=HG)
                    rot = q[:, :, 0:ROPE].rearrange("p j (a i) -> p j a i", a=2)
                    dve.wait_ge(q_psum, at(n + 1, NT))
                    if n >= 2:
                        dve.wait_ge(rope_done, at(n - 1, NT))
                        dve.wait_ge(t_psum, at(n - 1, NT))
                    dve.tensor_copy(Qtm[n % 2][:, :, ROPE:QW], q[:, :, ROPE:QW])
                    dve.tensor_tensor(RA[n % 2][:], rot, cosT[:, t].unsqueeze(1).to_broadcast([P, HG, 2, 32]), ALU.mult)
                    dve.tensor_tensor(RB[n % 2][:], rot[:, :, ::-1, :],
                                      sinT[:, t].unsqueeze(1).to_broadcast([P, HG, 2, 32]), ALU.mult).then_inc(ra_done, 1)

                def low_part(n, at):
                    qh, ql = QT[n % 4]
                    dve.wait_ge(qh_done, at(n + 1, NT))
                    dve.tensor_tensor(ql[0:QW, :], bank[TB][0:QW, :], qh[0:QW, :].bitcast(F32),
                                      ALU.subtract).then_inc(ql_done, 1)

                def maxima(n, c, at):
                    m, chunks = mx[n % 2], max_chunks(n)
                    heads, a, w = chunks[c]
                    dve.wait_ge(p1_psum, at(chunk_of(n, c) + 1, CHUNKS))
                    dve.tensor_reduce(m[:, heads[0]:heads[-1] + 1, a // 512:a // 512 + 1],
                                      bank[RING[place[("chunk", n, c)] % 2]][:, 0:len(heads) * w].rearrange(
                                          "p (s n) -> p s n", n=w), AX_X, ALU.max).then_inc(p1_read, 1)
                    if c == len(chunks) - 1:
                        dve.wait_ge(p1_read, at(chunk_of(n, c) + 1, CHUNKS))
                        if n >= 2:
                            dve.wait_ge(mrow_psum, at(n - 1, NT))
                        dve.tensor_reduce(negm[n % 2][:], m[:, :, 0:a // 512 + 1], AX_X, ALU.max,
                                          negate=True).then_inc(m_done, 1)

                def normalize(n, at):
                    od, t = bank[OD[n % 2]], tile_of(n)
                    dve.wait_ge(den_psum, at(n + 1, NT))
                    dve.reciprocal(rD[n % 2][:], od[:, P:2 * P]).then_inc(rd_done, 1)
                    dve.wait_ge(rd_done, at(n + 1, NT))
                    dve.tensor_tensor(OT[:, bass.ds(at(n // NT, 1) * S + t * P, P)], od[:, 0:P], rD[n % 2][:],
                                      ALU.mult).then_inc(o_done, 1)

                def side(kind, n, c, at):
                    if kind == "project":
                        rope(n, at)
                    elif kind == "transpose":
                        low_part(n, at)
                    elif kind == "chunk":
                        maxima(n, c, at)
                    elif kind == "denominator":
                        normalize(n, at)

                def prologue():
                    for i in range(4):
                        dve.memset(QT[i][1][:].bitcast(F32), 0.0).then_inc(qlzero, 1)
                    dve.wait_ge(qlzero, 4)
                    for e in PROLOGUE:
                        side(*e, lambda v, per: v)

                def step(x, at):
                    for e in side_work(x):
                        side(*e, at)

                groups(dve, prologue, step, lambda: normalize(UNITS - 1, lambda v, per: v))

            @block.gpsimd
            def _(pool):
                def rope_sum(n, at):
                    pool.wait_ge(ra_done, at(n + 1, NT))
                    pool.tensor_tensor(Qtm[n % 2][:, :, 0:ROPE], RA[n % 2][:].rearrange("p j a i -> p j (a i)"),
                                       RB[n % 2][:].rearrange("p j a i -> p j (a i)"), ALU.add).then_inc(rope_done, 1)

                def prologue():
                    for kind, n, _ in PROLOGUE:
                        if kind == "project":
                            rope_sum(n, lambda v, per: v)

                def add(x, at):
                    n, k = unit_of(x)
                    pool.wait_ge(p_done, at(x + 1, STEPS))
                    if k == 1 and n >= 2:
                        pool.wait_ge(den_psum, at(n - 1, NT))
                    if k >= 2:
                        pool.wait_ge(sum_done, at(sums_through(x - 1), STEPS - NT))
                    pool.tensor_tensor(PS[n % 2][:], PT[(x - 1) % NPT][:] if k == 1 else PS[n % 2][:], PT[x % NPT][:],
                                       ALU.add).then_inc(sum_done, 1)

                def step(x, at):
                    if unit_of(x)[1]:
                        add(x, at)
                    for kind, n, _ in side_work(x):
                        if kind == "project":
                            rope_sum(n, at)

                groups(pool, prologue, step)

            @block.scalar
            def _(act):
                def high_part(n, at):
                    act.wait_ge(t_psum, at(n + 1, NT))
                    act.copy(QT[n % 4][0][0:QW, :], bank[TB][0:QW, :]).then_inc(qh_done, 1)

                def copy_max_row(n, at):
                    act.wait_ge(mrow_psum, at(n + 1, NT))
                    act.copy(QT[n % 4][0][QW:QK, :], bank[TB][QW:QK, :]).then_inc(mrow_done, 1)

                def probabilities(x, at):
                    act.wait_ge(s_psum, at(x + 1, STEPS))
                    if x >= NPT:
                        n, k = unit_of(x - NPT)
                        act.wait_ge(pv_done, at(x - NPT + 1, STEPS))
                        y = x - NPT + 1 if unit_of(x - NPT + 1)[1] == 1 else x - NPT
                        act.wait_ge(sum_done, at(sums_through(y), STEPS - NT))
                        if tile_of(n) == 0:
                            act.wait_ge(den_psum, at(n + 1, NT))
                    act.activation(PT[x % NPT][:], bank[ST[x % 3]][:], ACT.Exp, scale=SOFTMAX_SCALE).then_inc(p_done, 1)

                def side(kind, n, at):
                    if kind == "transpose":
                        high_part(n, at)
                    elif kind == "maxrow":
                        copy_max_row(n, at)

                def prologue():
                    for kind, n, _ in PROLOGUE:
                        side(kind, n, lambda v, per: v)
                    for x in range(2):
                        probabilities(x, lambda v, per: v)

                def step(x, at):
                    if x + 2 < NG * STEPS:
                        probabilities(x + 2, at)
                    for kind, n, _ in side_work(x):
                        side(kind, n, at)

                groups(act, prologue, step)

        class FeedForward:
            PIECES = ((0, 2), (2, 5), (5, 8), (8, FT))

            def __init__(self, mem, tag):
                self.SG = [sb_in(mem, f"SG{i}_{tag}", [P, CH]) for i in range(2)]
                self.H = [sb_in(mem, f"H{i}_{tag}", [P, CH]) for i in range(2)]
                self.Wg, self.Wu = ([[sb_in(mem, f"{w}{s}{i}_{tag}", [P, DC, P], F32R) for i in "hl"] for s in range(2)]
                                    for w in ("WgT", "WuT"))
                self.Wd = [[sb_in(mem, f"WdT{s}{i}_{tag}", [P, DM], F32R) for i in "hl"] for s in range(5)]
                self.HT = [[sb_in(mem, f"HT{s}{i}_{tag}", [P, S], F32R) for i in "hl"] for s in range(4)]
                self.nat = [[sb_in(mem, f"nat{w}{s}_{tag}", [P, 3, DM]) for w in "gu"]
                            + [sb_in(mem, f"natd{s}_{tag}", [P, DC, 3 * P])] for s in range(2)]
                self.loads = [(3 if b < FT else 5) * 16 for _, b in self.PIECES]
                self.ld = [again(f"ffn_ld{p}", n) for p, n in enumerate(self.loads)]

            def load(self, sp, p):
                a, b = self.PIECES[p]
                full = min(b, FF // P)
                for i, w in enumerate((w_gate, w_up)):
                    dst = self.nat[p % 2][i]
                    sp.dma_start(dst[:, 0:full - a, :], w[a * P:full * P].rearrange("(f p) d -> p f d", p=P)).then_inc(self.ld[p].sem, 16)
                    if b == FT:
                        sp.dma_start(dst[0:FF - full * P, full - a, :], w[full * P:FF]).then_inc(self.ld[p].sem, 16)
                cols = slice(a * P, min(b * P, FF))
                sp.dma_start(self.nat[p % 2][2][:, :, 0:cols.stop - cols.start],
                             w_down.rearrange("(c p) f -> p c f", p=P)[:, :, cols]).then_inc(self.ld[p].sem, 16)

            def run(self, norm):
                PIECES, SG, H, Wg, Wu, Wd, HT = self.PIECES, self.SG, self.H, self.Wg, self.Wu, self.Wd, self.HT
                rows = [min(P, FF - f * P) for f in range(FT)]
                piece = [next(p for p, (a, b) in enumerate(PIECES) if f < b) for f in range(FT)]
                w_psum, w_high, w_low = (again(n, 3 * FT) for n in ("w_psum", "w_high", "w_low"))
                gate_psum, up_psum, silu_done, h_done, h_high, h_low = (
                    again(n, NCH * FT) for n in ("gate_psum", "up_psum", "silu_done", "h_done", "h_high", "h_low"))
                down_psum, down_added = (again(n, len(PIECES) * NT) for n in ("down_psum", "down_added"))

                def down_after(f):
                    return piece[f - 1] if f and piece[f - 1] != piece[f] else None

                def weight(f, m, hl):
                    r, b = rows[f], bank[(3 * f + m) % 2]
                    if m == 2:
                        return Wd[f % 5][hl][0:r, :], b[0:r, :]
                    return (Wg, Wu)[m][f % 2][hl][:, :, 0:r], b[:].rearrange("p (c n) -> p c n", c=DC)[:, :, 0:r]

                with nc.Block() as block:
                    @block.sync
                    def _(sp):
                        for p in range(2, len(PIECES)):
                            sp.wait_ge(*w_psum(3 * PIECES[p - 2][1]))
                            self.load(sp, p)
                        if norm is None:
                            rows_out = out[0].rearrange("(t p) d -> p t d", p=P)
                            for t in range(0, NT, 2):
                                sp.wait_ge(*down_added((len(PIECES) - 1) * NT + t + 2))
                                sp.dma_start(rows_out[:, t:t + 2, :], X[:, t:t + 2, :]).then_inc(stored, 16)
                            sp.wait_ge(stored, 16 * NT // 2)

                    @block.tensor
                    def _(pe):
                        def transpose(f, m):
                            if f >= FT:
                                return
                            i, r, p = 3 * f + m, rows[f], piece[f]
                            b, nat, k = bank[i % 2], self.nat[p % 2], f - PIECES[p][0]
                            if k == 0 and m == 0:
                                pe.wait_ge(*self.ld[p](self.loads[p]))
                            if i >= 2:
                                pe.wait_ge(*w_low(i - 1))
                            for c in range(DC):
                                if m < 2:
                                    last = pe.transpose(b[:, c * P:c * P + r], nat[m][0:r, k, c * P:(c + 1) * P],
                                                        ident[0:r, 0:r])
                                else:
                                    last = pe.transpose(b[0:r, c * P:(c + 1) * P], nat[2][:, c, k * P:k * P + r], ident[:])
                            last.then_inc(w_psum.sem, 1)

                        def product(f, ch, W, m, out, full):
                            r = rows[f]
                            tk = slice(ch * CH, (ch + 1) * CH)
                            for c in range(DC):
                                last = three_products(pe, out[0:r, :], [w[:, c, 0:r] for w in W[f % 2]],
                                                      [x[:, c, tk] for x in XnT], c == 0, c == DC - 1)
                            last.then_inc(full.sem, 1)

                        def down(p, t):
                            a, b = PIECES[p]
                            i = p * NT + t
                            if i >= 2:
                                pe.wait_ge(*down_added(i - 1))
                            for f in range(a, b):
                                last = three_products(pe, bank[6 + i % 2][:], [h[0:rows[f], t * P:(t + 1) * P] for h in HT[f % 4]],
                                                      [w[0:rows[f], :] for w in Wd[f % 5]], f == a, f == b - 1)
                            last.then_inc(down_psum.sem, 1)

                        for m in range(3):
                            transpose(0, m)
                        for f in range(FT):
                            for ch in range(NCH):
                                n = NCH * f + ch
                                if ch == 0:
                                    transpose(f + 1, 0)
                                    pe.wait_ge(*w_low(3 * f + 2))
                                if n >= 2:
                                    pe.wait_ge(*silu_done(n - 1))
                                product(f, ch, Wg, 0, bank[2 + n % 2], gate_psum)
                                transpose(f + 1, 1 + ch)
                                if n >= 2:
                                    pe.wait_ge(*h_done(n - 1))
                                product(f, ch, Wu, 1, bank[4 + n % 2], up_psum)
                            p = down_after(f)
                            if p is not None:
                                pe.wait_ge(*w_low(3 * PIECES[p][1]))
                                pe.wait_ge(*h_low(NCH * PIECES[p][1]))
                                for t in range(NT):
                                    down(p, t)
                        pe.wait_ge(*w_low(3 * FT))
                        for t in range(NT):
                            if t % TPC == 0:
                                pe.wait_ge(*h_low(NCH * (FT - 1) + t // TPC + 1))
                            down(len(PIECES) - 1, t)
                            if norm is not None and t >= 2:
                                norm.tensor_transpose(pe, t - 2)
                        if norm is not None:
                            norm.tensor_transpose(pe, NT - 2)
                            norm.tensor_transpose(pe, NT - 1)

                    @block.scalar
                    def _(act):
                        def high(f, m):
                            if f < FT:
                                act.wait_ge(*w_psum(3 * f + m + 1))
                                dst, src = weight(f, m, 0)
                                act.copy(dst, src).then_inc(w_high.sem, 1)

                        def silu(n):
                            r = rows[n // NCH]
                            act.wait_ge(*gate_psum(n + 1))
                            if n >= 2:
                                act.wait_ge(*h_done(n - 1))
                            act.activation(SG[n % 2][0:r, :], bank[2 + n % 2][0:r, :], ACT.Silu).then_inc(silu_done.sem, 1)

                        def hidden_high(n):
                            f, ch = divmod(n, NCH)
                            act.wait_ge(*h_done(n + 1))
                            act.copy(HT[f % 4][0][0:rows[f], ch * CH:(ch + 1) * CH], H[n % 2][0:rows[f], :]).then_inc(h_high.sem, 1)

                        for m in range(3):
                            high(0, m)
                        for f in range(FT):
                            high(f + 1, 0)
                            if f:
                                hidden_high(2 * f - 1)
                            silu(2 * f)
                            high(f + 1, 1)
                            hidden_high(2 * f)
                            silu(2 * f + 1)
                            high(f + 1, 2)
                        hidden_high(2 * FT - 1)
                        if norm is not None:
                            for t in range(NT):
                                norm.scalar_high(act, t)

                    @block.gpsimd
                    def _(pool):
                        for n in range(NCH * FT):
                            f, ch = divmod(n, NCH)
                            pool.wait_ge(*h_high(n + 1))
                            cols = slice(ch * CH, (ch + 1) * CH)
                            pool.tensor_tensor(HT[f % 4][1][0:rows[f], cols], H[n % 2][0:rows[f], :],
                                               HT[f % 4][0][0:rows[f], cols].bitcast(F32), ALU.subtract).then_inc(h_low.sem, 1)
                        if norm is not None:
                            for t in range(NT):
                                norm.pool_rstd(pool, t)

                    @block.vector
                    def _(dve):
                        def low(f, m):
                            if f < FT:
                                dve.wait_ge(*w_high(3 * f + m + 1))
                                dst, src = weight(f, m, 1)
                                dve.tensor_tensor(dst, src, weight(f, m, 0)[0].bitcast(F32), ALU.subtract).then_inc(w_low.sem, 1)

                        def hidden(n):
                            r = rows[n // NCH]
                            dve.wait_ge(*up_psum(n + 1))
                            dve.wait_ge(*silu_done(n + 1))
                            if n >= 2:
                                dve.wait_ge(*h_low(n - 1))
                            dve.tensor_tensor(H[n % 2][0:r, :], bank[4 + n % 2][0:r, :], SG[n % 2][0:r, :],
                                              ALU.mult).then_inc(h_done.sem, 1)

                        def add(p, t):
                            i = p * NT + t
                            dve.wait_ge(*down_psum(i + 1))
                            if p:
                                dve.wait_ge(*down_added(i - NT + 1))
                            dve.tensor_tensor(X[:, t, :], bank[6 + i % 2][:], X[:, t, :], ALU.add).then_inc(down_added.sem, 1)

                        for m in range(3):
                            low(0, m)
                        for f in range(FT):
                            low(f + 1, 0)
                            low(f + 1, 1)
                            hidden(2 * f)
                            low(f + 1, 2)
                            hidden(2 * f + 1)
                            p = down_after(f)
                            if p is not None:
                                for t in range(NT):
                                    add(p, t)
                        p = len(PIECES) - 1
                        for t in range(NT if norm is None else NT + 3):
                            if t < NT:
                                add(p, t)
                                if norm is not None:
                                    dve.wait_ge(*down_added(p * NT + t + 1))
                            if norm is not None:
                                norm.vector_step(dve, t)

        ot = OT[:].rearrange("p (g s) -> p g s", g=NG)
        ffn1, split = ExitStack(), ExitStack()
        f1 = FeedForward(ffn1, "f1")
        OTs = [[sb_in(split, f"OTs{i}{k}", [P, NG, P], F32R) for i in "hl"] for k in range(2)]
        split.close()
        ffn1.close()
        nf1 = Norm()
        ot_high, ot_low, attn_psum, attn_added = sem("ot_high"), sem("ot_low"), sem("attn_psum"), sem("attn_added")
        with nc.Block() as block:
            @block.sync
            def _(sp):
                f1.load(sp, 0)
                f1.load(sp, 1)

            @block.scalar
            def _(act):
                for t in range(NT + 3):
                    if t < NT:
                        if t >= 2:
                            act.wait_ge(attn_psum, t - 1)
                        act.copy(OTs[t % 2][0][:], ot[:, :, t * P:(t + 1) * P]).then_inc(ot_high, 1)
                    if t >= 3:
                        nf1.scalar_high(act, t - 3)

            @block.tensor
            def _(pe):
                for t in range(NT):
                    pe.wait_ge(ot_low, t + 1)
                    if t >= 2:
                        pe.wait_ge(attn_added, t - 1)
                    for g in range(NG):
                        last = three_products(pe, bank[2 + t % 2][:], [o[:, g, :] for o in OTs[t % 2]],
                                              [w[:, g, :] for w in WVO], g == 0, g == NG - 1)
                    last.then_inc(attn_psum, 1)
                    if t >= 2:
                        nf1.tensor_transpose(pe, t - 2)
                nf1.tensor_transpose(pe, NT - 2)
                nf1.tensor_transpose(pe, NT - 1)

            @block.gpsimd
            def _(pool):
                for t in range(NT):
                    nf1.pool_rstd(pool, t)

            @block.vector
            def _(dve):
                def low(t):
                    dve.wait_ge(ot_high, t + 1)
                    dve.tensor_tensor(OTs[t % 2][1][:], ot[:, :, t * P:(t + 1) * P], OTs[t % 2][0][:].bitcast(F32),
                                      ALU.subtract).then_inc(ot_low, 1)

                low(0)
                low(1)
                for t in range(NT + 3):
                    if t < NT:
                        dve.wait_ge(attn_psum, t + 1)
                        dve.tensor_tensor(X[:, t, :], bank[2 + t % 2][:], X[:, t, :], ALU.add).then_inc(attn_added, 1)
                        dve.wait_ge(attn_added, t + 1)
                    nf1.vector_step(dve, t)
                    if t + 2 < NT:
                        low(t + 2)

        ns = Norm()
        f1.run(ns)


        def project_onto_x(tag, lhs, rhs, n, tiles, norm=None, load=None):
            psum_full, added = again("psum_full", len(tiles)), again("added", len(tiles))
            done = NT - len(tiles)
            with nc.Block() as block:
                @block.sync
                def _(sp):
                    if load is not None:
                        load(sp)

                @block.tensor
                def _(pe):
                    ready = 0
                    for i, t in enumerate(tiles):
                        if i >= 2:
                            pe.wait_ge(*added(i - 1))
                        for k in range(n):
                            last = pe.matmul(bank[2 + i % 2][:], lhs(k, t), rhs(k), start=(k == 0), stop=(k == n - 1))
                        last.then_inc(psum_full.sem, 1)
                        if norm is not None:
                            until = min(ready + 2, done) if ready < done else done + i - 1
                            for u in range(ready, until):
                                norm.tensor_transpose(pe, u)
                            ready = max(ready, until)
                    if norm is not None:
                        for u in range(ready, NT):
                            norm.tensor_transpose(pe, u)

                @block.vector
                def _(dve):
                    if norm is not None:
                        for t in range(done):
                            norm.vector_step(dve, t)
                    for i, t in enumerate(tiles):
                        dve.wait_ge(*psum_full(i + 1))
                        dve.tensor_tensor(X[:, t, :], bank[2 + i % 2][:], X[:, t, :], ALU.add).then_inc(added.sem, 1)
                        if norm is not None:
                            dve.wait_ge(*added(i + 1))
                            norm.vector_step(dve, t)
                    if norm is not None:
                        for t in range(NT, NT + 3):
                            norm.vector_step(dve, t)

                @block.gpsimd
                def _(pool):
                    if norm is not None:
                        for t in range(NT):
                            norm.pool_rstd(pool, t)

                @block.scalar
                def _(act):
                    if norm is not None:
                        for t in range(NT):
                            norm.scalar_high(act, t)

        ssm = ExitStack()
        XS = sb_in(ssm, "XS", [P, DJ, S])
        WoutT = sb_in(ssm, "WoutT", [P, DJ, DM])
        G = sb_in(ssm, "G", [P, DJ, S])
        WxT = sb_in(ssm, "WxT", [P, DJ, RK + 2 * NS])
        WdtT = sb_in(ssm, "WdtT", [RK, DI])
        convw = sb_in(ssm, "convw", [P, DJ, KC])
        convb = sb_in(ssm, "convb", [P, DJ])
        bdt = sb_in(ssm, "bdt", [P, DJ])
        dsk = sb_in(ssm, "dsk", [P, DJ])
        Aneg = sb_in(ssm, "Aneg", [P, DJ, NS])
        state = sb_in(ssm, "state", [P, DJ, NS])
        inp = ExitStack()
        WinT = [[[sb_in(inp, f"WinT{w}{k}{i}", [P, DC, P], F32R) for i in "hl"] for k in range(2)] for w in "xg"]
        win_nat = [sb_in(inp, f"win_nat{i}", [P, 2, DM]) for i in range(3)]
        wout_nat = [sb_in(inp, f"wout_nat{i}", [P, DC, P]) for i in range(3)]
        XP = [sb_in(inp, f"XP{i}", [P, KC - 1 + S]) for i in range(2)]
        acc = [sb_in(inp, f"acc{i}", [P, S]) for i in range(2)]
        wx_nat = sb_in(inp, "wx_nat", [RK + 2 * NS, DI])
        wdt_nat = sb_in(inp, "wdt_nat", [P, DJ, RK])
        inp.close()

        ld_in = [sem(f"ld_in{i}") for i in range(DJ)]
        ld_s, ld_v = sem("ld_s"), sem("ld_v")
        in_psum, in_high, in_low, small_psum, small_done = (sem("in_psum"), sem("in_high"), sem("in_low"),
                                                            sem("small_psum"), sem("small_done"))
        xp_psum, xp_done, conv_step, conv_done, xs_done = (sem("xp_psum"), sem("xp_done"), sem("conv_step"),
                                                           sem("conv_done"), sem("xs_done"))
        g_psum, g_done, sx_psum = sem("g_psum"), sem("g_done"), sem("sx_psum")
        a_clamped, a_step, zero_done = sem("a_clamped"), sem("a_step"), sem("zero_done")
        W3 = RK + 2 * NS
        SMALL = [DJ, 0, 1, 2, 3, 4, 5, 6, DJ + 1, 7, DJ + 2]
        with nc.Block() as block:
            @block.sync
            def _(sp):
                rows_in = w_in.rearrange("(w j p) d -> j p w d", p=P, w=2)
                cols_out = w_out.rearrange("(c p) (j q) -> j p c q", p=P, q=P)
                for j in range(DJ):
                    if j >= 3:
                        sp.wait_ge(in_psum, 2 * (j - 2))
                        sp.wait_ge(small_psum, SMALL.index(j - 3) + 1)
                    sp.dma_start(win_nat[j % 3][:], rows_in[j]).then_inc(ld_in[j], 16)
                    sp.dma_start(wout_nat[j % 3][:], cols_out[j]).then_inc(ld_in[j], 16)
                    if j == 0:
                        sp.dma_start(convw[:], conv_w.rearrange("(j p) k -> p j k", p=P)).then_inc(ld_v, 16)
                        sp.dma_start(Aneg[:], a_log.rearrange("(j p) n -> p j n", p=P)).then_inc(ld_v, 16)
                        with nc.allow_non_contiguous_dma(reason="one value to a partition"):
                            for dst, src in ((convb, conv_b), (bdt, b_dt), (dsk, d_skip)):
                                sp.dma_start(dst[:], src.rearrange("(j p) -> p j", p=P)).then_inc(ld_v, 16)
                    if j == 0:
                        sp.dma_start(wx_nat[:], w_x).then_inc(ld_s, 16)
                        sp.dma_start(wdt_nat[:], w_dt.rearrange("(j p) r -> p j r", p=P)).then_inc(ld_s, 16)

            @block.tensor
            def _(pe):
                def transpose(j, w):
                    if j >= DJ:
                        return
                    i = 2 * j + w
                    pe.wait_ge(ld_in[j], 32)
                    if i >= 2:
                        pe.wait_ge(in_low, i - 1)
                    for c in range(DC):
                        last = pe.transpose(bank[i % 2][:, c * P:(c + 1) * P], win_nat[j % 3][:, w, c * P:(c + 1) * P], ident[:])
                    last.then_inc(in_psum, 1)

                def small(i):
                    k = SMALL.index(i)
                    if k:
                        pe.wait_ge(small_done, k)
                    b = bank[6]
                    if i == DJ:
                        pe.wait_ge(ld_s, 32)
                        for j in range(DJ):
                            last = pe.transpose(b[:, j * W3:(j + 1) * W3], wx_nat[:, j * P:(j + 1) * P], ident[0:W3, 0:W3])
                    elif i < DJ:
                        for c in range(DC):
                            last = pe.transpose(b[:, c * P:(c + 1) * P], wout_nat[i % 3][:, c, :], ident[:])
                    else:
                        for k in range(4):
                            last = pe.transpose(b[0:RK, k * P:(k + 1) * P], wdt_nat[:, 4 * (i - DJ - 1) + k, :], ident[:])
                    last.then_inc(small_psum, 1)

                def mix(j):
                    pe.wait_ge(xs_done, j + 1)
                    if j == 0:
                        pe.wait_ge(small_done, 1)
                    for t in range(NT):
                        last = pe.matmul(bank[7][:, t * W3:(t + 1) * W3], XS[:, j, t * P:(t + 1) * P], WxT[:, j, :],
                                         start=(j == 0 and t == 0), stop=(j == DJ - 1), skip_group_check=True)
                    if j == DJ - 1:
                        last.then_inc(sx_psum, 1)

                def product(j, ch, w):
                    n = NCH * j + ch
                    if n >= 2:
                        pe.wait_ge((xp_done, g_done)[w], n - 1)
                    for c in range(DC):
                        last = three_products(pe, bank[2 + 2 * w + n % 2][:], [m[:, c, :] for m in WinT[w][j % 2]],
                                              [m[:, c, ch * CH:(ch + 1) * CH] for m in XnT], c == 0, c == DC - 1)
                    last.then_inc((xp_psum, g_psum)[w], 1)

                transpose(0, 0)
                transpose(0, 1)
                for j in range(DJ):
                    transpose(j + 1, 0)
                    pe.wait_ge(in_low, 2 * j + 2)
                    product(j, 0, 0)
                    transpose(j + 1, 1)
                    product(j, 1, 0)
                    if j == 0:
                        small(DJ)
                    product(j, 0, 1)
                    small(j)
                    product(j, 1, 1)
                    if j >= DJ - 2:
                        small(j + 3)
                    if j >= 2:
                        mix(j - 2)
                mix(DJ - 2)
                mix(DJ - 1)

            @block.scalar
            def _(act):
                def high(j, w):
                    if j < DJ:
                        i = 2 * j + w
                        act.wait_ge(in_psum, i + 1)
                        act.copy(WinT[w][j % 2][0][:], bank[i % 2][:].rearrange("p (c n) -> p c n", c=DC)).then_inc(in_high, 1)

                def small(i):
                    act.wait_ge(small_psum, SMALL.index(i) + 1)
                    b = bank[6]
                    if i < DJ:
                        act.copy(WoutT[:, i, :], b[:]).then_inc(small_done, 1)
                    elif i == DJ:
                        act.copy(WxT[:].rearrange("p j w -> p (j w)"), b[:]).then_inc(small_done, 1)
                    else:
                        m = i - DJ - 1
                        act.copy(WdtT[:, m * 512:(m + 1) * 512], b[0:RK, :]).then_inc(small_done, 1)

                def conv_silu(j):
                    act.wait_ge(conv_done, j + 1)
                    act.activation(XS[:, j, :], acc[j % 2][:], ACT.Silu, bias=convb[:, j:j + 1]).then_inc(xs_done, 1)

                high(0, 0)
                high(0, 1)
                act.wait_ge(a_clamped, 1)
                act.activation(Aneg[:], Aneg[:], ACT.Exp).then_inc(a_step, 1)
                act.wait_ge(a_step, 1)
                act.mul(Aneg[:], Aneg[:], -1.0).then_inc(a_step, 1)
                for j in range(DJ):
                    high(j + 1, 0)
                    if j >= 2:
                        act.wait_ge(conv_done, j - 1)
                    for ch in range(NCH):
                        n = NCH * j + ch
                        act.wait_ge(xp_psum, n + 1)
                        act.copy(XP[j % 2][:, KC - 1 + ch * CH:KC - 1 + (ch + 1) * CH], bank[2 + n % 2][:]).then_inc(xp_done, 1)
                        if ch == 0:
                            high(j + 1, 1)
                    if j:
                        conv_silu(j - 1)
                    if j == 0:
                        small(DJ)
                    small(j)
                    for ch in range(NCH):
                        n = NCH * j + ch
                        act.wait_ge(g_psum, n + 1)
                        act.activation(G[:, j, ch * CH:(ch + 1) * CH], bank[4 + n % 2][:], ACT.Silu).then_inc(g_done, 1)
                    if j >= DJ - 2:
                        small(j + 3)
                conv_silu(DJ - 1)

            @block.gpsimd
            def _(pool):
                for i in range(2):
                    pool.memset(XP[i][:, 0:KC - 1], 0.0).then_inc(zero_done, 1)
                pool.memset(state[:], 0.0).then_inc(zero_done, 1)

            @block.vector
            def _(dve):
                def low(j, w):
                    if j < DJ:
                        i = 2 * j + w
                        high, low_ = WinT[w][j % 2]
                        dve.wait_ge(in_high, i + 1)
                        dve.tensor_tensor(low_[:], bank[i % 2][:].rearrange("p (c n) -> p c n", c=DC), high[:].bitcast(F32),
                                          ALU.subtract).then_inc(in_low, 1)

                low(0, 0)
                low(0, 1)
                dve.wait_ge(ld_v, 80)
                dve.tensor_scalar(Aneg[:], Aneg[:], A_LOG_MAX, None, ALU.min).then_inc(a_clamped, 1)
                dve.wait_ge(zero_done, 2)
                for j in range(DJ):
                    low(j + 1, 0)
                    low(j + 1, 1)
                    dve.wait_ge(xp_done, NCH * (j + 1))
                    if j >= 2:
                        dve.wait_ge(xs_done, j - 1)
                    a = acc[j % 2][:]
                    dve.tensor_scalar(a, XP[j % 2][:, KC - 1:], convw[:, j, KC - 1:KC], None, ALU.mult).then_inc(conv_step, 1)
                    for k in range(KC - 1):
                        dve.wait_ge(conv_step, 3 * j + k + 1)
                        dve.scalar_tensor_tensor(a, XP[j % 2][:, k:k + S], convw[:, j, k:k + 1], a, ALU.mult,
                                                 ALU.add).then_inc(conv_done if k == KC - 2 else conv_step, 1)

        mem = ExitStack()
        BC = sb_in(mem, "BC", [P, 2 * NS, CH])
        ss = sb_in(mem, "ss", [2 * W3, CH], F32R)
        pick = sb_in(mem, "pick", [2 * W3, W3], F32R)
        diag = [WxT[:].rearrange("p j w -> p (j w)")[:, i * P:(i + 1) * P] for i in range(2)]
        m3 = sb_in(mem, "m3", [P, 3, NT])
        r3 = sb_in(mem, "r3", [P, 3, NT])
        v3 = sb_in(mem, "v3", [P, 3, NT])
        nh3 = sb_in(mem, "nh3", [P, 3, NT])
        mem.close()
        SS, SSq = (x_[:].rearrange("p (k w) -> p k w", k=NT) for x_ in dA[0:2])
        twice = BC[:, 0:2, :].rearrange("p a n -> p (a n)").rearrange("p (t c) -> p t c", t=NT)
        E, R = (x_[:] for x_ in Xn)
        GROUPS = ((0, RK), (RK, RK + NS), (RK + NS, W3))
        sx_step, sx_ms, sx_eps, sx_r, sx_n = (sem(n) for n in ("sx_step", "sx_ms", "sx_eps", "sx_r", "sx_n"))
        st_psum, st_done, ss_high, ss_low, nh3_set, pick_done = sem("st_psum"), sem("st_done"), sem("ss_high"), sem("ss_low"), sem("nh3_set"), sem("pick_done")
        bc_psum, b_done, c_done = sem("bc_psum"), sem("b_done"), sem("c_done")
        z_psum, z_read, e_step, l_done, dt_done, dtu_done = (sem(n) for n in ("z_psum", "z_read", "e_step", "l_done", "dt_done",
                                                                              "dtu_done"))
        diag_done, y_done = sem("diag_done"), sem("y_done")
        da_done, db_done, scan_done, hc_done, y_acc, st_copied = (sem(n) for n in ("da_done", "db_done", "scan_done", "hc_done",
                                                                                   "y_acc", "st_copied"))
        out_psum, out_added = sem("out_psum"), sem("out_added")
        NJ, FIRST, LAG = NCH * DJ, 12, 5
        SWITCH = (DJ - 1) * NS
        OUT0, OUT_EVERY = DJ * NS + 12, 3
        ROWS = ((2, 3), (6, 7))
        SOFTPLUS = (4, 6, 8, 10)

        made_at = {r: 2 * (r - FIRST) for r in range(FIRST, NS)} | {NS + r: SWITCH + (3 * r + 1) // 2 for r in range(NS)}

        def tokens(jj):
            return slice(jj // DJ * CH, (jj // DJ + 1) * CH)

        def rows_made(i):
            return i // (DJ * NS) * NS + i % NS + 1

        with nc.Block() as block:
            @block.tensor
            def _(pe):
                def delta(jj):
                    if jj >= 2:
                        pe.wait_ge(z_read, 2 * (jj - 1))
                    j = jj % DJ
                    pe.matmul(bank[4 + jj % 2][:], WdtT[:, j * P:(j + 1) * P], ssT[0:RK, tokens(jj)], start=True,
                              stop=True).then_inc(z_psum, 1)

                def rows(r):
                    if r >= 2:
                        pe.wait_ge(b_done, r - 1)
                        pe.wait_ge(c_done, r - 1)
                    if r == NS:
                        pe.wait_ge(ss_low, 2)
                    for k in range(2):
                        c = RK + k * NS + r % NS
                        last = pe.matmul(bank[ROWS[r % 2][k]][:], pick[:, c:c + 1].to_broadcast([2 * W3, P]), ss[:], start=True, stop=True)
                    last.then_inc(bc_psum, 1)

                pe.wait_ge(sx_n, 6)
                for t in range(NT):
                    last = pe.transpose(bank[t // TPC][:, t % TPC * P:(t % TPC + 1) * P], twice[:, t], ident[:])
                last.then_inc(st_psum, 1)
                pe.wait_ge(st_done, 2)
                delta(0)
                delta(1)
                pe.wait_ge(ss_low, 1)
                pe.wait_ge(pick_done, 1)
                for r in range(FIRST):
                    rows(r)
                for i in range(NJ * NS):
                    jj, n = divmod(i, NS)
                    y = bank[jj % 2]
                    if n == 0:
                        pe.wait_ge(diag_done, jj + 1)
                        if jj >= 2:
                            pe.wait_ge(y_done, jj - 1)
                        pe.matmul(y[:], diag[jj % 2], XS[:, jj % DJ, tokens(jj)], start=True, stop=False)
                    if n == 12 and jj + 2 < NJ:
                        delta(jj + 2)
                    pe.wait_ge(hc_done, i + 1)
                    pe.matmul(y[:], ident[:], Hs[i % len(Hs)][:], start=False, stop=(n == NS - 1)).then_inc(y_acc, 1)
                    for r in (r for r in made_at if made_at[r] == i):
                        rows(r)
                    m, off = divmod(i - OUT0, OUT_EVERY)
                    if 0 <= m < TPC * DJ and off == 0:
                        t, j = divmod(m, DJ)
                        if m == 0:
                            pe.wait_ge(y_done, DJ)
                            pe.wait_ge(c_done, 2 * NS)
                        if j == 0 and t >= 2:
                            pe.wait_ge(out_added, t - 1)
                        last = pe.matmul(bank[6 + t % 2][:], XS[:, j, t * P:(t + 1) * P], WoutT[:, j, :], start=(j == 0),
                                         stop=(j == DJ - 1))
                        if j == DJ - 1:
                            last.then_inc(out_psum, 1)

            @block.scalar
            def _(act):
                def softplus(jj, part):
                    b, bias = bank[4 + jj % 2][:], bdt[:, jj % DJ:jj % DJ + 1]
                    if part == 0:
                        act.wait_ge(z_psum, jj + 1)
                        if jj:
                            act.wait_ge(dt_done, jj)
                        act.activation(E, b, ACT.Abs, bias=bias).then_inc(z_read, 1)
                    elif part == 1:
                        act.activation(R, b, ACT.Relu, bias=bias).then_inc(z_read, 1)
                    elif part == 2:
                        act.wait_ge(z_read, 2 * jj + 2)
                        act.activation(E, E, ACT.Exp, scale=-1.0).then_inc(e_step, 1)
                    else:
                        act.wait_ge(e_step, jj + 1)
                        act.activation(E, E, ACT.Ln, bias=1.0).then_inc(l_done, 1)

                def high(ch):
                    act.copy(ss[:], ssT[:, ch * CH:(ch + 1) * CH]).then_inc(ss_high, 1)

                def row(r, k):
                    act.wait_ge(bc_psum, r + 1)
                    act.copy(BC[:, k * NS + r % NS, :], bank[ROWS[r % 2][k]][:]).then_inc((b_done, c_done)[k], 1)

                for ch in range(NCH):
                    act.wait_ge(st_psum, 1)
                    act.copy(ssT[:, ch * CH:(ch + 1) * CH], bank[ch][:]).then_inc(st_done, 1)
                act.wait_ge(st_done, 1)
                high(0)
                for part in range(4):
                    softplus(0, part)
                for r in range(FIRST):
                    row(r, 0)
                for i in range(NJ * NS + 4):
                    jj, n = divmod(i, NS)
                    if 3 <= i < DJ * NS + 3:
                        act.wait_ge(scan_done, i - 2)
                        act.copy(state[:, (i - 3) // NS, (i - 3) % NS:(i - 3) % NS + 1], Hs[(i - 3) % len(Hs)][:, CH - 1:CH]).then_inc(st_copied, 1)
                    if i < NJ * NS:
                        if n == 0:
                            act.wait_ge(dt_done, jj + 1)
                        if i >= 3:
                            act.wait_ge(scan_done, i - 2)
                        act.activation(dA[i % 3][:], DT[jj % 2][:], ACT.Exp, scale=Aneg[:, jj % DJ, n:n + 1]).then_inc(da_done, 1)
                    for k in (1, 0):
                        for r in (r for r in made_at if made_at[r] == i - LAG - k):
                            row(r, k)
                    if i == SWITCH - NS:
                        act.wait_ge(b_done, NS)
                        high(1)
                    if n in SOFTPLUS and jj + 1 < NJ:
                        softplus(jj + 1, SOFTPLUS.index(n))

            @block.gpsimd
            def _(pool):
                pool.memset(nh3[:], -0.5).then_inc(nh3_set, 1)
                pool.tensor_tensor(pick[:], ident[:, 0:W3], ident[:, W3:], ALU.add).then_inc(pick_done, 1)
                pool.wait_ge(sx_ms, 3)
                for i, (a, b) in enumerate(GROUPS):
                    pool.tensor_scalar(v3[:, i, :], m3[:, i, :], 1.0 / (b - a), 1e-6, ALU.mult, ALU.add).then_inc(sx_eps, 1)
                pool.wait_ge(sx_eps, 3)
                pool.wait_ge(nh3_set, 1)
                pool.tensor_tensor(r3[:], v3[:], nh3[:], ALU.pow).then_inc(sx_r, 1)

                def skip(jj):
                    if jj >= 2:
                        pool.wait_ge(y_acc, NS * (jj - 1))
                    pool.tensor_tensor(diag[jj % 2], ident[:], dsk[:, jj % DJ:jj % DJ + 1].to_broadcast([P, P]),
                                       ALU.mult).then_inc(diag_done, 1)

                def delta_u(jj):
                    pool.wait_ge(dt_done, jj + 1)
                    if jj >= 2:
                        pool.wait_ge(db_done, NS * (jj - 1))
                    pool.tensor_tensor(DTU[jj % 2][:], DT[jj % 2][:], XS[:, jj % DJ, tokens(jj)], ALU.mult).then_inc(dtu_done, 1)

                pool.wait_ge(sx_psum, 1)
                skip(0)
                delta_u(0)
                for i in range(NJ * NS):
                    jj, n = divmod(i, NS)
                    if n == 0:
                        pool.wait_ge(dtu_done, jj + 1)
                    if jj % DJ == 0:
                        pool.wait_ge(b_done, rows_made(i))
                    if i >= len(Hs):
                        pool.wait_ge(y_acc, i - len(Hs) + 1)
                    pool.tensor_tensor(Hs[i % len(Hs)][:], DTU[jj % 2][:], BC[:, n, :], ALU.mult).then_inc(db_done, 1)
                    if jj + 1 < NJ:
                        if n == 8:
                            skip(jj + 1)
                        if n == 13:
                            delta_u(jj + 1)

            @block.vector
            def _(dve):
                dve.wait_ge(sx_psum, 1)
                dve.tensor_copy(SS.rearrange("p k w -> p (k w)"), bank[7][:]).then_inc(sx_step, 1)
                dve.wait_ge(sx_step, 1)
                dve.tensor_tensor(SSq, SS, SS, ALU.mult).then_inc(sx_step, 1)
                dve.wait_ge(sx_step, 2)
                for i, (a, b) in enumerate(GROUPS):
                    dve.tensor_reduce(m3[:, i, :], SSq[:, :, a:b], AX_X, ALU.add).then_inc(sx_ms, 1)
                dve.wait_ge(sx_r, 1)
                for i, (a, b) in enumerate(GROUPS):
                    for o in (0, W3):
                        dve.tensor_tensor(twice[:, :, o + a:o + b], SS[:, :, a:b],
                                          r3[:, i, :].unsqueeze(2).to_broadcast([P, NT, b - a]), ALU.mult).then_inc(sx_n, 1)

                def low(ch):
                    dve.wait_ge(ss_high, ch + 1)
                    dve.tensor_tensor(ss[W3:, :], ssT[W3:, ch * CH:(ch + 1) * CH], ss[W3:, :].bitcast(F32),
                                       ALU.subtract).then_inc(ss_low, 1)

                def delta(jj):
                    dve.wait_ge(l_done, jj + 1)
                    if jj >= 2:
                        dve.wait_ge(da_done, NS * (jj - 1))
                        dve.wait_ge(dtu_done, jj - 1)
                    dve.tensor_tensor(DT[jj % 2][:], R, E, ALU.add).then_inc(dt_done, 1)

                def weigh(i):
                    dve.wait_ge(scan_done, i + 1)
                    if i < DJ * NS:
                        dve.wait_ge(st_copied, i + 1)
                    if i // NS % DJ == 0:
                        dve.wait_ge(c_done, rows_made(i))
                    h = Hs[i % len(Hs)][:]
                    dve.tensor_tensor(h, h, BC[:, NS + i % NS, :], ALU.mult).then_inc(hc_done, 1)

                def gate(jj):
                    dve.wait_ge(y_acc, NS * (jj + 1))
                    dve.tensor_tensor(XS[:, jj % DJ, tokens(jj)], bank[jj % 2][:], G[:, jj % DJ, tokens(jj)],
                                      ALU.mult).then_inc(y_done, 1)

                low(0)
                delta(0)
                for r in range(FIRST):
                    dve.wait_ge(bc_psum, r + 1)
                    dve.tensor_copy(BC[:, NS + r, :], bank[ROWS[r % 2][1]][:]).then_inc(c_done, 1)
                for i in range(NJ * NS):
                    jj, n = divmod(i, NS)
                    if n == 11 and jj + 1 < NJ:
                        delta(jj + 1)
                    dve.wait_ge(da_done, i + 1)
                    dve.wait_ge(db_done, i + 1)
                    first = jj < DJ
                    if i == DJ * NS:
                        dve.wait_ge(st_copied, DJ * NS)
                    dve.tensor_tensor_scan(Hs[i % len(Hs)][:], dA[i % 3][:], Hs[i % len(Hs)][:],
                                           0.0 if first else state[:, jj % DJ, n:n + 1], ALU.mult, ALU.add).then_inc(scan_done, 1)
                    if i >= 2:
                        weigh(i - 2)
                    if i == SWITCH - NS + 2:
                        low(1)
                    if n == 4 and jj:
                        gate(jj - 1)
                    t, off = divmod(i - OUT0 - OUT_EVERY * DJ, OUT_EVERY * DJ)
                    if 0 <= t < TPC and off == 0:
                        dve.wait_ge(out_psum, t + 1)
                        dve.tensor_tensor(X[:, t, :], bank[6 + t % 2][:], X[:, t, :], ALU.add).then_inc(out_added, 1)
                weigh(NJ * NS - 2)
                weigh(NJ * NS - 1)
                gate(NJ - 1)

        ssm.close()
        ffn2 = ExitStack()
        f2 = FeedForward(ffn2, "f2")
        ffn2.close()

        def load_first(sp):
            f2.load(sp, 0)
            f2.load(sp, 1)

        project_onto_x("ssm", lambda j, t: XS[:, j, t * P:(t + 1) * P], lambda j: WoutT[:, j, :], DJ,
                       range(TPC, NT), Norm(), load_first)
        f2.run(None)


NAMES = ["x", "wq_a", "q_a_ln_w", "wq_b", "wkv_a", "kv_a_ln_w", "wkv_b", "wo"]
INPUTS = ([f"L0_attn_a_{n}" for n in NAMES]
          + [f"L0_attn_b_{n}" for n in ("W_in", "conv_w", "conv_b", "W_x", "W_dt", "b_dt", "A_log", "D", "W_out")]
          + [f"L0_ffn_{n}" for n in ("W_gate", "W_up", "W_down")])


def kernel(**inputs):
    import concourse.bacc as bacc
    from concourse.bass_utils import run_bass_kernel_spmd

    nc = bacc.Bacc("TRN2", target_bir_lowering=False, num_devices=1)
    arrays = {f"in_{n}": np.ascontiguousarray(inputs[n]) for n in INPUTS}
    arrays["rope_cos"], arrays["rope_sin"] = rope_tables()
    args = [nc.dram_tensor(n, a.shape, mybir.dt.from_np(a.dtype), kind="ExternalInput").ap() for n, a in arrays.items()]
    args.append(nc.dram_tensor("out", (1, S, DM), F32, kind="ExternalOutput").ap())
    layer(nc, *args)
    r = run_bass_kernel_spmd(nc, [arrays], core_ids=[0])
    return r.results[0]["out"]
```

```python
import math
from contextlib import ExitStack

import numpy as np

import concourse.bass as bass
from concourse import mybir

F32 = mybir.dt.float32
F32R = mybir.dt.float32r
BF16 = mybir.dt.bfloat16
ALU = mybir.AluOpType
ACT = mybir.ActivationFunctionType
AX_X = mybir.AxisListType.X

P = 128
S, DM = 1024, 512
NT = S // P
DC = DM // P
H, NOPE, ROPE, VD = 32, 64, 64, 128
QR, KVR = 128, 32
HG = 4
NG = H // HG
QW = ROPE + KVR
QK = QW + 1
SOFTMAX_SCALE = (NOPE + ROPE) ** -0.5 * (0.1 * math.log(128.0) + 1.0) ** 2
MASKED = -1e30
A_LOG_MAX = 80.0
FF = 1376
FT = -(-FF // P)
DI, NS, KC, RK = 1024, 16, 4, 32
DJ = DI // P
CH = 512
NCH = S // CH
TPC = CH // P


def rope_tables():
    base, factor, orig = 10000.0, 128.0, 1024

    def corr_dim(r):
        return ROPE * math.log(orig / (r * 2 * math.pi)) / (2 * math.log(base))

    low = max(math.floor(corr_dim(32.0)), 0)
    high = min(math.ceil(corr_dim(1.0)), ROPE - 1)
    hi = high + 0.001 if low == high else float(high)
    ramp = np.clip((np.arange(ROPE // 2, dtype=np.float32) - low) / (hi - low), 0.0, 1.0)
    mask = 1.0 - ramp
    extra = 1.0 / base ** (np.arange(0, ROPE, 2, dtype=np.float32) / ROPE)
    inter = extra / factor
    freqs = np.outer(np.arange(S, dtype=np.float32), inter * (1.0 - mask) + extra * mask)
    cos, sin = np.cos(freqs).astype(np.float32), np.sin(freqs).astype(np.float32)
    return np.concatenate([cos, cos], axis=1), np.concatenate([-sin, sin], axis=1)


class Run:

    def __init__(self, handle, base):
        self.sem, self.base = handle, base

    def __call__(self, value):
        return self.sem, self.base + value


def layer(nc, x, wq_a, q_ln, wq_b, wkv_a, kv_ln, wkv_b, wo, w_in, conv_w, conv_b, w_x, w_dt, b_dt,
          a_log, d_skip, w_out, w_gate, w_up, w_down, rope_cos, rope_sin, out):
    top = ExitStack()

    def sb_in(stack, name, shape, dt=F32):
        return stack.enter_context(nc.sbuf_tensor(name, shape, dt))

    def sem(name):
        return top.enter_context(nc.semaphore(name))

    with top:
        bank = [top.enter_context(nc.psum_tensor(f"bank{i}", [P, 512], F32)) for i in range(8)]
        X = sb_in(top, "X", [P, NT, DM])
        scan_space = ExitStack()
        dA, Hs, DT, DTU = ([sb_in(scan_space, f"{n}{i}", [P, CH]) for i in range(ring)]
                           for n, ring in (("dA", 3), ("Hs", 7), ("DT", 2), ("DTU", 2)))
        ssT = sb_in(scan_space, "ssT", [2 * (RK + 2 * NS), S])
        scan_space.close()
        XnT = [sb_in(top, f"XnT{i}", [P, DC, S], F32R) for i in "hl"]
        Xn = [sb_in(top, f"Xn{i}", [P, DM]) for i in range(2)]
        ident = sb_in(top, "ident", [P, P])
        identb = sb_in(top, "identb", [P, P], BF16)
        ones = sb_in(top, "ones", [P, KVR])
        neghalf = sb_in(top, "neghalf", [P, 16])
        stats = sb_in(top, "stats", [P, NT, 6])
        meanvar = sb_in(top, "meanvar", [P, NT, 2])
        veps = sb_in(top, "veps", [P, 16])
        rstd = sb_in(top, "rstd", [P, 16])

        runs = {}

        def again(name, total):
            if name not in runs:
                runs[name] = [sem(name), 0]
            handle, base = runs[name]
            runs[name][1] += total
            return Run(handle, base)

        consts = sem("consts")
        stored = sem("stored")
        const_step = sem("const_step")

        class Norm:

            def __init__(self):
                self.high, self.low = XnT
                (self.stats_done, self.aggr_done, self.eps_done, self.rstd_done, self.xn_done, self.psum_full,
                 self.high_done, self.low_done) = (again(f"norm_{n}", NT) for n in
                                                   ("stats", "aggr", "eps", "rstd", "xn", "psum", "high", "low"))

            def tile(self, t):
                return t, bank[t % 2][:].rearrange("p (c n) -> p c n", c=DC), slice(t * P, (t + 1) * P)

            def vector_stats(self, dve, t):
                i, _, _ = self.tile(t)
                dve.bn_stats(stats[:, t, :], X[:, t, :]).then_inc(self.stats_done.sem, 1)
                dve.wait_ge(*self.stats_done(i + 1))
                dve.bn_aggr(meanvar[:, t, :], stats[:, t, :]).then_inc(self.aggr_done.sem, 1)

            def pool_rstd(self, pool, t):
                i, _, _ = self.tile(t)
                pool.wait_ge(*self.aggr_done(i + 1))
                pool.tensor_scalar(veps[:, t:t + 1], meanvar[:, t, 1:2], 1e-5, None, ALU.add).then_inc(self.eps_done.sem, 1)
                pool.wait_ge(*self.eps_done(i + 1))
                pool.tensor_tensor(rstd[:, t:t + 1], veps[:, t:t + 1], neghalf[:, 0:1], ALU.pow).then_inc(self.rstd_done.sem, 1)

            def vector_normalize(self, dve, t):
                i, _, _ = self.tile(t)
                dve.wait_ge(*self.rstd_done(i + 1))
                if i >= 2:
                    dve.wait_ge(*self.psum_full(i - 1))
                dve.tensor_scalar(Xn[i % 2][:], X[:, t, :], meanvar[:, t, 0:1], rstd[:, t:t + 1],
                                  ALU.subtract, ALU.mult).then_inc(self.xn_done.sem, 1)

            def tensor_transpose(self, pe, t):
                i, _, _ = self.tile(t)
                pe.wait_ge(*self.xn_done(i + 1))
                if i >= 2:
                    pe.wait_ge(*self.low_done(i - 1))
                for c in range(DC):
                    last = pe.transpose(bank[i % 2][:, c * P:(c + 1) * P], Xn[i % 2][:, c * P:(c + 1) * P], ident[:])
                last.then_inc(self.psum_full.sem, 1)

            def scalar_high(self, act, t):
                i, b, cols = self.tile(t)
                act.wait_ge(*self.psum_full(i + 1))
                act.copy(self.high[:, :, cols], b).then_inc(self.high_done.sem, 1)

            def vector_low(self, dve, t):
                i, b, cols = self.tile(t)
                dve.wait_ge(*self.high_done(i + 1))
                dve.tensor_tensor(self.low[:, :, cols], b, self.high[:, :, cols].bitcast(F32),
                                  ALU.subtract).then_inc(self.low_done.sem, 1)

            def vector_step(self, dve, i):
                if i < NT:
                    self.vector_stats(dve, i)
                if 0 <= i - 1 < NT:
                    self.vector_normalize(dve, i - 1)
                if 0 <= i - 3 < NT:
                    self.vector_low(dve, i - 3)

        def three_products(pe, out, lhs, rhs, first, last):
            (lh, ll), (rh, rl) = lhs, rhs
            pe.matmul(out, lh, rh, start=first, stop=False)
            pe.matmul(out, lh, rl, start=False, stop=False)
            return pe.matmul(out, ll, rh, start=False, stop=last)

        att = ExitStack()
        WVO = [sb_in(att, f"WVO{i}", [P, NG, DM], F32R) for i in "hl"]
        NQW = QR + KVR + ROPE
        HP = H // 4
        early = ExitStack()
        wqb_nat = [sb_in(early, f"wqb_nat{i}", [P, HP, QR]) for i in range(2)]
        QA = sb_in(early, "QA", [P, NT, NQW])
        SQ = sb_in(early, "SQ", [P, NT, QR + KVR])
        wk_nat = sb_in(early, "wk_nat", [NOPE, H, KVR])
        woT = [sb_in(early, "woT0", [P, HG, DM])]
        early.close()
        OT = sb_in(att, "OT", [P, NG * S])
        WQ = [sb_in(att, f"WQ{i}", [P, H * QW], F32R) for i in "hl"]
        QnT = [sb_in(att, f"QnT{i}", [P, S], F32R) for i in "hl"]
        KTM = sb_in(att, "KTM", [P, NT, QK])
        KTh = sb_in(att, "KTh", [QK, S], F32R)
        KTl = sb_in(att, "KTl", [QK, S], F32R)
        cosT = sb_in(att, "cosT", [P, NT, 2, 32])
        sinT = sb_in(att, "sinT", [P, NT, 2, 32])
        maskqk = sb_in(att, "maskqk", [P, P], BF16)
        maskkq = sb_in(att, "maskkq", [P, P], BF16)

        prep = ExitStack()
        na = Norm()
        wa_nat = sb_in(prep, "wa_nat", [P, DM])
        wkva_nat = sb_in(prep, "wkva_nat", [KVR + ROPE, DM])
        WaT = [sb_in(prep, f"WaT{i}", [P, DC, NQW], F32R) for i in "hl"]
        wv_nat = sb_in(prep, "wv_nat", [P, H, KVR])
        woT.append(sb_in(prep, "woT1", [P, HG, DM]))
        wo_nat = [sb_in(prep, f"wo_nat{i}", [P, DC, 2 * VD]) for i in range(3)]
        qlnw = sb_in(prep, "qlnw", [P, QR])
        kvlnw = sb_in(prep, "kvlnw", [P, KVR])
        QAn = [x_[:].rearrange("p (t r) -> p t r", r=QR) for x_ in Xn]
        RAk = sb_in(prep, "RAk", [P, NT, 2, 32])
        RBk = sb_in(prep, "RBk", [P, NT, 2, 32])
        rs = sb_in(prep, "rs", [P, 2 * NT])
        ms = sb_in(prep, "ms", [P, 2 * NT])
        prep.close()
        ld_x = [sem(f"ld_x{i}") for i in range(NT // 2)]
        ld_a, ld_k, ld_v_up, ld_small = sem("ld_a"), sem("ld_k"), sem("ld_v_up"), sem("ld_small")
        ld_q, ld_wo = [sem(f"ld_q{i}") for i in range(2)], [sem(f"ld_wo{i}") for i in range(3)]
        wot_psum, wot_done, wot_copied = sem("wot_psum"), sem("wot_done"), sem("wot_copied")

        def by_vector(h):
            return h >= 4 * HG and h % 2 == 1

        def copied(h):
            mine = [k for k in range(h + 1) if by_vector(k) == by_vector(h)]
            return (wot_copied if by_vector(h) else wot_done), len(mine)
        wvo_psum, wvo_high, wvo_low = sem("wvo_psum"), sem("wvo_high"), sem("wvo_low")
        masks0, masks = sem("masks0"), sem("masks")
        wa_psum, wa_high, wa_low = sem("wa_psum"), sem("wa_high"), sem("wa_low")
        proj_psum, proj_out = sem("proj_psum"), sem("proj_out")
        wq_psum, wq_high, wq_low = sem("wq_psum"), sem("wq_high"), sem("wq_low")
        qn_psum, qn_high, qn_low = sem("qn_psum"), sem("qn_high"), sem("qn_low")
        kt_psum, kt_high, kt_low = sem("kt_psum"), sem("kt_high"), sem("kt_low")
        sq_done, ms_done, rs_step, rs_done = sem("sq_done"), sem("ms_done"), sem("rs_step"), sem("rs_done")
        kstep, qn_done, ktm_done = sem("kstep"), sem("qn_done"), sem("ktm_done")

        with nc.Block() as block:
            @block.sync
            def _(sp):
                rows = x[0].rearrange("(t p) d -> p t d", p=P)
                for i in range(4):
                    sp.dma_start(X[:, 2 * i:2 * i + 2, :], rows[:, 2 * i:2 * i + 2, :]).then_inc(ld_x[i], 16)
                    if i == 0:
                        sp.dma_start(wa_nat[:], wq_a).then_inc(ld_a, 16)
                        sp.dma_start(wkva_nat[:], wkv_a).then_inc(ld_a, 16)
                kvb = wkv_b.rearrange("(h m) r -> m h r", m=NOPE + VD)
                wqb = wq_b.rearrange("(q h m) r -> q m h r", m=P, q=H // HP)
                sp.dma_start(wqb_nat[0][:], wqb[0]).then_inc(ld_q[0], 16)
                sp.dma_start(wk_nat[:], kvb[0:NOPE]).then_inc(ld_k, 16)
                sp.dma_start(wqb_nat[1][:], wqb[1]).then_inc(ld_q[1], 16)
                sp.dma_start(cosT[:], rope_cos.rearrange("(t p) (a i) -> p t a i", p=P, a=2)).then_inc(ld_small, 16)
                sp.dma_start(sinT[:], rope_sin.rearrange("(t p) (a i) -> p t a i", p=P, a=2)).then_inc(ld_small, 16)
                sp.dma_start(qlnw[:], q_ln.rearrange("(a r) -> a r", a=1).to_broadcast([P, QR])).then_inc(ld_small, 16)
                sp.dma_start(kvlnw[:], kv_ln.rearrange("(a r) -> a r", a=1).to_broadcast([P, KVR])).then_inc(ld_small, 16)
                wo_cols = wo.rearrange("(c p) (k n) -> k p c n", p=P, n=2 * VD)

                def load_wo(k):
                    if k >= 3:
                        sp.wait_ge(wot_psum, 2 * (k - 2))
                    sp.dma_start(wo_nat[k % 3][:], wo_cols[k]).then_inc(ld_wo[k % 3], 16)

                sp.dma_start(wv_nat[:], kvb[NOPE:NOPE + VD]).then_inc(ld_v_up, 16)
                for k in range(3):
                    load_wo(k)
                for q in range(2, H // HP):
                    sp.wait_ge(wq_psum, HP // HG * (q - 1))
                    sp.dma_start(wqb_nat[q % 2][:], wqb[q]).then_inc(ld_q[q % 2], 16)
                for k in range(3, H // 2):
                    load_wo(k)

            @block.gpsimd
            def _(pool):
                pool.memset(neghalf[:], -0.5).then_inc(const_step, 1)
                pool.memset(ident[:], 0.0).then_inc(const_step, 1)
                pool.memset(ones[:], 1.0).then_inc(consts, 1)
                pool.wait_ge(const_step, 2)
                pool.affine_select(out=ident[:], in_=ident[:], compare_op=ALU.not_equal, fill=1.0, base=0,
                                   pattern=[[-1, P]], channel_multiplier=1).then_inc(consts, 1)
                pool.wait_ge(consts, 2)
                pool.tensor_copy(identb[:], ident[:]).then_inc(consts, 1)
                for t in range(NT):
                    na.pool_rstd(pool, t)
                pool.memset(maskqk[:], 0.0).then_inc(masks0, 1)
                pool.memset(maskkq[:], 0.0).then_inc(masks0, 1)
                pool.wait_ge(masks0, 2)
                pool.affine_select(out=maskqk[:], in_=maskqk[:], compare_op=ALU.is_ge, fill=MASKED, base=0,
                                   pattern=[[-1, P]], channel_multiplier=1).then_inc(masks, 1)
                pool.affine_select(out=maskkq[:], in_=maskkq[:], compare_op=ALU.is_ge, fill=MASKED, base=0,
                                   pattern=[[1, P]], channel_multiplier=-1).then_inc(masks, 1)
                pool.memset(KTM[:, :, QW:QK], 1.0).then_inc(ktm_done, 1)
                pool.wait_ge(ms_done, 2)
                pool.tensor_scalar(veps[:, 0:NT], ms[:, 0:NT], 1.0 / QR, 1e-6, ALU.mult, ALU.add).then_inc(rs_step, 1)
                pool.tensor_scalar(veps[:, NT:], ms[:, NT:], 1.0 / KVR, 1e-6, ALU.mult, ALU.add).then_inc(rs_step, 1)
                pool.wait_ge(rs_step, 2)
                pool.tensor_tensor(rs[:], veps[:], neghalf[:], ALU.pow).then_inc(rs_done, 1)

            @block.tensor
            def _(pe):
                pe.wait_ge(consts, 3)
                pe.wait_ge(ld_a, 32)
                for c in range(DC):
                    if c >= 2:
                        pe.wait_ge(wa_low, c - 1)
                    pe.transpose(bank[2 + c % 2][:, 0:QR], wa_nat[:, c * P:(c + 1) * P], ident[:])
                    pe.transpose(bank[2 + c % 2][:, QR:NQW], wkva_nat[:, c * P:(c + 1) * P],
                                 ident[0:KVR + ROPE, 0:KVR + ROPE]).then_inc(wa_psum, 1)

                def project(t):
                    pe.wait_ge(*na.low_done(t + 1))
                    if t == 0:
                        pe.wait_ge(wa_low, DC)
                    if t >= 2:
                        pe.wait_ge(proj_out, t - 1)
                    tk = slice(t * P, (t + 1) * P)
                    for c in range(DC):
                        last = three_products(pe, bank[4 + t % 2][:, 0:NQW], (na.high[:, c, tk], na.low[:, c, tk]),
                                              (WaT[0][:, c, :], WaT[1][:, c, :]), c == 0, c == DC - 1)
                    last.then_inc(proj_psum, 1)

                def query_weights(g):
                    if g == 0:
                        pe.wait_ge(wa_low, DC)
                        pe.wait_ge(ld_k, 16)
                    q, at = divmod(HG * g, HP)
                    if at == 0:
                        pe.wait_ge(ld_q[q % 2], 16 * (q // 2 + 1))
                    if g:
                        pe.wait_ge(wq_low, g)
                    for j in range(HG):
                        pe.transpose(bank[2][:, j * ROPE:(j + 1) * ROPE], wqb_nat[q % 2][NOPE:P, at + j, :], ident[NOPE:P, NOPE:P])
                        last = pe.matmul(bank[3][:, j * KVR:(j + 1) * KVR], wqb_nat[q % 2][0:NOPE, at + j, :],
                                         wk_nat[:, HG * g + j, :], start=True, stop=True)
                    last.then_inc(wq_psum, 1)

                def output_weights(g):
                    for h in range(HG * g, HG * g + HG):
                        if h % 2 == 0:
                            pe.wait_ge(ld_wo[h // 2 % 3], 16 * (h // 6 + 1))
                        if h >= 2:
                            pe.wait_ge(*copied(h - 2))
                        for c in range(DC):
                            last = pe.transpose(bank[6 + h % 2][:, c * P:(c + 1) * P],
                                                wo_nat[h // 2 % 3][:, c, h % 2 * VD:(h % 2 + 1) * VD], ident[:])
                        last.then_inc(wot_psum, 1)

                def value_output(g):
                    pe.wait_ge(*copied(HG * g + HG - 2))
                    pe.wait_ge(*copied(HG * g + HG - 1))
                    if g == 0:
                        pe.wait_ge(ld_v_up, 16)
                        pe.wait_ge(proj_out, NT)
                    if g >= 2:
                        pe.wait_ge(wvo_low, g - 1)
                    for j in range(HG):
                        last = pe.matmul(bank[4 + g % 2][32 * j:32 * j + 32, :], wv_nat[:, HG * g + j, :], woT[g % 2][:, j, :],
                                         start=True, stop=True)
                    last.then_inc(wvo_psum, 1)

                for t in range(NT + 2):
                    if t < NT:
                        na.tensor_transpose(pe, t)
                    if t >= 2:
                        project(t - 2)
                    if t >= 4:
                        query_weights(t - 4)
                    if t >= NT:
                        output_weights(t - NT)
                query_weights(NG - 2)
                value_output(0)
                output_weights(2)
                query_weights(NG - 1)
                value_output(1)
                output_weights(3)
                pe.wait_ge(qn_done, 2)
                for i in range(2):
                    for k in range(4):
                        last = pe.transpose(bank[i][:, k * P:(k + 1) * P], QAn[i][:, k, :], ident[:])
                    last.then_inc(qn_psum, 1)
                pe.wait_ge(ktm_done, 3)
                pe.wait_ge(wq_low, NG)
                for i in range(2):
                    for k in range(4):
                        last = pe.transpose(bank[2 + i][0:QK, k * P:(k + 1) * P], KTM[:, 4 * i + k, :], ident[:])
                    last.then_inc(kt_psum, 1)
                value_output(2)
                for g in range(4, NG):
                    output_weights(g)
                    value_output(g - 1)
                value_output(NG - 1)

            @block.scalar
            def _(act):
                for c in range(DC):
                    act.wait_ge(wa_psum, c + 1)
                    act.copy(WaT[0][:, c, :], bank[2 + c % 2][:, 0:NQW]).then_inc(wa_high, 1)
                def query_weights(g):
                    act.wait_ge(wq_psum, g + 1)
                    dst = WQ[0][:, g * HG * QW:(g + 1) * HG * QW].rearrange("p (j w) -> p j w", j=HG)
                    src = bank[2][:, 0:HG * ROPE].rearrange("p (j w) -> p j w", j=HG)
                    for a in range(2):
                        act.copy(dst[:, :, 32 * a:32 * a + 32], src[:, :, a:ROPE:2])
                    act.copy(dst[:, :, ROPE:QW],
                             bank[3][:, 0:HG * KVR].rearrange("p (j w) -> p j w", j=HG)).then_inc(wq_high, 1)

                def output_weights(g):
                    for h in (h for h in range(HG * g, HG * g + HG) if not by_vector(h)):
                        act.wait_ge(wot_psum, h + 1)
                        if g >= 2:
                            act.wait_ge(wvo_psum, g - 1)
                        act.copy(woT[g % 2][:, h % HG, :], bank[6 + h % 2][:]).then_inc(wot_done, 1)

                def value_output(g):
                    act.wait_ge(wvo_psum, g + 1)
                    act.copy(WVO[0][:, g, :], bank[4 + g % 2][:]).then_inc(wvo_high, 1)

                for t in range(NT):
                    na.scalar_high(act, t)
                    if t >= 4:
                        query_weights(t - 4)
                query_weights(NG - 4)
                output_weights(0)
                query_weights(NG - 3)
                output_weights(1)
                query_weights(NG - 2)
                value_output(0)
                output_weights(2)
                query_weights(NG - 1)
                value_output(1)
                output_weights(3)
                for i in range(2):
                    act.wait_ge(qn_psum, i + 1)
                    act.copy(QnT[0][:, i * 512:(i + 1) * 512], bank[i][:]).then_inc(qn_high, 1)
                for i in range(2):
                    act.wait_ge(kt_psum, i + 1)
                    act.copy(KTh[:, i * 512:(i + 1) * 512], bank[2 + i][0:QK, :]).then_inc(kt_high, 1)
                value_output(2)
                for g in range(4, NG):
                    output_weights(g)
                    value_output(g - 1)
                value_output(NG - 1)

            @block.vector
            def _(dve):
                for c in range(DC):
                    dve.wait_ge(wa_high, c + 1)
                    dve.tensor_tensor(WaT[1][:, c, :], bank[2 + c % 2][:, 0:NQW], WaT[0][:, c, :].bitcast(F32),
                                      ALU.subtract).then_inc(wa_low, 1)
                def query_low(g):
                    dve.wait_ge(wq_high, g + 1)
                    dst, high = (w[:, g * HG * QW:(g + 1) * HG * QW].rearrange("p (j w) -> p j w", j=HG) for w in WQ[::-1])
                    src = bank[2][:, 0:HG * ROPE].rearrange("p (j w) -> p j w", j=HG)
                    for a in range(2):
                        cols = slice(32 * a, 32 * a + 32)
                        dve.tensor_tensor(dst[:, :, cols], src[:, :, a:ROPE:2], high[:, :, cols].bitcast(F32), ALU.subtract)
                    dve.tensor_tensor(dst[:, :, ROPE:QW], bank[3][:, 0:HG * KVR].rearrange("p (j w) -> p j w", j=HG),
                                      high[:, :, ROPE:QW].bitcast(F32), ALU.subtract).then_inc(wq_low, 1)

                def output_weights(g):
                    for h in (h for h in range(HG * g, HG * g + HG) if by_vector(h)):
                        dve.wait_ge(wot_psum, h + 1)
                        dve.wait_ge(wvo_psum, g - 1)
                        dve.tensor_copy(woT[g % 2][:, h % HG, :], bank[6 + h % 2][:]).then_inc(wot_copied, 1)

                def value_output_low(g):
                    dve.wait_ge(wvo_high, g + 1)
                    dve.tensor_tensor(WVO[1][:, g, :], bank[4 + g % 2][:], WVO[0][:, g, :].bitcast(F32),
                                      ALU.subtract).then_inc(wvo_low, 1)

                for t in range(NT + 4):
                    if t < NT:
                        dve.wait_ge(ld_x[t // 2], 16)
                        na.vector_stats(dve, t)
                    if 1 <= t <= NT:
                        na.vector_normalize(dve, t - 1)
                    if 2 <= t <= NT + 1:
                        na.vector_low(dve, t - 2)
                    if t >= 4:
                        dve.wait_ge(proj_psum, t - 3)
                        dve.tensor_copy(QA[:, t - 4, :], bank[4 + t % 2][:, 0:NQW]).then_inc(proj_out, 1)
                    if t >= 6:
                        query_low(t - 6)
                dve.wait_ge(proj_out, NT)
                dve.tensor_tensor(SQ[:], QA[:, :, 0:QR + KVR], QA[:, :, 0:QR + KVR], ALU.mult).then_inc(sq_done, 1)
                dve.wait_ge(sq_done, 1)
                dve.tensor_reduce(ms[:, 0:NT], SQ[:, :, 0:QR], AX_X, ALU.add).then_inc(ms_done, 1)
                dve.tensor_reduce(ms[:, NT:], SQ[:, :, QR:], AX_X, ALU.add).then_inc(ms_done, 1)
                query_low(NG - 2)
                dve.wait_ge(ld_small, 64)
                pairs = QA[:, :, QR + KVR:].rearrange("p t (i a) -> p t a i", a=2)
                for a in range(2):
                    dve.tensor_tensor(RAk[:, :, a, :], pairs[:, :, a, :], cosT[:, :, a, :], ALU.mult)
                    last = dve.tensor_tensor(RBk[:, :, a, :], pairs[:, :, 1 - a, :], sinT[:, :, a, :], ALU.mult)
                last.then_inc(kstep, 1)
                dve.wait_ge(kstep, 1)
                dve.tensor_tensor(KTM[:, :, 0:ROPE], RAk[:].rearrange("p t a i -> p t (a i)"),
                                  RBk[:].rearrange("p t a i -> p t (a i)"), ALU.add).then_inc(ktm_done, 1)
                query_low(NG - 1)
                dve.wait_ge(rs_done, 1)
                dve.tensor_tensor(SQ[:, :, 0:QR], QA[:, :, 0:QR], rs[:, 0:NT].unsqueeze(2).to_broadcast([P, NT, QR]),
                                  ALU.mult).then_inc(kstep, 1)
                dve.tensor_tensor(SQ[:, :, QR:], QA[:, :, QR:QR + KVR],
                                  rs[:, NT:].unsqueeze(2).to_broadcast([P, NT, KVR]), ALU.mult).then_inc(kstep, 1)
                dve.wait_ge(kstep, 3)
                for i in range(2):
                    dve.tensor_tensor(QAn[i], SQ[:, 4 * i:4 * i + 4, 0:QR], qlnw[:].unsqueeze(1).to_broadcast([P, 4, QR]),
                                      ALU.mult).then_inc(qn_done, 1)
                dve.tensor_tensor(KTM[:, :, ROPE:QW], SQ[:, :, QR:], kvlnw[:].unsqueeze(1).to_broadcast([P, NT, KVR]),
                                  ALU.mult).then_inc(ktm_done, 1)
                value_output_low(0)
                for i in range(2):
                    cols = slice(i * 512, (i + 1) * 512)
                    dve.wait_ge(qn_high, i + 1)
                    dve.tensor_tensor(QnT[1][:, cols], bank[i][:], QnT[0][:, cols].bitcast(F32), ALU.subtract).then_inc(qn_low, 1)
                for i in range(2):
                    cols = slice(i * 512, (i + 1) * 512)
                    dve.wait_ge(kt_high, i + 1)
                    dve.tensor_tensor(KTl[:, cols], bank[2 + i][0:QK, :], KTh[:, cols].bitcast(F32),
                                      ALU.subtract).then_inc(kt_low, 1)
                for g in range(4, NG):
                    value_output_low(g - 3)
                    output_weights(g)
                for g in range(NG - 3, NG):
                    value_output_low(g)

        core = ExitStack()
        QT = [(sb_in(core, f"QTh{i}", [QK, HG * P], F32R), sb_in(core, f"QTl{i}", [QK, HG * P], F32R)) for i in range(4)]
        Qtm = [sb_in(core, f"Qtm{i}", [P, HG, QW]) for i in range(2)]
        RA = [sb_in(core, f"RA{i}", [P, HG, 2, 32]) for i in range(2)]
        RB = [sb_in(core, f"RB{i}", [P, HG, 2, 32]) for i in range(2)]
        mx = [sb_in(core, f"mx{i}", [P, HG, 2]) for i in range(2)]
        negm = [sb_in(core, f"negm{i}", [P, HG], BF16) for i in range(2)]
        NPT = 6
        PT = [sb_in(core, f"PT{i}", [P, HG * P]) for i in range(NPT)]
        PS = [sb_in(core, f"PS{i}", [P, HG * P]) for i in range(2)]
        rD = [sb_in(core, f"rD{i}", [P, P]) for i in range(2)]
        core.close()
        att.close()

        q_psum, ra_done, rope_done = sem("q_psum"), sem("ra_done"), sem("rope_done")
        t_psum, qh_done, ql_done = sem("t_psum"), sem("qh_done"), sem("ql_done")
        p1_psum, p1_read, m_done, mrow_psum, mrow_done = (sem("p1_psum"), sem("p1_read"), sem("m_done"),
                                                          sem("mrow_psum"), sem("mrow_done"))
        s_psum, p_done, pv_done, sum_done = sem("s_psum"), sem("p_done"), sem("pv_done"), sem("sum_done")
        den_psum, rd_done, o_done, qlzero = sem("den_psum"), sem("rd_done"), sem("o_done"), sem("qlzero")
        RING, TB, ST, OD = (0, 1), 2, (3, 4, 5), (6, 7)

        ORDER = [7, 0, 6, 1, 5, 2, 4, 3]
        UNITS, PAIR = NG * NT, NT + 1
        STEPS = NT * (NT + 1) // 2
        first_step = [sum(ORDER[i] + 1 for i in range(n)) for n in range(NT)]

        def tile_of(n):
            return ORDER[n % NT]

        def unit_of(x):
            i = max(i for i in range(NT) if first_step[i] <= x % STEPS)
            return x // STEPS * NT + i, x % STEPS - first_step[i]

        def step_of(n, k):
            return n // NT * STEPS + first_step[n % NT] + k

        def sums_through(x):
            n, _ = unit_of(x)
            return x + 1 - (n + 1)

        def max_chunks(n):
            keys = (tile_of(n) + 1) * P
            if keys <= 256:
                return [((0, 1), 0, keys), ((2, 3), 0, keys)]
            return [((j,), a, min(keys, a + 512) - a) for j in range(HG) for a in range(0, keys, 512)]

        CHUNKS = sum(len(max_chunks(i)) for i in range(NT))

        def chunk_of(n, c):
            return n // NT * CHUNKS + sum(len(max_chunks(i)) for i in range(n % NT)) + c

        def side_work(x):
            w, cur = x % PAIR, x // PAIR * 2
            a1, b1, a2 = cur + 2, cur + 3, cur + 4
            nb = len(max_chunks(b1))
            todo = {0: [("project", b1, 0)], 1: [("transpose", a1, 0), ("maxrow", cur + 1, 0)],
                    5: [("chunk", a1, 6), ("chunk", a1, 7), ("transpose", b1, 0)],
                    6: [("maxrow", a1, 0)] + [("chunk", b1, c) for c in range(nb // 2)],
                    7: [("chunk", b1, c) for c in range(nb // 2, nb)], 8: [("project", a2, 0)]}.get(w, [])
            if 2 <= w <= 4:
                todo = [("chunk", a1, 2 * w - 4), ("chunk", a1, 2 * w - 3)]
            for late in (1, 2):
                if x >= late:
                    n, k = unit_of(x - late)
                    if k == tile_of(n) and late == (1 if ORDER[(n + 1) % NT] == 0 else 2):
                        todo = [("denominator", n, 0)] + todo
            return [e for e in todo if e[1] < UNITS]

        PROLOGUE = ([("project", 0, 0), ("project", 1, 0), ("transpose", 0, 0)] + [("chunk", 0, c) for c in range(8)]
                    + [("transpose", 1, 0)] + [("chunk", 1, c) for c in range(2)] + [("maxrow", 0, 0), ("project", 2, 0)])

        ring = [e for e in PROLOGUE if e[0] in ("project", "chunk")]
        for x in range(UNITS // NT * STEPS):
            ring += [e for e in side_work(x) if e[0] in ("project", "chunk")]
        place = {e: i for i, e in enumerate(ring)}

        def groups(eng, prologue, step, epilogue=None):
            prologue()
            for x in range(STEPS):
                step(x, lambda v, per: v)
            with eng.Fori(1, NG - 1) as g:
                for x in range(STEPS, 2 * STEPS):
                    step(x, lambda v, per: g * per + (v - per))
            for x in range((NG - 1) * STEPS, NG * STEPS):
                step(x, lambda v, per: v)
            if epilogue is not None:
                epilogue()

        with nc.Block() as block:
            @block.tensor
            def _(pe):
                def ring_bank(e, at):
                    i = place[e]
                    if i >= 2:
                        kind, n, c = ring[i - 2]
                        if kind == "project":
                            pe.wait_ge(ra_done, at(n + 1, NT))
                        else:
                            pe.wait_ge(p1_read, at(chunk_of(n, c) + 1, CHUNKS))
                    return bank[RING[i % 2]]

                def project(n, at):
                    t = tile_of(n)
                    b = ring_bank(("project", n, 0), at)
                    cols = bass.ds(at(n // NT, 1) * (HG * QW), HG * QW)
                    tk = slice(t * P, (t + 1) * P)
                    three_products(pe, b[:, 0:HG * QW], (QnT[0][:, tk], QnT[1][:, tk]), (WQ[0][:, cols], WQ[1][:, cols]),
                                   True, True).then_inc(q_psum, 1)

                def transpose(n, at):
                    pe.wait_ge(rope_done, at(n + 1, NT))
                    if n >= 1:
                        pe.wait_ge(ql_done, at(n, NT))
                    for j in range(HG):
                        last = pe.transpose(bank[TB][0:QW, j * P:(j + 1) * P], Qtm[n % 2][:, j, :], ident[:])
                    last.then_inc(t_psum, 1)

                def chunk(n, c, at):
                    qh = QT[n % 4][0]
                    heads, a, m = max_chunks(n)[c]
                    b = ring_bank(("chunk", n, c), at)
                    pe.wait_ge(qh_done, at(n + 1, NT))
                    diag = a + m == (tile_of(n) + 1) * P
                    for i, j in enumerate(heads):
                        last = pe.matmul(b[:, i * m:(i + 1) * m], qh[0:QW, j * P:(j + 1) * P], KTh[0:QW, a:a + m],
                                         start=(i == 0), stop=not diag, skip_group_check=True)
                    if diag:
                        for i in range(len(heads)):
                            last = pe.matmul(b[:, (i + 1) * m - P:(i + 1) * m], identb[:], maskqk[:],
                                             start=False, stop=True, skip_group_check=True)
                    last.then_inc(p1_psum, 1)

                def max_row(n, at):
                    pe.wait_ge(m_done, at(n + 1, NT))
                    if n >= 1:
                        pe.wait_ge(mrow_done, at(n, NT))
                    for j in range(HG):
                        last = pe.matmul(bank[TB][QW:QK, j * P:(j + 1) * P], negm[n % 2][:, j:j + 1], identb[:],
                                         start=True, stop=True)
                    last.then_inc(mrow_psum, 1)

                def scores(x, at):
                    n, k = unit_of(x)
                    b = bank[ST[x % 3]]
                    if x >= 3:
                        pe.wait_ge(p_done, at(x - 2, STEPS))
                    if k == 0:
                        pe.wait_ge(mrow_done, at(n + 1, NT))
                        pe.wait_ge(ql_done, at(n + 1, NT))
                    qh, ql = QT[n % 4]
                    kt = slice(k * P, (k + 1) * P)
                    diag = k == tile_of(n)
                    pe.matmul(b[:], KTh[:, kt], qh[:], start=True, stop=False)
                    pe.matmul(b[:], KTh[:, kt], ql[:], start=False, stop=False)
                    last = pe.matmul(b[:], KTl[:, kt], qh[:], start=False, stop=not diag)
                    if diag:
                        last = pe.matmul(b[:].rearrange("p (j n) -> p j n", j=HG), identb[:],
                                         maskkq[:].unsqueeze(1).to_broadcast([P, HG, P]), start=False, stop=True)
                    last.then_inc(s_psum, 1)

                def values(x, at):
                    n, k = unit_of(x)
                    pe.wait_ge(p_done, at(x + 1, STEPS))
                    if k == 0 and n >= 2:
                        pe.wait_ge(o_done, at(n - 1, NT))
                    for j in range(HG):
                        last = pe.matmul(bank[OD[n % 2]][32 * j:32 * j + 32, 0:P], KTM[:, k, ROPE:QW],
                                         PT[x % NPT][:, j * P:(j + 1) * P], start=(k == 0), stop=(k == tile_of(n)),
                                         skip_group_check=True)
                    last.then_inc(pv_done, 1)

                def denominator(n, at):
                    t = tile_of(n)
                    last_step = step_of(n, t)
                    if t:
                        pe.wait_ge(sum_done, at(sums_through(last_step), STEPS - NT))
                    src = PS[n % 2] if t else PT[last_step % NPT]
                    for j in range(HG):
                        last = pe.matmul(bank[OD[n % 2]][32 * j:32 * j + 32, P:2 * P], ones[:], src[:, j * P:(j + 1) * P],
                                         start=False, stop=True, skip_group_check=True)
                    last.then_inc(den_psum, 1)

                def side(kind, n, c, at):
                    if kind == "project":
                        project(n, at)
                    elif kind == "transpose":
                        transpose(n, at)
                    elif kind == "chunk":
                        chunk(n, c, at)
                    elif kind == "maxrow":
                        max_row(n, at)
                    else:
                        denominator(n, at)

                def prologue():
                    pe.wait_ge(qlzero, 4)
                    for e in PROLOGUE:
                        side(*e, lambda v, per: v)
                    for x in range(2):
                        scores(x, lambda v, per: v)

                def step(x, at):
                    w = x % PAIR
                    if w == 7:
                        for e in side_work(x):
                            side(*e, at)
                    if x + 2 < NG * STEPS:
                        scores(x + 2, at)
                    if 0 < w < 7:
                        for e in side_work(x):
                            side(*e, at)
                    values(x, at)
                    if w in (0, 8):
                        for e in side_work(x):
                            side(*e, at)

                groups(pe, prologue, step, lambda: denominator(UNITS - 1, lambda v, per: v))

            @block.vector
            def _(dve):
                def rope(n, at):
                    t = tile_of(n)
                    q = bank[RING[place[("project", n, 0)] % 2]][:, 0:HG * QW].rearrange("p (j w) -> p j w", j=HG)
                    rot = q[:, :, 0:ROPE].rearrange("p j (a i) -> p j a i", a=2)
                    dve.wait_ge(q_psum, at(n + 1, NT))
                    if n >= 2:
                        dve.wait_ge(rope_done, at(n - 1, NT))
                        dve.wait_ge(t_psum, at(n - 1, NT))
                    dve.tensor_copy(Qtm[n % 2][:, :, ROPE:QW], q[:, :, ROPE:QW])
                    dve.tensor_tensor(RA[n % 2][:], rot, cosT[:, t].unsqueeze(1).to_broadcast([P, HG, 2, 32]), ALU.mult)
                    dve.tensor_tensor(RB[n % 2][:], rot[:, :, ::-1, :],
                                      sinT[:, t].unsqueeze(1).to_broadcast([P, HG, 2, 32]), ALU.mult).then_inc(ra_done, 1)

                def low_part(n, at):
                    qh, ql = QT[n % 4]
                    dve.wait_ge(qh_done, at(n + 1, NT))
                    dve.tensor_tensor(ql[0:QW, :], bank[TB][0:QW, :], qh[0:QW, :].bitcast(F32),
                                      ALU.subtract).then_inc(ql_done, 1)

                def maxima(n, c, at):
                    m, chunks = mx[n % 2], max_chunks(n)
                    heads, a, w = chunks[c]
                    dve.wait_ge(p1_psum, at(chunk_of(n, c) + 1, CHUNKS))
                    dve.tensor_reduce(m[:, heads[0]:heads[-1] + 1, a // 512:a // 512 + 1],
                                      bank[RING[place[("chunk", n, c)] % 2]][:, 0:len(heads) * w].rearrange(
                                          "p (s n) -> p s n", n=w), AX_X, ALU.max).then_inc(p1_read, 1)
                    if c == len(chunks) - 1:
                        dve.wait_ge(p1_read, at(chunk_of(n, c) + 1, CHUNKS))
                        if n >= 2:
                            dve.wait_ge(mrow_psum, at(n - 1, NT))
                        dve.tensor_reduce(negm[n % 2][:], m[:, :, 0:a // 512 + 1], AX_X, ALU.max,
                                          negate=True).then_inc(m_done, 1)

                def normalize(n, at):
                    od, t = bank[OD[n % 2]], tile_of(n)
                    dve.wait_ge(den_psum, at(n + 1, NT))
                    dve.reciprocal(rD[n % 2][:], od[:, P:2 * P]).then_inc(rd_done, 1)
                    dve.wait_ge(rd_done, at(n + 1, NT))
                    dve.tensor_tensor(OT[:, bass.ds(at(n // NT, 1) * S + t * P, P)], od[:, 0:P], rD[n % 2][:],
                                      ALU.mult).then_inc(o_done, 1)

                def side(kind, n, c, at):
                    if kind == "project":
                        rope(n, at)
                    elif kind == "transpose":
                        low_part(n, at)
                    elif kind == "chunk":
                        maxima(n, c, at)
                    elif kind == "denominator":
                        normalize(n, at)

                def prologue():
                    for i in range(4):
                        dve.memset(QT[i][1][:].bitcast(F32), 0.0).then_inc(qlzero, 1)
                    dve.wait_ge(qlzero, 4)
                    for e in PROLOGUE:
                        side(*e, lambda v, per: v)

                def step(x, at):
                    for e in side_work(x):
                        side(*e, at)

                groups(dve, prologue, step, lambda: normalize(UNITS - 1, lambda v, per: v))

            @block.gpsimd
            def _(pool):
                def rope_sum(n, at):
                    pool.wait_ge(ra_done, at(n + 1, NT))
                    pool.tensor_tensor(Qtm[n % 2][:, :, 0:ROPE], RA[n % 2][:].rearrange("p j a i -> p j (a i)"),
                                       RB[n % 2][:].rearrange("p j a i -> p j (a i)"), ALU.add).then_inc(rope_done, 1)

                def prologue():
                    for kind, n, _ in PROLOGUE:
                        if kind == "project":
                            rope_sum(n, lambda v, per: v)

                def add(x, at):
                    n, k = unit_of(x)
                    pool.wait_ge(p_done, at(x + 1, STEPS))
                    if k == 1 and n >= 2:
                        pool.wait_ge(den_psum, at(n - 1, NT))
                    if k >= 2:
                        pool.wait_ge(sum_done, at(sums_through(x - 1), STEPS - NT))
                    pool.tensor_tensor(PS[n % 2][:], PT[(x - 1) % NPT][:] if k == 1 else PS[n % 2][:], PT[x % NPT][:],
                                       ALU.add).then_inc(sum_done, 1)

                def step(x, at):
                    if unit_of(x)[1]:
                        add(x, at)
                    for kind, n, _ in side_work(x):
                        if kind == "project":
                            rope_sum(n, at)

                groups(pool, prologue, step)

            @block.scalar
            def _(act):
                def high_part(n, at):
                    act.wait_ge(t_psum, at(n + 1, NT))
                    act.copy(QT[n % 4][0][0:QW, :], bank[TB][0:QW, :]).then_inc(qh_done, 1)

                def copy_max_row(n, at):
                    act.wait_ge(mrow_psum, at(n + 1, NT))
                    act.copy(QT[n % 4][0][QW:QK, :], bank[TB][QW:QK, :]).then_inc(mrow_done, 1)

                def probabilities(x, at):
                    act.wait_ge(s_psum, at(x + 1, STEPS))
                    if x >= NPT:
                        n, k = unit_of(x - NPT)
                        act.wait_ge(pv_done, at(x - NPT + 1, STEPS))
                        y = x - NPT + 1 if unit_of(x - NPT + 1)[1] == 1 else x - NPT
                        act.wait_ge(sum_done, at(sums_through(y), STEPS - NT))
                        if tile_of(n) == 0:
                            act.wait_ge(den_psum, at(n + 1, NT))
                    act.activation(PT[x % NPT][:], bank[ST[x % 3]][:], ACT.Exp, scale=SOFTMAX_SCALE).then_inc(p_done, 1)

                def side(kind, n, at):
                    if kind == "transpose":
                        high_part(n, at)
                    elif kind == "maxrow":
                        copy_max_row(n, at)

                def prologue():
                    for kind, n, _ in PROLOGUE:
                        side(kind, n, lambda v, per: v)
                    for x in range(2):
                        probabilities(x, lambda v, per: v)

                def step(x, at):
                    if x + 2 < NG * STEPS:
                        probabilities(x + 2, at)
                    for kind, n, _ in side_work(x):
                        side(kind, n, at)

                groups(act, prologue, step)

        class FeedForward:
            PIECES = ((0, 2), (2, 5), (5, 8), (8, FT))

            def __init__(self, mem, tag, head_banks):
                self.head_banks = head_banks

                def weights(s):
                    return [sb_in(mem, f"WdT{s}{i}_{tag}", [P, DM], F32R) for i in "hl"]

                def natural(s):
                    return ([sb_in(mem, f"nat{w}{s}_{tag}", [P, 3, DM]) for w in "gu"]
                            + [sb_in(mem, f"natd{s}_{tag}", [P, DC, 3 * P])])

                self.HT = [[sb_in(mem, f"HT{s}{i}_{tag}", [P, S], F32R) for i in "hl"] for s in range(4)]
                self.SG = [sb_in(mem, f"SG{i}_{tag}", [P, CH]) for i in range(2)]
                self.H = [sb_in(mem, f"H{i}_{tag}", [P, CH]) for i in range(2)]
                nat1 = natural(1)
                later = [weights(s) for s in range(1, 5)]
                self.Wd = [weights(0)] + later
                self.Wg, self.Wu = ([[sb_in(mem, f"{w}{s}{i}_{tag}", [P, DC, P], F32R) for i in "hl"] for s in range(2)]
                                    for w in ("WgT", "WuT"))
                self.nat = [natural(0), nat1]
                self.w_psum, self.w_high, self.w_low = (again(n, 3 * FT) for n in ("w_psum", "w_high", "w_low"))
                self.loads = [(3 if b < FT else 5) * 16 for _, b in self.PIECES]
                self.ld = [again(f"ffn_ld{p}", n) for p, n in enumerate(self.loads)]

            def load(self, sp, p):
                a, b = self.PIECES[p]
                full = min(b, FF // P)
                for i, w in enumerate((w_gate, w_up)):
                    dst = self.nat[p % 2][i]
                    sp.dma_start(dst[:, 0:full - a, :], w[a * P:full * P].rearrange("(f p) d -> p f d", p=P)).then_inc(self.ld[p].sem, 16)
                    if b == FT:
                        sp.dma_start(dst[0:FF - full * P, full - a, :], w[full * P:FF]).then_inc(self.ld[p].sem, 16)
                cols = slice(a * P, min(b * P, FF))
                sp.dma_start(self.nat[p % 2][2][:, :, 0:cols.stop - cols.start],
                             w_down.rearrange("(c p) f -> p c f", p=P)[:, :, cols]).then_inc(self.ld[p].sem, 16)

            def weight(self, f, m, hl):
                r, b = min(P, FF - f * P), bank[(3 * f + m) % 2 if f else self.head_banks[m]]
                if m == 2:
                    return self.Wd[f % 5][hl][0:r, :], b[0:r, :]
                return ((self.Wg, self.Wu)[m][f % 2][hl][:, :, 0:r],
                        b[:].rearrange("p (c n) -> p c n", c=DC)[:, :, 0:r])

            def transpose(self, pe, f, m):
                i, r = 3 * f + m, min(P, FF - f * P)
                p = next(p for p, (_, b) in enumerate(self.PIECES) if f < b)
                b, nat, k = bank[i % 2 if f else self.head_banks[m]], self.nat[p % 2], f - self.PIECES[p][0]
                if k == 0 and m == 0:
                    pe.wait_ge(*self.ld[p](self.loads[p]))
                if i >= 5 or (i == 2 and self.head_banks[0] == self.head_banks[2]):
                    pe.wait_ge(*self.w_low(i - 1))
                for c in range(DC):
                    if m < 2:
                        last = pe.transpose(b[:, c * P:c * P + r], nat[m][0:r, k, c * P:(c + 1) * P], ident[0:r, 0:r])
                    else:
                        last = pe.transpose(b[0:r, c * P:(c + 1) * P], nat[2][:, c, k * P:k * P + r], ident[:])
                last.then_inc(self.w_psum.sem, 1)

            def high(self, act, f, m):
                act.wait_ge(*self.w_psum(3 * f + m + 1))
                dst, src = self.weight(f, m, 0)
                act.copy(dst, src).then_inc(self.w_high.sem, 1)

            def low(self, dve, f, m):
                dve.wait_ge(*self.w_high(3 * f + m + 1))
                dst, src = self.weight(f, m, 1)
                dve.tensor_tensor(dst, src, self.weight(f, m, 0)[0].bitcast(F32), ALU.subtract).then_inc(self.w_low.sem, 1)

            def head(self, step, engine):
                for m in range(3):
                    step(engine, 0, m)

            def run(self, norm, load_next=None):
                PIECES, SG, H, Wg, Wu, Wd, HT = self.PIECES, self.SG, self.H, self.Wg, self.Wu, self.Wd, self.HT
                rows = [min(P, FF - f * P) for f in range(FT)]
                piece = [next(p for p, (a, b) in enumerate(PIECES) if f < b) for f in range(FT)]
                w_psum, w_low = self.w_psum, self.w_low
                gate_psum, up_psum, silu_done, h_done, h_high, h_low = (
                    again(n, NCH * FT) for n in ("gate_psum", "up_psum", "silu_done", "h_done", "h_high", "h_low"))
                down_psum, down_added = (again(n, len(PIECES) * NT) for n in ("down_psum", "down_added"))

                def down_after(f):
                    return piece[f - 1] if f and piece[f - 1] != piece[f] else None

                with nc.Block() as block:
                    @block.sync
                    def _(sp):
                        for p in range(1, len(PIECES)):
                            if p >= 2:
                                sp.wait_ge(*w_psum(3 * PIECES[p - 2][1]))
                            self.load(sp, p)
                        if load_next is not None:
                            sp.wait_ge(*w_psum(3 * PIECES[-2][1]))
                            load_next(sp)
                        if norm is None:
                            rows_out = out[0].rearrange("(t p) d -> p t d", p=P)
                            for t in range(0, NT, 2):
                                sp.wait_ge(*down_added((len(PIECES) - 1) * NT + t + 2))
                                sp.dma_start(rows_out[:, t:t + 2, :], X[:, t:t + 2, :]).then_inc(stored, 16)
                            sp.wait_ge(stored, 16 * NT // 2)

                    @block.tensor
                    def _(pe):
                        def transpose(f, m):
                            if f < FT:
                                self.transpose(pe, f, m)

                        def product(f, ch, W, m, out, full):
                            r = rows[f]
                            tk = slice(ch * CH, (ch + 1) * CH)
                            for c in range(DC):
                                last = three_products(pe, out[0:r, :], [w[:, c, 0:r] for w in W[f % 2]],
                                                      [x[:, c, tk] for x in XnT], c == 0, c == DC - 1)
                            last.then_inc(full.sem, 1)

                        def down(p, t):
                            a, b = PIECES[p]
                            i = p * NT + t
                            if i >= 2:
                                pe.wait_ge(*down_added(i - 1))
                            for f in range(a, b):
                                last = three_products(pe, bank[6 + i % 2][:], [h[0:rows[f], t * P:(t + 1) * P] for h in HT[f % 4]],
                                                      [w[0:rows[f], :] for w in Wd[f % 5]], f == a, f == b - 1)
                            last.then_inc(down_psum.sem, 1)

                        for f in range(FT):
                            for ch in range(NCH):
                                n = NCH * f + ch
                                if ch == 0:
                                    transpose(f + 1, 0)
                                    pe.wait_ge(*w_low(3 * f + 2))
                                if n >= 2:
                                    pe.wait_ge(*silu_done(n - 1))
                                product(f, ch, Wg, 0, bank[2 + n % 2], gate_psum)
                                transpose(f + 1, 1 + ch)
                                if n >= 2:
                                    pe.wait_ge(*h_done(n - 1))
                                product(f, ch, Wu, 1, bank[4 + n % 2], up_psum)
                            p = down_after(f)
                            if p is not None:
                                pe.wait_ge(*w_low(3 * PIECES[p][1]))
                                pe.wait_ge(*h_low(NCH * PIECES[p][1]))
                                for t in range(NT):
                                    down(p, t)
                        pe.wait_ge(*w_low(3 * FT))
                        for t in range(NT):
                            if t % TPC == 0:
                                pe.wait_ge(*h_low(NCH * (FT - 1) + t // TPC + 1))
                            down(len(PIECES) - 1, t)
                            if norm is not None and t >= 2:
                                norm.tensor_transpose(pe, t - 2)
                        if norm is not None:
                            norm.tensor_transpose(pe, NT - 2)
                            norm.tensor_transpose(pe, NT - 1)

                    @block.scalar
                    def _(act):
                        def high(f, m):
                            if f < FT:
                                self.high(act, f, m)

                        def silu(n):
                            r = rows[n // NCH]
                            act.wait_ge(*gate_psum(n + 1))
                            if n >= 2:
                                act.wait_ge(*h_done(n - 1))
                            act.activation(SG[n % 2][0:r, :], bank[2 + n % 2][0:r, :], ACT.Silu).then_inc(silu_done.sem, 1)

                        def hidden_high(n):
                            f, ch = divmod(n, NCH)
                            act.wait_ge(*h_done(n + 1))
                            act.copy(HT[f % 4][0][0:rows[f], ch * CH:(ch + 1) * CH], H[n % 2][0:rows[f], :]).then_inc(h_high.sem, 1)

                        for f in range(FT):
                            high(f + 1, 0)
                            if f:
                                hidden_high(2 * f - 1)
                            silu(2 * f)
                            high(f + 1, 1)
                            hidden_high(2 * f)
                            silu(2 * f + 1)
                            high(f + 1, 2)
                        hidden_high(2 * FT - 1)
                        if norm is not None:
                            for t in range(NT):
                                norm.scalar_high(act, t)

                    @block.gpsimd
                    def _(pool):
                        for n in range(NCH * FT):
                            f, ch = divmod(n, NCH)
                            pool.wait_ge(*h_high(n + 1))
                            cols = slice(ch * CH, (ch + 1) * CH)
                            pool.tensor_tensor(HT[f % 4][1][0:rows[f], cols], H[n % 2][0:rows[f], :],
                                               HT[f % 4][0][0:rows[f], cols].bitcast(F32), ALU.subtract).then_inc(h_low.sem, 1)
                        if norm is not None:
                            for t in range(NT):
                                norm.pool_rstd(pool, t)

                    @block.vector
                    def _(dve):
                        def low(f, m):
                            if f < FT:
                                self.low(dve, f, m)

                        def hidden(n):
                            r = rows[n // NCH]
                            dve.wait_ge(*up_psum(n + 1))
                            dve.wait_ge(*silu_done(n + 1))
                            if n >= 2:
                                dve.wait_ge(*h_low(n - 1))
                            dve.tensor_tensor(H[n % 2][0:r, :], bank[4 + n % 2][0:r, :], SG[n % 2][0:r, :],
                                              ALU.mult).then_inc(h_done.sem, 1)

                        def add(p, t):
                            i = p * NT + t
                            dve.wait_ge(*down_psum(i + 1))
                            if p:
                                dve.wait_ge(*down_added(i - NT + 1))
                            dve.tensor_tensor(X[:, t, :], bank[6 + i % 2][:], X[:, t, :], ALU.add).then_inc(down_added.sem, 1)

                        for f in range(FT):
                            low(f + 1, 0)
                            low(f + 1, 1)
                            hidden(2 * f)
                            low(f + 1, 2)
                            hidden(2 * f + 1)
                            p = down_after(f)
                            if p is not None:
                                for t in range(NT):
                                    add(p, t)
                        p = len(PIECES) - 1
                        for t in range(NT if norm is None else NT + 3):
                            if t < NT:
                                add(p, t)
                                if norm is not None:
                                    dve.wait_ge(*down_added(p * NT + t + 1))
                            if norm is not None:
                                norm.vector_step(dve, t)

        ot = OT[:].rearrange("p (g s) -> p g s", g=NG)
        ffn1, split = ExitStack(), ExitStack()
        f1 = FeedForward(ffn1, "f1", (4, 5, 6))
        OTs = [[sb_in(split, f"OTs{i}{k}", [P, NG, P], F32R) for i in "hl"] for k in range(2)]
        split.close()
        ffn1.close()
        nf1 = Norm()
        ot_high, ot_low, attn_psum, attn_added = sem("ot_high"), sem("ot_low"), sem("attn_psum"), sem("attn_added")
        with nc.Block() as block:
            @block.sync
            def _(sp):
                f1.load(sp, 0)

            @block.scalar
            def _(act):
                for t in range(NT + 3):
                    if t < NT:
                        if t >= 2:
                            act.wait_ge(attn_psum, t - 1)
                        act.copy(OTs[t % 2][0][:], ot[:, :, t * P:(t + 1) * P]).then_inc(ot_high, 1)
                    if t >= 3:
                        nf1.scalar_high(act, t - 3)
                    if t == 4:
                        f1.head(f1.high, act)

            @block.tensor
            def _(pe):
                for t in range(NT):
                    pe.wait_ge(ot_low, t + 1)
                    if t >= 2:
                        pe.wait_ge(attn_added, t - 1)
                    for g in range(NG):
                        last = three_products(pe, bank[2 + t % 2][:], [o[:, g, :] for o in OTs[t % 2]],
                                              [w[:, g, :] for w in WVO], g == 0, g == NG - 1)
                    last.then_inc(attn_psum, 1)
                    if t == 3:
                        f1.head(f1.transpose, pe)
                    if t >= 2:
                        nf1.tensor_transpose(pe, t - 2)
                nf1.tensor_transpose(pe, NT - 2)
                nf1.tensor_transpose(pe, NT - 1)

            @block.gpsimd
            def _(pool):
                for t in range(NT):
                    nf1.pool_rstd(pool, t)

            @block.vector
            def _(dve):
                def low(t):
                    dve.wait_ge(ot_high, t + 1)
                    dve.tensor_tensor(OTs[t % 2][1][:], ot[:, :, t * P:(t + 1) * P], OTs[t % 2][0][:].bitcast(F32),
                                      ALU.subtract).then_inc(ot_low, 1)

                low(0)
                low(1)
                for t in range(NT + 3):
                    if t < NT:
                        dve.wait_ge(attn_psum, t + 1)
                        dve.tensor_tensor(X[:, t, :], bank[2 + t % 2][:], X[:, t, :], ALU.add).then_inc(attn_added, 1)
                        dve.wait_ge(attn_added, t + 1)
                    nf1.vector_step(dve, t)
                    if t + 2 < NT:
                        low(t + 2)
                    if t == 4:
                        f1.head(f1.low, dve)


        ssm = ExitStack()
        XS = sb_in(ssm, "XS", [P, DJ, S])
        WoutT = sb_in(ssm, "WoutT", [P, DJ, DM])
        G = sb_in(ssm, "G", [P, DJ, S])
        WxT = sb_in(ssm, "WxT", [P, DJ, RK + 2 * NS])
        WdtT = sb_in(ssm, "WdtT", [RK, DI])
        convw = sb_in(ssm, "convw", [P, DJ, KC])
        convb = sb_in(ssm, "convb", [P, DJ])
        bdt = sb_in(ssm, "bdt", [P, DJ])
        dsk = sb_in(ssm, "dsk", [P, DJ])
        Aneg = sb_in(ssm, "Aneg", [P, DJ, NS])
        state = sb_in(ssm, "state", [P, DJ, NS])
        inp = ExitStack()
        WinT = [[[sb_in(inp, f"WinT{w}{k}{i}", [P, DC, P], F32R) for i in "hl"] for k in range(2)] for w in "xg"]
        win_nat = [sb_in(inp, f"win_nat{i}", [P, 2, DM]) for i in range(3)]
        wout_nat = [sb_in(inp, f"wout_nat{i}", [P, DC, P]) for i in range(3)]
        XP = [sb_in(inp, f"XP{i}", [P, KC - 1 + S]) for i in range(2)]
        acc = [sb_in(inp, f"acc{i}", [P, S]) for i in range(2)]
        wx_nat = sb_in(inp, "wx_nat", [RK + 2 * NS, DI])
        wdt_nat = sb_in(inp, "wdt_nat", [P, DJ, RK])
        inp.close()

        ld_in = [sem(f"ld_in{i}") for i in range(DJ)]
        ld_s, ld_v = sem("ld_s"), sem("ld_v")
        in_psum, in_high, in_low, small_psum, small_done = (sem("in_psum"), sem("in_high"), sem("in_low"),
                                                            sem("small_psum"), sem("small_done"))
        xp_psum, xp_done, conv_step, conv_done, xs_done = (sem("xp_psum"), sem("xp_done"), sem("conv_step"),
                                                           sem("conv_done"), sem("xs_done"))
        g_psum, g_done, sx_psum = sem("g_psum"), sem("g_done"), sem("sx_psum")
        a_clamped, a_step, zero_done = sem("a_clamped"), sem("a_step"), sem("zero_done")
        W3 = RK + 2 * NS
        def load_in(sp, j):
            sp.dma_start(win_nat[j % 3][:], w_in.rearrange("(w j p) d -> j p w d", p=P, w=2)[j]).then_inc(ld_in[j], 16)
            sp.dma_start(wout_nat[j % 3][:], w_out.rearrange("(c p) (j q) -> j p c q", p=P, q=P)[j]).then_inc(ld_in[j], 16)

        def load_in_first(sp):
            for j in range(3):
                load_in(sp, j)

        ns = Norm()
        f1.run(ns, load_in_first)

        SMALL = [DJ, 0, 1, 2, 3, 4, 5, 6, DJ + 1, 7, DJ + 2]
        with nc.Block() as block:
            @block.sync
            def _(sp):
                sp.dma_start(wx_nat[:], w_x).then_inc(ld_s, 16)
                sp.dma_start(wdt_nat[:], w_dt.rearrange("(j p) r -> p j r", p=P)).then_inc(ld_s, 16)
                sp.dma_start(convw[:], conv_w.rearrange("(j p) k -> p j k", p=P)).then_inc(ld_v, 16)
                sp.dma_start(Aneg[:], a_log.rearrange("(j p) n -> p j n", p=P)).then_inc(ld_v, 16)
                with nc.allow_non_contiguous_dma(reason="one value to a partition"):
                    for dst, src in ((convb, conv_b), (bdt, b_dt), (dsk, d_skip)):
                        sp.dma_start(dst[:], src.rearrange("(j p) -> p j", p=P)).then_inc(ld_v, 16)
                for j in range(3, DJ):
                    sp.wait_ge(in_psum, 2 * (j - 2))
                    sp.wait_ge(small_psum, SMALL.index(j - 3) + 1)
                    load_in(sp, j)

            @block.tensor
            def _(pe):
                def transpose(j, w):
                    if j >= DJ:
                        return
                    i = 2 * j + w
                    pe.wait_ge(ld_in[j], 32)
                    if i >= 2:
                        pe.wait_ge(in_low, i - 1)
                    for c in range(DC):
                        last = pe.transpose(bank[i % 2][:, c * P:(c + 1) * P], win_nat[j % 3][:, w, c * P:(c + 1) * P], ident[:])
                    last.then_inc(in_psum, 1)

                def small(i):
                    k = SMALL.index(i)
                    if k:
                        pe.wait_ge(small_done, k)
                    b = bank[6]
                    if i == DJ:
                        pe.wait_ge(ld_s, 32)
                        for j in range(DJ):
                            last = pe.transpose(b[:, j * W3:(j + 1) * W3], wx_nat[:, j * P:(j + 1) * P], ident[0:W3, 0:W3])
                    elif i < DJ:
                        for c in range(DC):
                            last = pe.transpose(b[:, c * P:(c + 1) * P], wout_nat[i % 3][:, c, :], ident[:])
                    else:
                        for k in range(4):
                            last = pe.transpose(b[0:RK, k * P:(k + 1) * P], wdt_nat[:, 4 * (i - DJ - 1) + k, :], ident[:])
                    last.then_inc(small_psum, 1)

                def mix(j):
                    pe.wait_ge(xs_done, j + 1)
                    if j == 0:
                        pe.wait_ge(small_done, 1)
                    for t in range(NT):
                        last = pe.matmul(bank[7][:, t * W3:(t + 1) * W3], XS[:, j, t * P:(t + 1) * P], WxT[:, j, :],
                                         start=(j == 0 and t == 0), stop=(j == DJ - 1), skip_group_check=True)
                    if j == DJ - 1:
                        last.then_inc(sx_psum, 1)

                def product(j, ch, w):
                    n = NCH * j + ch
                    if n >= 2:
                        pe.wait_ge((xp_done, g_done)[w], n - 1)
                    for c in range(DC):
                        last = three_products(pe, bank[2 + 2 * w + n % 2][:], [m[:, c, :] for m in WinT[w][j % 2]],
                                              [m[:, c, ch * CH:(ch + 1) * CH] for m in XnT], c == 0, c == DC - 1)
                    last.then_inc((xp_psum, g_psum)[w], 1)

                transpose(0, 0)
                transpose(0, 1)
                for j in range(DJ):
                    transpose(j + 1, 0)
                    pe.wait_ge(in_low, 2 * j + 2)
                    product(j, 0, 0)
                    transpose(j + 1, 1)
                    product(j, 1, 0)
                    if j == 0:
                        small(DJ)
                    product(j, 0, 1)
                    small(j)
                    product(j, 1, 1)
                    if j >= DJ - 2:
                        small(j + 3)
                    if j >= 2:
                        mix(j - 2)
                mix(DJ - 2)
                mix(DJ - 1)

            @block.scalar
            def _(act):
                def high(j, w):
                    if j < DJ:
                        i = 2 * j + w
                        act.wait_ge(in_psum, i + 1)
                        act.copy(WinT[w][j % 2][0][:], bank[i % 2][:].rearrange("p (c n) -> p c n", c=DC)).then_inc(in_high, 1)

                def small(i):
                    act.wait_ge(small_psum, SMALL.index(i) + 1)
                    b = bank[6]
                    if i < DJ:
                        act.copy(WoutT[:, i, :], b[:]).then_inc(small_done, 1)
                    elif i == DJ:
                        act.copy(WxT[:].rearrange("p j w -> p (j w)"), b[:]).then_inc(small_done, 1)
                    else:
                        m = i - DJ - 1
                        act.copy(WdtT[:, m * 512:(m + 1) * 512], b[0:RK, :]).then_inc(small_done, 1)

                def conv_silu(j):
                    act.wait_ge(conv_done, j + 1)
                    act.activation(XS[:, j, :], acc[j % 2][:], ACT.Silu, bias=convb[:, j:j + 1]).then_inc(xs_done, 1)

                high(0, 0)
                high(0, 1)
                act.wait_ge(a_clamped, 1)
                act.activation(Aneg[:], Aneg[:], ACT.Exp).then_inc(a_step, 1)
                act.wait_ge(a_step, 1)
                act.mul(Aneg[:], Aneg[:], -1.0).then_inc(a_step, 1)
                for j in range(DJ):
                    high(j + 1, 0)
                    if j >= 2:
                        act.wait_ge(conv_done, j - 1)
                    for ch in range(NCH):
                        n = NCH * j + ch
                        act.wait_ge(xp_psum, n + 1)
                        act.copy(XP[j % 2][:, KC - 1 + ch * CH:KC - 1 + (ch + 1) * CH], bank[2 + n % 2][:]).then_inc(xp_done, 1)
                        if ch == 0:
                            high(j + 1, 1)
                    if j:
                        conv_silu(j - 1)
                    if j == 0:
                        small(DJ)
                    small(j)
                    for ch in range(NCH):
                        n = NCH * j + ch
                        act.wait_ge(g_psum, n + 1)
                        act.activation(G[:, j, ch * CH:(ch + 1) * CH], bank[4 + n % 2][:], ACT.Silu).then_inc(g_done, 1)
                    if j >= DJ - 2:
                        small(j + 3)
                conv_silu(DJ - 1)

            @block.gpsimd
            def _(pool):
                for i in range(2):
                    pool.memset(XP[i][:, 0:KC - 1], 0.0).then_inc(zero_done, 1)
                pool.memset(state[:], 0.0).then_inc(zero_done, 1)

            @block.vector
            def _(dve):
                def low(j, w):
                    if j < DJ:
                        i = 2 * j + w
                        high, low_ = WinT[w][j % 2]
                        dve.wait_ge(in_high, i + 1)
                        dve.tensor_tensor(low_[:], bank[i % 2][:].rearrange("p (c n) -> p c n", c=DC), high[:].bitcast(F32),
                                          ALU.subtract).then_inc(in_low, 1)

                low(0, 0)
                low(0, 1)
                dve.wait_ge(ld_v, 80)
                dve.tensor_scalar(Aneg[:], Aneg[:], A_LOG_MAX, None, ALU.min).then_inc(a_clamped, 1)
                dve.wait_ge(zero_done, 2)
                for j in range(DJ):
                    low(j + 1, 0)
                    low(j + 1, 1)
                    dve.wait_ge(xp_done, NCH * (j + 1))
                    if j >= 2:
                        dve.wait_ge(xs_done, j - 1)
                    a = acc[j % 2][:]
                    dve.tensor_scalar(a, XP[j % 2][:, KC - 1:], convw[:, j, KC - 1:KC], None, ALU.mult).then_inc(conv_step, 1)
                    for k in range(KC - 1):
                        dve.wait_ge(conv_step, 3 * j + k + 1)
                        dve.scalar_tensor_tensor(a, XP[j % 2][:, k:k + S], convw[:, j, k:k + 1], a, ALU.mult,
                                                 ALU.add).then_inc(conv_done if k == KC - 2 else conv_step, 1)

        mem = ExitStack()
        BC = sb_in(mem, "BC", [P, 2 * NS, CH])
        ss = sb_in(mem, "ss", [2 * W3, CH], F32R)
        pick = sb_in(mem, "pick", [2 * W3, W3], F32R)
        diag = [WxT[:].rearrange("p j w -> p (j w)")[:, i * P:(i + 1) * P] for i in range(2)]
        m3 = sb_in(mem, "m3", [P, 3, NT])
        r3 = sb_in(mem, "r3", [P, 3, NT])
        v3 = sb_in(mem, "v3", [P, 3, NT])
        nh3 = sb_in(mem, "nh3", [P, 3, NT])
        mem.close()
        SS, SSq = (x_[:].rearrange("p (k w) -> p k w", k=NT) for x_ in dA[0:2])
        twice = BC[:, 2 * NS - 2:, :].rearrange("p a n -> p (a n)").rearrange("p (t a w) -> p t a w", t=NT, a=2)
        E, R = (x_[:] for x_ in Xn)
        GROUPS = ((0, RK), (RK, RK + NS), (RK + NS, W3))
        sx_step, sx_ms, sx_eps, sx_r, sx_n = (sem(n) for n in ("sx_step", "sx_ms", "sx_eps", "sx_r", "sx_n"))
        st_psum, st_done, ss_high, ss_low, nh3_set, pick_done = (sem(n) for n in ("st_psum", "st_done", "ss_high", "ss_low",
                                                                                  "nh3_set", "pick_done"))
        bc_psum, b_done, c_done = sem("bc_psum"), sem("b_done"), sem("c_done")
        z_psum, z_read, e_step, l_done, dt_done, dtu_done = (sem(n) for n in ("z_psum", "z_read", "e_step", "l_done", "dt_done",
                                                                              "dtu_done"))
        diag_done, y_done = sem("diag_done"), sem("y_done")
        da_done, db_done, scan_done, hc_done, y_acc, st_copied = (sem(n) for n in ("da_done", "db_done", "scan_done", "hc_done",
                                                                                   "y_acc", "st_copied"))
        out_psum, out_added = sem("out_psum"), sem("out_added")
        NJ, EARLY, FIRST, LAG = NCH * DJ, 4, 12, 6
        SWITCH = (DJ - 1) * NS
        OUT_BANK = (2, 3, 7, 6)
        CUT = DJ - 2
        SECOND, THIRD = (DJ + 1) * NS, (DJ + 2) * NS + 8
        OUT, ADD = {}, {}
        for t in range(TPC):
            for j in range(CUT):
                OUT[(j + 1) * NS + 5 + 2 * t] = (t, j, j == 0, j == CUT - 1)
            for j in range(CUT, DJ):
                OUT[SECOND + 6 * t + 3 * (j - CUT)] = (t, j, j == CUT, j == DJ - 1)
            for j in range(DJ - 1):
                OUT[max(THIRD + 3 * TPC * j, (DJ + j + 1) * NS + 6) + 3 * t] = (TPC + t, j, j == 0, False)
        for step in sorted(OUT):
            if OUT[step][3]:
                ADD[step + 5] = len(ADD)
        SOFTPLUS = (4, 6, 8, 10)
        ROWS = ((2, 3), (6, 7))
        made_at = {r: 2 * (r - FIRST) for r in range(FIRST, NS)} | {NS + r: SWITCH + (3 * r + 1) // 2 for r in range(NS)}

        def tokens(jj):
            return slice(jj // DJ * CH, (jj // DJ + 1) * CH)

        def rows_made(i):
            return i // (DJ * NS) * NS + i % NS + 1

        with nc.Block() as block:
            @block.tensor
            def _(pe):
                def delta(jj):
                    if jj >= 2:
                        pe.wait_ge(z_read, 2 * (jj - 1))
                    j = jj % DJ
                    pe.matmul(bank[4 + jj % 2][:], WdtT[:, j * P:(j + 1) * P], ssT[0:RK, tokens(jj)], start=True,
                              stop=True).then_inc(z_psum, 1)

                def rows(r):
                    if r >= 2:
                        pe.wait_ge(b_done, r - 1)
                        pe.wait_ge(c_done, r - 1)
                    if r == NS:
                        pe.wait_ge(ss_low, 2)
                        pe.wait_ge(out_added, TPC)
                    for k in range(2):
                        c = RK + k * NS + r % NS
                        last = pe.matmul(bank[ROWS[r % 2][k]][:], pick[:, c:c + 1].to_broadcast([2 * W3, P]), ss[:],
                                         start=True, stop=True)
                    last.then_inc(bc_psum, 1)

                def transpose(ch):
                    pe.wait_ge(sx_n, 3 * (ch + 1))
                    for t in range(ch * TPC, (ch + 1) * TPC):
                        last = pe.transpose(bank[ch][:, t % TPC * P:(t % TPC + 1) * P],
                                            twice[:, t].rearrange("p a w -> p (a w)"), ident[:])
                    last.then_inc(st_psum, 1)

                transpose(0)
                pe.wait_ge(st_done, 1)
                delta(0)
                pe.wait_ge(ss_low, 1)
                pe.wait_ge(pick_done, 1)
                for r in range(EARLY):
                    rows(r)
                transpose(1)
                delta(1)
                for r in range(EARLY, FIRST):
                    rows(r)
                for i in range(NJ * NS):
                    jj, n = divmod(i, NS)
                    y = bank[jj % 2]
                    if n == 0:
                        pe.wait_ge(diag_done, jj + 1)
                        if jj >= 2:
                            pe.wait_ge(y_done, jj - 1)
                        pe.matmul(y[:], diag[jj % 2], XS[:, jj % DJ, tokens(jj)], start=True, stop=False)
                    if n == 12 and jj + 2 < NJ:
                        delta(jj + 2)
                    if i == 0:
                        pe.wait_ge(st_done, NCH)
                    pe.wait_ge(hc_done, i + 1)
                    pe.matmul(y[:], ident[:], Hs[i % len(Hs)][:], start=False, stop=(n == NS - 1)).then_inc(y_acc, 1)
                    for r in (r for r in made_at if made_at[r] == i):
                        rows(r)
                    if i in OUT:
                        t, j, first, last = OUT[i]
                        if first and t == 0:
                            pe.wait_ge(b_done, NS * (1 if i < SWITCH else 2))
                            pe.wait_ge(c_done, NS * (1 if i < SWITCH else 2))
                        if t >= TPC and first:
                            pe.wait_ge(out_added, t + 1)
                        pe.wait_ge(y_done, t // TPC * DJ + j + 1)
                        product = pe.matmul(bank[OUT_BANK[t % TPC]][:], XS[:, j, t * P:(t + 1) * P], WoutT[:, j, :],
                                            start=first, stop=last)
                        if last:
                            product.then_inc(out_psum, 1)

            @block.scalar
            def _(act):
                def softplus(jj, part):
                    b, bias = bank[4 + jj % 2][:], bdt[:, jj % DJ:jj % DJ + 1]
                    if part == 0:
                        act.wait_ge(z_psum, jj + 1)
                        if jj:
                            act.wait_ge(dt_done, jj)
                        act.activation(E, b, ACT.Abs, bias=bias).then_inc(z_read, 1)
                    elif part == 1:
                        act.activation(R, b, ACT.Relu, bias=bias).then_inc(z_read, 1)
                    elif part == 2:
                        act.wait_ge(z_read, 2 * jj + 2)
                        act.activation(E, E, ACT.Exp, scale=-1.0).then_inc(e_step, 1)
                    else:
                        act.wait_ge(e_step, jj + 1)
                        act.activation(E, E, ACT.Ln, bias=1.0).then_inc(l_done, 1)

                def high(ch):
                    act.copy(ss[:], ssT[:, ch * CH:(ch + 1) * CH]).then_inc(ss_high, 1)

                def row(r, k):
                    act.wait_ge(bc_psum, r + 1)
                    act.copy(BC[:, k * NS + r % NS, :], bank[ROWS[r % 2][k]][:]).then_inc((b_done, c_done)[k], 1)

                def skip(jj):
                    if jj >= 2:
                        act.wait_ge(y_acc, NS * (jj - 1))
                    act.activation(diag[jj % 2], ident[:], ACT.Copy, scale=dsk[:, jj % DJ:jj % DJ + 1]).then_inc(diag_done, 1)

                def transposed(ch):
                    act.wait_ge(st_psum, ch + 1)
                    act.copy(ssT[:, ch * CH:(ch + 1) * CH], bank[ch][:]).then_inc(st_done, 1)

                transposed(0)
                act.wait_ge(st_done, 1)
                high(0)
                for part in range(4):
                    softplus(0, part)
                transposed(1)
                skip(0)
                act.wait_ge(b_done, EARLY)
                for r in range(EARLY, FIRST):
                    row(r, 0)
                for i in range(NJ * NS + 4):
                    jj, n = divmod(i, NS)
                    if 3 <= i < DJ * NS + 3:
                        act.wait_ge(scan_done, i - 2)
                        j, k = divmod(i - 3, NS)
                        act.copy(state[:, j, k:k + 1], Hs[(i - 3) % len(Hs)][:, CH - 1:CH]).then_inc(st_copied, 1)
                    if i < NJ * NS:
                        if n == 0:
                            act.wait_ge(dt_done, jj + 1)
                        if i >= 3:
                            act.wait_ge(scan_done, i - 2)
                        act.activation(dA[i % 3][:], DT[jj % 2][:], ACT.Exp, scale=Aneg[:, jj % DJ, n:n + 1]).then_inc(da_done, 1)
                    for k in (1, 0):
                        for r in (r for r in made_at if made_at[r] == i - LAG - k):
                            row(r, k)
                    if i == SWITCH - NS:
                        act.wait_ge(b_done, NS)
                        high(1)
                    if n == 13 and jj + 1 < NJ:
                        skip(jj + 1)
                    if n in SOFTPLUS and jj + 1 < NJ:
                        softplus(jj + 1, SOFTPLUS.index(n))

            @block.gpsimd
            def _(pool):
                pool.memset(nh3[:], -0.5).then_inc(nh3_set, 1)
                pool.tensor_tensor(pick[:], ident[:, 0:W3], ident[:, W3:], ALU.add).then_inc(pick_done, 1)
                pool.wait_ge(sx_ms, 3)
                for i, (a, b) in enumerate(GROUPS):
                    pool.tensor_scalar(v3[:, i, :], m3[:, i, :], 1.0 / (b - a), 1e-6, ALU.mult, ALU.add).then_inc(sx_eps, 1)
                pool.wait_ge(sx_eps, 3)
                pool.wait_ge(nh3_set, 1)
                for ch in range(NCH):
                    tiles = slice(ch * TPC, (ch + 1) * TPC)
                    pool.tensor_tensor(r3[:, :, tiles], v3[:, :, tiles], nh3[:, :, tiles], ALU.pow).then_inc(sx_r, 1)

                def delta_u(jj):
                    pool.wait_ge(dt_done, jj + 1)
                    if jj >= 2:
                        pool.wait_ge(db_done, NS * (jj - 1))
                    pool.tensor_tensor(DTU[jj % 2][:], DT[jj % 2][:], XS[:, jj % DJ, tokens(jj)], ALU.mult).then_inc(dtu_done, 1)

                delta_u(0)
                for i in range(NJ * NS):
                    jj, n = divmod(i, NS)
                    if n == 0:
                        pool.wait_ge(dtu_done, jj + 1)
                    if jj % DJ == 0:
                        pool.wait_ge(b_done, rows_made(i))
                    if i >= len(Hs):
                        pool.wait_ge(y_acc, i - len(Hs) + 1)
                    pool.tensor_tensor(Hs[i % len(Hs)][:], DTU[jj % 2][:], BC[:, n, :], ALU.mult).then_inc(db_done, 1)
                    if n == 13 and jj + 1 < NJ:
                        delta_u(jj + 1)

            @block.vector
            def _(dve):
                dve.wait_ge(sx_psum, 1)
                dve.tensor_copy(SS.rearrange("p k w -> p (k w)"), bank[7][:]).then_inc(sx_step, 1)
                dve.wait_ge(sx_step, 1)
                dve.tensor_tensor(SSq, SS, SS, ALU.mult).then_inc(sx_step, 1)
                dve.wait_ge(sx_step, 2)
                for i, (a, b) in enumerate(GROUPS):
                    dve.tensor_reduce(m3[:, i, :], SSq[:, :, a:b], AX_X, ALU.add).then_inc(sx_ms, 1)
                for ch in range(NCH):
                    dve.wait_ge(sx_r, ch + 1)
                    tiles = slice(ch * TPC, (ch + 1) * TPC)
                    for i, (a, b) in enumerate(GROUPS):
                        dve.tensor_tensor(twice[:, tiles, :, a:b], SS[:, tiles, a:b].unsqueeze(2).to_broadcast([P, TPC, 2, b - a]),
                                          r3[:, i, tiles].unsqueeze(2).unsqueeze(3).to_broadcast([P, TPC, 2, b - a]),
                                          ALU.mult).then_inc(sx_n, 1)

                def low(ch):
                    dve.wait_ge(ss_high, ch + 1)
                    dve.tensor_tensor(ss[W3:, :], ssT[W3:, ch * CH:(ch + 1) * CH], ss[W3:, :].bitcast(F32),
                                       ALU.subtract).then_inc(ss_low, 1)

                def delta(jj):
                    dve.wait_ge(l_done, jj + 1)
                    if jj >= 2:
                        dve.wait_ge(da_done, NS * (jj - 1))
                        dve.wait_ge(dtu_done, jj - 1)
                    dve.tensor_tensor(DT[jj % 2][:], R, E, ALU.add).then_inc(dt_done, 1)

                def weigh(i):
                    dve.wait_ge(scan_done, i + 1)
                    if i < DJ * NS:
                        dve.wait_ge(st_copied, i + 1)
                    if i // NS % DJ == 0:
                        dve.wait_ge(c_done, rows_made(i))
                    h = Hs[i % len(Hs)][:]
                    dve.tensor_tensor(h, h, BC[:, NS + i % NS, :], ALU.mult).then_inc(hc_done, 1)

                def gate(jj):
                    dve.wait_ge(y_acc, NS * (jj + 1))
                    dve.tensor_tensor(XS[:, jj % DJ, tokens(jj)], bank[jj % 2][:], G[:, jj % DJ, tokens(jj)],
                                      ALU.mult).then_inc(y_done, 1)

                low(0)
                for r in range(FIRST):
                    dve.wait_ge(bc_psum, r + 1)
                    if r < EARLY:
                        dve.tensor_copy(BC[:, r, :], bank[ROWS[r % 2][0]][:]).then_inc(b_done, 1)
                    dve.tensor_copy(BC[:, NS + r, :], bank[ROWS[r % 2][1]][:]).then_inc(c_done, 1)
                    if r == EARLY - 1:
                        delta(0)
                for i in range(NJ * NS):
                    jj, n = divmod(i, NS)
                    if n == 11 and jj + 1 < NJ:
                        delta(jj + 1)
                    dve.wait_ge(da_done, i + 1)
                    dve.wait_ge(db_done, i + 1)
                    first = jj < DJ
                    if i == DJ * NS:
                        dve.wait_ge(st_copied, DJ * NS)
                    dve.tensor_tensor_scan(Hs[i % len(Hs)][:], dA[i % 3][:], Hs[i % len(Hs)][:],
                                           0.0 if first else state[:, jj % DJ, n:n + 1], ALU.mult, ALU.add).then_inc(scan_done, 1)
                    if i >= 2:
                        weigh(i - 2)
                    if i == SWITCH - NS + 2:
                        low(1)
                    if n == 4 and jj:
                        gate(jj - 1)
                    if i in ADD:
                        k = ADD[i]
                        t = k % TPC
                        dve.wait_ge(out_psum, k + 1)
                        if k >= TPC:
                            dve.wait_ge(out_added, k - TPC + 1)
                        dve.tensor_tensor(X[:, t, :], bank[OUT_BANK[t]][:], X[:, t, :], ALU.add).then_inc(out_added, 1)
                weigh(NJ * NS - 2)
                weigh(NJ * NS - 1)
                gate(NJ - 1)

        ssm.close()
        ffn2 = ExitStack()
        f2 = FeedForward(ffn2, "f2", (4, 5, 4))
        ffn2.close()

        nf2 = Norm()
        last_psum, last_added = sem("last_psum"), sem("last_added")
        with nc.Block() as block:
            @block.sync
            def _(sp):
                f2.load(sp, 0)

            @block.tensor
            def _(pe):
                for i in range(TPC):
                    t, j = TPC + i, DJ - 1
                    pe.matmul(bank[OUT_BANK[i]][:], XS[:, j, t * P:(t + 1) * P], WoutT[:, j, :], start=False,
                              stop=True).then_inc(last_psum, 1)
                for t in range(NT):
                    nf2.tensor_transpose(pe, t)
                    if t == TPC:
                        f2.head(f2.transpose, pe)

            @block.vector
            def _(dve):
                for t in range(NT + 3):
                    if TPC <= t < NT:
                        dve.wait_ge(last_psum, t - TPC + 1)
                        dve.tensor_tensor(X[:, t, :], bank[OUT_BANK[t - TPC]][:], X[:, t, :], ALU.add).then_inc(last_added, 1)
                        dve.wait_ge(last_added, t - TPC + 1)
                    nf2.vector_step(dve, t)
                    if t == TPC + 2:
                        f2.head(f2.low, dve)

            @block.gpsimd
            def _(pool):
                for t in range(NT):
                    nf2.pool_rstd(pool, t)

            @block.scalar
            def _(act):
                for t in range(NT):
                    nf2.scalar_high(act, t)
                    if t == TPC:
                        f2.head(f2.high, act)

        f2.run(None)


NAMES = ["x", "wq_a", "q_a_ln_w", "wq_b", "wkv_a", "kv_a_ln_w", "wkv_b", "wo"]
INPUTS = ([f"L0_attn_a_{n}" for n in NAMES]
          + [f"L0_attn_b_{n}" for n in ("W_in", "conv_w", "conv_b", "W_x", "W_dt", "b_dt", "A_log", "D", "W_out")]
          + [f"L0_ffn_{n}" for n in ("W_gate", "W_up", "W_down")])


def kernel(**inputs):
    import concourse.bacc as bacc
    from concourse.bass_utils import run_bass_kernel_spmd

    nc = bacc.Bacc("TRN2", target_bir_lowering=False, num_devices=1)
    arrays = {f"in_{n}": np.ascontiguousarray(inputs[n]) for n in INPUTS}
    arrays["rope_cos"], arrays["rope_sin"] = rope_tables()
    args = [nc.dram_tensor(n, a.shape, mybir.dt.from_np(a.dtype), kind="ExternalInput").ap() for n, a in arrays.items()]
    args.append(nc.dram_tensor("out", (1, S, DM), F32, kind="ExternalOutput").ap())
    layer(nc, *args)
    r = run_bass_kernel_spmd(nc, [arrays], core_ids=[0])
    return r.results[0]["out"]
```
